# Optimizing a Trainium2 kernel written in Bass

```python
import numpy as np
import jax
import jax.numpy as jnp

def _softmax(x, axis=-1):
    return jax.nn.softmax(x, axis=axis)

def _gelu(x):
    return jax.nn.gelu(x, approximate=True)

def _silu(x):
    return jax.nn.silu(x)

def _sigmoid(x):
    return jax.nn.sigmoid(x)

def _layernorm(x, axis=-1, eps=1e-05):
    m = jnp.mean(x, axis=axis, keepdims=True)
    v = jnp.var(x, axis=axis, keepdims=True)
    return (x - m) / jnp.sqrt(v + eps)

def _scatter_add(tgt, idx, src, axis=0):
    return tgt.at[idx].add(src)

def _segment_sum(src, seg, n):
    return jax.ops.segment_sum(src, seg, n)
kernel_name = 'mk_vit_tower_d4_tok_img1024_r4_1d1927'

def setup_inputs(seed: int=0):
    np.random.seed(seed)
    _w = jnp.asarray

    def _rec_inputs():
        import jax
        import jax.numpy as jnp
        _rk = jax.random.key(seed)
        x = -0.00016672 + 0.999947 * jax.random.normal(jax.random.fold_in(_rk, 1), (16, 3, 96, 96), jnp.float32)
        return x
    x = _rec_inputs()

    def _L0_tok_setup():
        import jax, jax.numpy as jnp
        import numpy as np
        DIM = 256
        IMG = 96
        P = 16
        C = 3
        TEMP = 10000.0
        EPS = 1e-05
        PATCH_DIM = C * P * P
        HP = IMG // P

        def layernorm(x, gamma, beta):
            mu = jnp.mean(x, axis=-1, keepdims=True)
            var = jnp.var(x, axis=-1, keepdims=True)
            return (x - mu) * jax.lax.rsqrt(var + EPS) * gamma + beta

        def posemb_sincos_2d(h, w, dim, dtype):
            y, x = jnp.meshgrid(jnp.arange(h), jnp.arange(w), indexing='ij')
            omega = jnp.arange(dim // 4, dtype=jnp.float32) / (dim // 4 - 1)
            omega = 1.0 / TEMP ** omega
            y = y.reshape(-1)[:, None] * omega[None, :]
            x = x.reshape(-1)[:, None] * omega[None, :]
            pe = jnp.concatenate((jnp.sin(x), jnp.cos(x), jnp.sin(y), jnp.cos(y)), axis=1)
            return pe.astype(dtype)
        key = jax.random.key(seed)
        ks = jax.random.split(key, 8)
        B = 64
        img = jax.random.normal(ks[0], (B, C, IMG, IMG), dtype=jnp.float32)
        cls_token = jax.random.normal(ks[1], (1, 1, DIM), dtype=jnp.float32)
        cls_pos_embedding = jax.random.normal(ks[2], (1, 1, DIM), dtype=jnp.float32)
        ln1_g = jnp.ones((PATCH_DIM,), jnp.float32)
        ln1_b = jnp.zeros((PATCH_DIM,), jnp.float32)
        W = jax.random.normal(ks[3], (PATCH_DIM, DIM), dtype=jnp.float32) / np.sqrt(PATCH_DIM)
        bias = jnp.zeros((DIM,), jnp.float32)
        ln2_g = jnp.ones((DIM,), jnp.float32)
        ln2_b = jnp.zeros((DIM,), jnp.float32)
        return {'img': img, 'cls_token': cls_token, 'cls_pos_embedding': cls_pos_embedding, 'ln1_g': ln1_g, 'ln1_b': ln1_b, 'W': W, 'bias': bias, 'ln2_g': ln2_g, 'ln2_b': ln2_b}
    _L0_tok_all = _L0_tok_setup()
    _L0_tok_in = {k: v for k, v in _L0_tok_all.items() if k in ('cls_token', 'cls_pos_embedding', 'ln1_g', 'ln1_b', 'W', 'bias', 'ln2_g', 'ln2_b')}
    del _L0_tok_all

    def _L0_attn_setup():
        import jax, jax.numpy as jnp
        import numpy as np
        import math
        B, S, D, H = (1, 512, 256, 16)
        HD = D // H
        SCALE = 1.0 / math.sqrt(HD)
        ENT = 0.5
        DECAY = 0.1
        SUP = 0.3
        EPS = 1e-05

        def _heads(x):
            b, s, _ = x.shape
            return x.reshape(b, s, H, HD).transpose(0, 2, 1, 3)
        key = jax.random.key(seed)
        ks = jax.random.split(key, 24)

        def w(k, shape, s=0.02):
            return jax.random.normal(k, shape, dtype=jnp.float32) * s
        return {'hidden_states': jax.random.normal(ks[0], (B, S, D), dtype=jnp.float32), 'Wq': w(ks[1], (D, D)), 'bq': jnp.zeros((D,), jnp.float32), 'Wk': w(ks[2], (D, D)), 'bk': jnp.zeros((D,), jnp.float32), 'Wv': w(ks[3], (D, D)), 'bv': jnp.zeros((D,), jnp.float32), 'Wo': w(ks[4], (D, D)), 'bo': jnp.zeros((D,), jnp.float32), 'Weq': w(ks[5], (D, D), 0.002), 'beq': jnp.zeros((D,), jnp.float32), 'Wek': w(ks[6], (D, D), 0.002), 'bek': jnp.zeros((D,), jnp.float32), 'amp_w': w(ks[7], (H, D)), 'amp_b': jnp.zeros((H,), jnp.float32), 'ph_w': w(ks[8], (H, D)), 'ph_b': jnp.zeros((H,), jnp.float32), 'mix_w': w(ks[9], (H, HD, HD)), 'mix_b': jnp.zeros((H, HD), jnp.float32), 'ln_g': jnp.ones((D,), jnp.float32), 'ln_b': jnp.zeros((D,), jnp.float32)}
    _L0_attn_all = _L0_attn_setup()
    _L0_attn_in = {k: v for k, v in _L0_attn_all.items() if k in ('Wq', 'bq', 'Wk', 'bk', 'Wv', 'bv', 'Wo', 'bo', 'Weq', 'beq', 'Wek', 'bek', 'amp_w', 'amp_b', 'ph_w', 'ph_b', 'mix_w', 'mix_b', 'ln_g', 'ln_b')}
    del _L0_attn_all

    def _L0_ffn_setup():
        import jax, jax.numpy as jnp
        import numpy as np
        K_TOP = 4
        ALPHA = 1.702
        LIMIT = 7.0
        key = jax.random.key(seed)
        ks = jax.random.split(key, 4)
        B, S, H, E, inter = (2, 512, 256, 16, 256)
        return {'hidden_states': jax.random.normal(ks[0], (B, S, H), dtype=jnp.float32), 'router_weight': jax.random.normal(ks[1], (E, H), dtype=jnp.float32) * 0.02, 'router_bias': jnp.zeros((E,), dtype=jnp.float32), 'gate_up_proj': jax.random.normal(ks[2], (E, H, 2 * inter), dtype=jnp.float32) * 0.02, 'gate_up_bias': jnp.zeros((E, 2 * inter), dtype=jnp.float32), 'down_proj': jax.random.normal(ks[3], (E, inter, H), dtype=jnp.float32) * 0.02, 'down_bias': jnp.zeros((E, H), dtype=jnp.float32)}
    _L0_ffn_all = _L0_ffn_setup()
    _L0_ffn_in = {k: v for k, v in _L0_ffn_all.items() if k in ('router_weight', 'router_bias', 'gate_up_proj', 'gate_up_bias', 'down_proj', 'down_bias')}
    del _L0_ffn_all

    def _L1_attn_setup():
        import jax, jax.numpy as jnp
        import numpy as np
        INFTY_APPROX = 1e+30
        ROTARY_BASE = 10000.0
        D_HEAD = 128

        def rope(x):
            *_, length, width = x.shape
            half = width // 2
            positions = jnp.arange(length)[:, None].astype(x.dtype)
            dims = jnp.arange(half).astype(x.dtype)
            ang_freqs = jnp.power(ROTARY_BASE, -dims / half)[None, :]
            radians = positions * ang_freqs
            cos = jnp.cos(radians)[None, None].astype(x.dtype)
            sin = jnp.sin(radians)[None, None].astype(x.dtype)
            even, odd = jnp.split(x, 2, axis=-1)
            r_even = even * cos - odd * sin
            r_odd = even * sin + odd * cos
            return jnp.concatenate([r_even, r_odd], axis=-1)
        key = jax.random.key(seed)
        ks = jax.random.split(key, 5)
        B, T, M, D = (4, 512, 256, D_HEAD)
        H = M // D
        x = jax.random.normal(ks[0], (B, T, M), dtype=jnp.float32)
        scale = M ** (-0.5)
        wq = jax.random.normal(ks[1], (H, M, D), dtype=jnp.float32) * scale
        wk = jax.random.normal(ks[2], (H, M, D), dtype=jnp.float32) * scale
        wv = jax.random.normal(ks[3], (H, M, D), dtype=jnp.float32) * scale
        wo = jax.random.normal(ks[4], (H, D, M), dtype=jnp.float32) * scale
        return {'x': x, 'wq': wq, 'wk': wk, 'wv': wv, 'wo': wo}
    _L1_attn_all = _L1_attn_setup()
    _L1_attn_in = {k: v for k, v in _L1_attn_all.items() if k in ('wq', 'wk', 'wv', 'wo')}
    del _L1_attn_all

    def _L1_ffn_setup():
        import jax, jax.numpy as jnp
        import numpy as np
        TOP_K = 2
        key = jax.random.key(seed)
        ks = jax.random.split(key, 5)
        B, S, D, H, E = (2, 256, 256, 352, 8)
        scale = 0.02
        x = jax.random.normal(ks[0], (B, S, D), dtype=jnp.float32)
        Wr = jax.random.normal(ks[1], (D, E), dtype=jnp.float32) * scale
        W1 = jax.random.normal(ks[2], (E, D, H), dtype=jnp.float32) * scale
        W2 = jax.random.normal(ks[3], (E, D, H), dtype=jnp.float32) * scale
        W3 = jax.random.normal(ks[4], (E, H, D), dtype=jnp.float32) * scale
        return {'x': x, 'Wr': Wr, 'W1': W1, 'W2': W2, 'W3': W3}
    _L1_ffn_all = _L1_ffn_setup()
    _L1_ffn_in = {k: v for k, v in _L1_ffn_all.items() if k in ('Wr', 'W1', 'W2', 'W3')}
    del _L1_ffn_all

    def _L2_attn_setup():
        import jax, jax.numpy as jnp
        import numpy as np
        import math
        B, L, D, H = (2, 512, 256, 16)

        def _log_sparse_mask(L):
            m = np.zeros((L, L), dtype=bool)
            for i in range(L):
                for k in range(int(math.log2(i + 1)) + 1):
                    j = i - 2 ** k
                    if j >= 0:
                        m[i, j] = True
                m[i, i] = True
            return m
        key = jax.random.key(seed)
        ks = jax.random.split(key, 9)
        s = 0.02
        return {'x': jax.random.normal(ks[0], (B, L, D), dtype=jnp.float32), 'Wq': jax.random.normal(ks[1], (D, D), dtype=jnp.float32) * s, 'bq': jnp.zeros((D,), dtype=jnp.float32), 'Wk': jax.random.normal(ks[2], (D, D), dtype=jnp.float32) * s, 'bk': jnp.zeros((D,), dtype=jnp.float32), 'Wv': jax.random.normal(ks[3], (D, D), dtype=jnp.float32) * s, 'bv': jnp.zeros((D,), dtype=jnp.float32), 'Wo': jax.random.normal(ks[4], (D, D), dtype=jnp.float32) * s, 'bo': jnp.zeros((D,), dtype=jnp.float32)}
    _L2_attn_all = _L2_attn_setup()
    _L2_attn_in = {k: v for k, v in _L2_attn_all.items() if k in ('Wq', 'bq', 'Wk', 'bk', 'Wv', 'bv', 'Wo', 'bo')}
    del _L2_attn_all

    def _L2_ffn_setup():
        import jax, jax.numpy as jnp
        import numpy as np
        H = 256
        NH = 16
        HD = H // NH
        HH = HD // 2
        L = H // 4
        I = int(H * 1.0)
        ER = 7
        TOPK = 2
        BASE = 10000.0
        EPS = 1e-05

        def rmsnorm(x, w):
            norm = jnp.sqrt(jnp.mean(x * x, axis=-1, keepdims=True)) + EPS
            return x / norm * w

        def rope_tables(seq_len):
            inv_freq = 1.0 / BASE ** (jnp.arange(0, HH, 2, dtype=jnp.float32) / HH)
            t = jnp.arange(seq_len, dtype=jnp.float32)
            freqs = jnp.einsum('i,j->ij', t, inv_freq)
            emb = jnp.concatenate([freqs, freqs], axis=-1)
            cos = jnp.cos(emb)[None, :, None, :]
            sin = jnp.sin(emb)[None, :, None, :]
            return (cos, sin)

        def rotate_half(x):
            x1, x2 = jnp.split(x, 2, axis=-1)
            return jnp.concatenate([-x2, x1], axis=-1)

        def silu(x):
            return x * jax.nn.sigmoid(x)

        def mla(xn, W_kvd, W_qd, W_ku, W_qu, W_vu, W_ropeq, W_ropek, W_o):
            B, S, _ = xn.shape
            kv_lat = xn @ W_kvd
            q_lat = xn @ W_qd
            k = (kv_lat @ W_ku).reshape(B, S, NH, HH)
            q = (q_lat @ W_qu).reshape(B, S, NH, HH)
            v = (kv_lat @ W_vu).reshape(B, S, NH, HD)
            q_rope = (q_lat @ W_ropeq).reshape(B, S, NH, HH)
            k_rope = (xn @ W_ropek).reshape(B, S, NH, HH)
            cos, sin = rope_tables(S)
            k_rope = k_rope * cos + rotate_half(k_rope) * sin
            q_rope = q_rope * cos + rotate_half(q_rope) * sin
            kk = jnp.concatenate([k, k_rope], axis=-1)
            qq = jnp.concatenate([q, q_rope], axis=-1)
            scale = 1.0 / jnp.sqrt(jnp.float32(HD))
            scores = jnp.einsum('bqhd,bkhd->bhqk', qq, kk) * scale
            causal = jnp.tril(jnp.ones((S, S), dtype=bool))
            scores = jnp.where(causal[None, None], scores, jnp.finfo(scores.dtype).min)
            probs = jax.nn.softmax(scores, axis=-1)
            y = jnp.einsum('bhqk,bkhd->bqhd', probs, v).reshape(B, S, H)
            return y @ W_o

        def moe(xn, Wg_s, Wu_s, Wd_s, Wg_r, Wu_r, Wd_r, W_router, routing_bias):
            B, S, _ = xn.shape
            xt = xn.reshape(B * S, H)
            shared = silu(xt @ Wg_s) * (xt @ Wu_s) @ Wd_s
            logits = xt @ W_router + routing_bias
            probs = jax.nn.sigmoid(logits)
            scores, idx = jax.lax.top_k(probs, TOPK)
            scores = scores / jnp.sum(scores, axis=-1, keepdims=True)
            wts = jnp.sum(jax.nn.one_hot(idx, ER, dtype=xt.dtype) * scores[..., None], axis=1)
            g = jnp.einsum('th,ehi->tei', xt, Wg_r)
            u = jnp.einsum('th,ehi->tei', xt, Wu_r)
            hmid = silu(g) * u
            combined = jnp.einsum('tei,eih,te->th', hmid, Wd_r, wts)
            return (shared + combined).reshape(B, S, H)
        key = jax.random.key(seed)
        ks = jax.random.split(key, 20)
        s = 0.02
        r = lambda k, shp: jax.random.normal(k, shp, dtype=jnp.float32) * s
        return {'x': jax.random.normal(ks[0], (4, 256, H), dtype=jnp.float32), 'w_ln1': jnp.ones((H,), jnp.float32), 'w_ln2': jnp.ones((H,), jnp.float32), 'W_kvd': r(ks[1], (H, L)), 'W_qd': r(ks[2], (H, L)), 'W_ku': r(ks[3], (L, NH * HH)), 'W_qu': r(ks[4], (L, NH * HH)), 'W_vu': r(ks[5], (L, H)), 'W_ropeq': r(ks[6], (L, H // 2)), 'W_ropek': r(ks[7], (H, H // 2)), 'W_o': r(ks[8], (H, H)), 'Wg_s': r(ks[9], (H, I)), 'Wu_s': r(ks[10], (H, I)), 'Wd_s': r(ks[11], (I, H)), 'Wg_r': r(ks[12], (ER, H, I)), 'Wu_r': r(ks[13], (ER, H, I)), 'Wd_r': r(ks[14], (ER, I, H)), 'W_router': r(ks[15], (H, ER)), 'routing_bias': jnp.zeros((ER,), jnp.float32)}
    _L2_ffn_all = _L2_ffn_setup()
    _L2_ffn_in = {k: v for k, v in _L2_ffn_all.items() if k in ('w_ln1', 'w_ln2', 'W_kvd', 'W_qd', 'W_ku', 'W_qu', 'W_vu', 'W_ropeq', 'W_ropek', 'W_o', 'Wg_s', 'Wu_s', 'Wd_s', 'Wg_r', 'Wu_r', 'Wd_r', 'W_router', 'routing_bias')}
    del _L2_ffn_all

    def _L3_attn_setup():
        import jax, jax.numpy as jnp
        import numpy as np
        NUM_HEADS = 16
        key = jax.random.key(seed)
        k1, k2, k3 = jax.random.split(key, 3)
        S, B, E = (512, 4, 256)
        std = float(np.sqrt(2.0 / (E + E)))
        query = jax.random.normal(k1, (S, B, E), dtype=jnp.float32)
        in_proj_weight = jax.random.normal(k2, (3 * E, E), dtype=jnp.float32) * std
        in_proj_bias = jnp.zeros((3 * E,), dtype=jnp.float32)
        out_proj_weight = jax.random.normal(k3, (E, E), dtype=jnp.float32) * std
        out_proj_bias = jnp.zeros((E,), dtype=jnp.float32)
        return {'query': query, 'in_proj_weight': in_proj_weight, 'in_proj_bias': in_proj_bias, 'out_proj_weight': out_proj_weight, 'out_proj_bias': out_proj_bias}
    _L3_attn_all = _L3_attn_setup()
    _L3_attn_in = {k: v for k, v in _L3_attn_all.items() if k in ('in_proj_weight', 'in_proj_bias', 'out_proj_weight', 'out_proj_bias')}
    del _L3_attn_all

    def _L3_ffn_setup():
        import jax, jax.numpy as jnp
        import numpy as np
        B, T, D, FF, E, TOP_K = (4, 512, 256, 1024, 8, 2)
        key = jax.random.key(seed)
        k0, k1, k2, k3 = jax.random.split(key, 4)
        x = jax.random.normal(k0, (B, T, D), dtype=jnp.float32)
        router_w = jax.random.normal(k1, (E, D), dtype=jnp.float32) * D ** (-0.5)
        w1 = jax.random.normal(k2, (E, D, FF), dtype=jnp.float32) * D ** (-0.5)
        w2 = jax.random.normal(k3, (E, FF, D), dtype=jnp.float32) * FF ** (-0.5)
        return {'x': x, 'router_w': router_w, 'w1': w1, 'w2': w2}
    _L3_ffn_all = _L3_ffn_setup()
    _L3_ffn_in = {k: v for k, v in _L3_ffn_all.items() if k in ('router_w', 'w1', 'w2')}
    del _L3_ffn_all
    return {'x': x, 'L0_tok_cls_token': _L0_tok_in['cls_token'], 'L0_tok_cls_pos_embedding': _L0_tok_in['cls_pos_embedding'], 'L0_tok_ln1_g': _L0_tok_in['ln1_g'], 'L0_tok_ln1_b': _L0_tok_in['ln1_b'], 'L0_tok_W': _L0_tok_in['W'], 'L0_tok_bias': _L0_tok_in['bias'], 'L0_tok_ln2_g': _L0_tok_in['ln2_g'], 'L0_tok_ln2_b': _L0_tok_in['ln2_b'], 'L0_attn_Wq': _L0_attn_in['Wq'], 'L0_attn_bq': _L0_attn_in['bq'], 'L0_attn_Wk': _L0_attn_in['Wk'], 'L0_attn_bk': _L0_attn_in['bk'], 'L0_attn_Wv': _L0_attn_in['Wv'], 'L0_attn_bv': _L0_attn_in['bv'], 'L0_attn_Wo': _L0_attn_in['Wo'], 'L0_attn_bo': _L0_attn_in['bo'], 'L0_attn_Weq': _L0_attn_in['Weq'], 'L0_attn_beq': _L0_attn_in['beq'], 'L0_attn_Wek': _L0_attn_in['Wek'], 'L0_attn_bek': _L0_attn_in['bek'], 'L0_attn_amp_w': _L0_attn_in['amp_w'], 'L0_attn_amp_b': _L0_attn_in['amp_b'], 'L0_attn_ph_w': _L0_attn_in['ph_w'], 'L0_attn_ph_b': _L0_attn_in['ph_b'], 'L0_attn_mix_w': _L0_attn_in['mix_w'], 'L0_attn_mix_b': _L0_attn_in['mix_b'], 'L0_attn_ln_g': _L0_attn_in['ln_g'], 'L0_attn_ln_b': _L0_attn_in['ln_b'], 'L0_ffn_router_weight': _L0_ffn_in['router_weight'], 'L0_ffn_router_bias': _L0_ffn_in['router_bias'], 'L0_ffn_gate_up_proj': _L0_ffn_in['gate_up_proj'], 'L0_ffn_gate_up_bias': _L0_ffn_in['gate_up_bias'], 'L0_ffn_down_proj': _L0_ffn_in['down_proj'], 'L0_ffn_down_bias': _L0_ffn_in['down_bias'], 'L1_attn_wq': _L1_attn_in['wq'], 'L1_attn_wk': _L1_attn_in['wk'], 'L1_attn_wv': _L1_attn_in['wv'], 'L1_attn_wo': _L1_attn_in['wo'], 'L1_ffn_Wr': _L1_ffn_in['Wr'], 'L1_ffn_W1': _L1_ffn_in['W1'], 'L1_ffn_W2': _L1_ffn_in['W2'], 'L1_ffn_W3': _L1_ffn_in['W3'], 'L2_attn_Wq': _L2_attn_in['Wq'], 'L2_attn_bq': _L2_attn_in['bq'], 'L2_attn_Wk': _L2_attn_in['Wk'], 'L2_attn_bk': _L2_attn_in['bk'], 'L2_attn_Wv': _L2_attn_in['Wv'], 'L2_attn_bv': _L2_attn_in['bv'], 'L2_attn_Wo': _L2_attn_in['Wo'], 'L2_attn_bo': _L2_attn_in['bo'], 'L2_ffn_w_ln1': _L2_ffn_in['w_ln1'], 'L2_ffn_w_ln2': _L2_ffn_in['w_ln2'], 'L2_ffn_W_kvd': _L2_ffn_in['W_kvd'], 'L2_ffn_W_qd': _L2_ffn_in['W_qd'], 'L2_ffn_W_ku': _L2_ffn_in['W_ku'], 'L2_ffn_W_qu': _L2_ffn_in['W_qu'], 'L2_ffn_W_vu': _L2_ffn_in['W_vu'], 'L2_ffn_W_ropeq': _L2_ffn_in['W_ropeq'], 'L2_ffn_W_ropek': _L2_ffn_in['W_ropek'], 'L2_ffn_W_o': _L2_ffn_in['W_o'], 'L2_ffn_Wg_s': _L2_ffn_in['Wg_s'], 'L2_ffn_Wu_s': _L2_ffn_in['Wu_s'], 'L2_ffn_Wd_s': _L2_ffn_in['Wd_s'], 'L2_ffn_Wg_r': _L2_ffn_in['Wg_r'], 'L2_ffn_Wu_r': _L2_ffn_in['Wu_r'], 'L2_ffn_Wd_r': _L2_ffn_in['Wd_r'], 'L2_ffn_W_router': _L2_ffn_in['W_router'], 'L2_ffn_routing_bias': _L2_ffn_in['routing_bias'], 'L3_attn_in_proj_weight': _L3_attn_in['in_proj_weight'], 'L3_attn_in_proj_bias': _L3_attn_in['in_proj_bias'], 'L3_attn_out_proj_weight': _L3_attn_in['out_proj_weight'], 'L3_attn_out_proj_bias': _L3_attn_in['out_proj_bias'], 'L3_ffn_router_w': _L3_ffn_in['router_w'], 'L3_ffn_w1': _L3_ffn_in['w1'], 'L3_ffn_w2': _L3_ffn_in['w2']}

def reference(x, L0_tok_cls_token, L0_tok_cls_pos_embedding, L0_tok_ln1_g, L0_tok_ln1_b, L0_tok_W, L0_tok_bias, L0_tok_ln2_g, L0_tok_ln2_b, L0_attn_Wq, L0_attn_bq, L0_attn_Wk, L0_attn_bk, L0_attn_Wv, L0_attn_bv, L0_attn_Wo, L0_attn_bo, L0_attn_Weq, L0_attn_beq, L0_attn_Wek, L0_attn_bek, L0_attn_amp_w, L0_attn_amp_b, L0_attn_ph_w, L0_attn_ph_b, L0_attn_mix_w, L0_attn_mix_b, L0_attn_ln_g, L0_attn_ln_b, L0_ffn_router_weight, L0_ffn_router_bias, L0_ffn_gate_up_proj, L0_ffn_gate_up_bias, L0_ffn_down_proj, L0_ffn_down_bias, L1_attn_wq, L1_attn_wk, L1_attn_wv, L1_attn_wo, L1_ffn_Wr, L1_ffn_W1, L1_ffn_W2, L1_ffn_W3, L2_attn_Wq, L2_attn_bq, L2_attn_Wk, L2_attn_bk, L2_attn_Wv, L2_attn_bv, L2_attn_Wo, L2_attn_bo, L2_ffn_w_ln1, L2_ffn_w_ln2, L2_ffn_W_kvd, L2_ffn_W_qd, L2_ffn_W_ku, L2_ffn_W_qu, L2_ffn_W_vu, L2_ffn_W_ropeq, L2_ffn_W_ropek, L2_ffn_W_o, L2_ffn_Wg_s, L2_ffn_Wu_s, L2_ffn_Wd_s, L2_ffn_Wg_r, L2_ffn_Wu_r, L2_ffn_Wd_r, L2_ffn_W_router, L2_ffn_routing_bias, L3_attn_in_proj_weight, L3_attn_in_proj_bias, L3_attn_out_proj_weight, L3_attn_out_proj_bias, L3_ffn_router_w, L3_ffn_w1, L3_ffn_w2):
    import jax
    import jax.numpy as jnp

    def _L0_tok_ref(img, cls_token, cls_pos_embedding, ln1_g, ln1_b, W, bias, ln2_g, ln2_b):
        import jax, jax.numpy as jnp
        import numpy as np
        DIM = 256
        IMG = 96
        P = 16
        C = 3
        TEMP = 10000.0
        EPS = 1e-05
        PATCH_DIM = C * P * P
        HP = IMG // P

        def layernorm(x, gamma, beta):
            mu = jnp.mean(x, axis=-1, keepdims=True)
            var = jnp.var(x, axis=-1, keepdims=True)
            return (x - mu) * jax.lax.rsqrt(var + EPS) * gamma + beta

        def posemb_sincos_2d(h, w, dim, dtype):
            y, x = jnp.meshgrid(jnp.arange(h), jnp.arange(w), indexing='ij')
            omega = jnp.arange(dim // 4, dtype=jnp.float32) / (dim // 4 - 1)
            omega = 1.0 / TEMP ** omega
            y = y.reshape(-1)[:, None] * omega[None, :]
            x = x.reshape(-1)[:, None] * omega[None, :]
            pe = jnp.concatenate((jnp.sin(x), jnp.cos(x), jnp.sin(y), jnp.cos(y)), axis=1)
            return pe.astype(dtype)
        b = img.shape[0]
        x = img.reshape(b, C, HP, P, HP, P)
        x = jnp.transpose(x, (0, 2, 4, 3, 5, 1))
        x = x.reshape(b, HP, HP, PATCH_DIM)
        x = layernorm(x, ln1_g, ln1_b)
        x = jnp.einsum('bhwp,pd->bhwd', x, W) + bias
        x = layernorm(x, ln2_g, ln2_b)
        pe = posemb_sincos_2d(HP, HP, DIM, x.dtype)
        x = x.reshape(b, HP * HP, DIM) + pe[None]
        cls_tokens = jnp.broadcast_to(cls_token + cls_pos_embedding, (b, 1, DIM))
        return jnp.concatenate((cls_tokens, x), axis=1)

    def _L0_attn_ref(hidden_states, Wq, bq, Wk, bk, Wv, bv, Wo, bo, Weq, beq, Wek, bek, amp_w, amp_b, ph_w, ph_b, mix_w, mix_b, ln_g, ln_b):
        import jax, jax.numpy as jnp
        import numpy as np
        import math
        B, S, D, H = (1, 512, 256, 16)
        HD = D // H
        SCALE = 1.0 / math.sqrt(HD)
        ENT = 0.5
        DECAY = 0.1
        SUP = 0.3
        EPS = 1e-05

        def _heads(x):
            b, s, _ = x.shape
            return x.reshape(b, s, H, HD).transpose(0, 2, 1, 3)
        hs = hidden_states
        b, s, _ = hs.shape
        q = _heads(hs @ Wq.T + bq)
        k = _heads(hs @ Wk.T + bk)
        v = _heads(hs @ Wv.T + bv)
        scores = jnp.einsum('bhqd,bhkd->bhqk', q, k) * SCALE
        eq = _heads(hs @ Weq.T + beq)
        ek = _heads(hs @ Wek.T + bek)
        pos = jnp.arange(s)
        decay = jnp.exp(-DECAY * jnp.abs(pos[:, None] - pos[None, :]).astype(jnp.float32))
        esc = jnp.einsum('bhqd,bhkd->bhqk', eq, ek) * (1.0 / math.sqrt(HD)) * decay
        attn = jax.nn.softmax(scores + ENT * esc, axis=-1)
        amps = jax.nn.sigmoid(hs @ amp_w.T + amp_b)
        phases = jnp.tanh(hs @ ph_w.T + ph_b) * math.pi
        a = amps.transpose(0, 2, 1)[..., None]
        p = phases.transpose(0, 2, 1)[..., None]
        sup = jnp.einsum('bhsd,hod->bhso', v, mix_w) + mix_b[None, :, None, :]
        mixed = v + SUP * a * jnp.cos(p) * sup + SUP * a * jnp.sin(p) * jnp.roll(sup, 1, axis=-1)
        ctx = jnp.einsum('bhqk,bhkd->bhqd', attn, mixed)
        ctx = ctx.transpose(0, 2, 1, 3).reshape(b, s, D)
        out = ctx @ Wo.T + bo
        res = hs + out
        mu = jnp.mean(res, axis=-1, keepdims=True)
        var = jnp.mean((res - mu) ** 2, axis=-1, keepdims=True)
        return (res - mu) * jax.lax.rsqrt(var + EPS) * ln_g + ln_b

    def _L0_ffn_ref(hidden_states, router_weight, router_bias, gate_up_proj, gate_up_bias, down_proj, down_bias):
        import jax, jax.numpy as jnp
        import numpy as np
        K_TOP = 4
        ALPHA = 1.702
        LIMIT = 7.0
        B, S, H = hidden_states.shape
        E, inter, _ = down_proj.shape
        logits = jnp.einsum('bsh,eh->bse', hidden_states, router_weight) + router_bias
        scores = jax.nn.softmax(logits, axis=-1)
        topk_w, topk_i = jax.lax.top_k(scores, K_TOP)
        gu = jnp.einsum('bsh,ehn->bsen', hidden_states, gate_up_proj) + gate_up_bias
        gate = jnp.minimum(gu[..., :inter], LIMIT)
        up = jnp.clip(gu[..., inter:], -LIMIT, LIMIT)
        glu = gate * jax.nn.sigmoid(gate * ALPHA)
        activated = (up + 1.0) * glu
        down = jnp.einsum('bsek,ekh->bseh', activated, down_proj) + down_bias
        sel = jnp.take_along_axis(down, topk_i[..., None], axis=2)
        out = jnp.sum(sel * topk_w[..., None], axis=2)
        return out

    def _L1_attn_ref(x, wq, wk, wv, wo):
        import jax, jax.numpy as jnp
        import numpy as np
        INFTY_APPROX = 1e+30
        ROTARY_BASE = 10000.0
        D_HEAD = 128

        def rope(x):
            *_, length, width = x.shape
            half = width // 2
            positions = jnp.arange(length)[:, None].astype(x.dtype)
            dims = jnp.arange(half).astype(x.dtype)
            ang_freqs = jnp.power(ROTARY_BASE, -dims / half)[None, :]
            radians = positions * ang_freqs
            cos = jnp.cos(radians)[None, None].astype(x.dtype)
            sin = jnp.sin(radians)[None, None].astype(x.dtype)
            even, odd = jnp.split(x, 2, axis=-1)
            r_even = even * cos - odd * sin
            r_odd = even * sin + odd * cos
            return jnp.concatenate([r_even, r_odd], axis=-1)
        q = jnp.einsum('bim,hmd->bhid', x, wq)
        k = jnp.einsum('bim,hmd->bhid', x, wk)
        v = jnp.einsum('bim,hmd->bhid', x, wv)
        q = rope(q)
        k = rope(k)
        mult = jnp.asarray(D_HEAD ** (-0.5), dtype=x.dtype)
        s = jnp.einsum('bhid,bhjd->bhij', q * mult, k * mult)
        T = s.shape[-1]
        i = jnp.arange(T)[:, None]
        j = jnp.arange(T)[None, :]
        mask = (i < j).astype(s.dtype)[None, None]
        s = s - jnp.asarray(INFTY_APPROX, dtype=s.dtype) * mask
        p = jax.nn.softmax(s, axis=-1)
        o = jnp.einsum('bhij,bhjd->bhid', p, v)
        r = jnp.einsum('bhid,hdm->bim', o, wo)
        return r

    def _L1_ffn_ref(x, Wr, W1, W2, W3):
        import jax, jax.numpy as jnp
        import numpy as np
        TOP_K = 2
        B, S, D = x.shape
        E = Wr.shape[1]
        tokens = x.reshape(-1, D)
        logits = tokens @ Wr
        probs = jax.nn.softmax(logits, axis=-1)
        topw, tope = jax.lax.top_k(probs, TOP_K)
        gate = jnp.sum(jax.nn.one_hot(tope, E, dtype=topw.dtype) * topw[..., None], axis=1)
        a = jnp.einsum('td,edh->teh', tokens, W2)
        b = jnp.einsum('td,edh->teh', tokens, W1)
        y = jnp.einsum('teh,ehd->ted', jax.nn.silu(a) * b, W3)
        out = jnp.einsum('ted,te->td', y, gate)
        return out.reshape(B, S, D)

    def _L2_attn_ref(x, Wq, bq, Wk, bk, Wv, bv, Wo, bo):
        import jax, jax.numpy as jnp
        import numpy as np
        import math
        B, L, D, H = (2, 512, 256, 16)

        def _log_sparse_mask(L):
            m = np.zeros((L, L), dtype=bool)
            for i in range(L):
                for k in range(int(math.log2(i + 1)) + 1):
                    j = i - 2 ** k
                    if j >= 0:
                        m[i, j] = True
                m[i, i] = True
            return m
        Bx, Lx, Dx = x.shape
        dh = Dx // H
        scale = math.sqrt(dh)
        mask = jnp.asarray(_log_sparse_mask(Lx))
        q = (x @ Wq.T + bq).reshape(Bx, Lx, H, dh)
        k = (x @ Wk.T + bk).reshape(Bx, Lx, H, dh)
        v = (x @ Wv.T + bv).reshape(Bx, Lx, H, dh)
        raw = jnp.einsum('blhd,bmhd->bhlm', q, k)
        scores = jnp.where(mask, raw, 0.0) / scale
        attn = jax.nn.softmax(scores, axis=-1)
        out = jnp.einsum('bhlm,bmhd->blhd', attn, v).reshape(Bx, Lx, Dx)
        return out @ Wo.T + bo

    def _L2_ffn_ref(x, w_ln1, w_ln2, W_kvd, W_qd, W_ku, W_qu, W_vu, W_ropeq, W_ropek, W_o, Wg_s, Wu_s, Wd_s, Wg_r, Wu_r, Wd_r, W_router, routing_bias):
        import jax, jax.numpy as jnp
        import numpy as np
        H = 256
        NH = 16
        HD = H // NH
        HH = HD // 2
        L = H // 4
        I = int(H * 1.0)
        ER = 7
        TOPK = 2
        BASE = 10000.0
        EPS = 1e-05

        def rmsnorm(x, w):
            norm = jnp.sqrt(jnp.mean(x * x, axis=-1, keepdims=True)) + EPS
            return x / norm * w

        def rope_tables(seq_len):
            inv_freq = 1.0 / BASE ** (jnp.arange(0, HH, 2, dtype=jnp.float32) / HH)
            t = jnp.arange(seq_len, dtype=jnp.float32)
            freqs = jnp.einsum('i,j->ij', t, inv_freq)
            emb = jnp.concatenate([freqs, freqs], axis=-1)
            cos = jnp.cos(emb)[None, :, None, :]
            sin = jnp.sin(emb)[None, :, None, :]
            return (cos, sin)

        def rotate_half(x):
            x1, x2 = jnp.split(x, 2, axis=-1)
            return jnp.concatenate([-x2, x1], axis=-1)

        def silu(x):
            return x * jax.nn.sigmoid(x)

        def mla(xn, W_kvd, W_qd, W_ku, W_qu, W_vu, W_ropeq, W_ropek, W_o):
            B, S, _ = xn.shape
            kv_lat = xn @ W_kvd
            q_lat = xn @ W_qd
            k = (kv_lat @ W_ku).reshape(B, S, NH, HH)
            q = (q_lat @ W_qu).reshape(B, S, NH, HH)
            v = (kv_lat @ W_vu).reshape(B, S, NH, HD)
            q_rope = (q_lat @ W_ropeq).reshape(B, S, NH, HH)
            k_rope = (xn @ W_ropek).reshape(B, S, NH, HH)
            cos, sin = rope_tables(S)
            k_rope = k_rope * cos + rotate_half(k_rope) * sin
            q_rope = q_rope * cos + rotate_half(q_rope) * sin
            kk = jnp.concatenate([k, k_rope], axis=-1)
            qq = jnp.concatenate([q, q_rope], axis=-1)
            scale = 1.0 / jnp.sqrt(jnp.float32(HD))
            scores = jnp.einsum('bqhd,bkhd->bhqk', qq, kk) * scale
            causal = jnp.tril(jnp.ones((S, S), dtype=bool))
            scores = jnp.where(causal[None, None], scores, jnp.finfo(scores.dtype).min)
            probs = jax.nn.softmax(scores, axis=-1)
            y = jnp.einsum('bhqk,bkhd->bqhd', probs, v).reshape(B, S, H)
            return y @ W_o

        def moe(xn, Wg_s, Wu_s, Wd_s, Wg_r, Wu_r, Wd_r, W_router, routing_bias):
            B, S, _ = xn.shape
            xt = xn.reshape(B * S, H)
            shared = silu(xt @ Wg_s) * (xt @ Wu_s) @ Wd_s
            logits = xt @ W_router + routing_bias
            probs = jax.nn.sigmoid(logits)
            scores, idx = jax.lax.top_k(probs, TOPK)
            scores = scores / jnp.sum(scores, axis=-1, keepdims=True)
            wts = jnp.sum(jax.nn.one_hot(idx, ER, dtype=xt.dtype) * scores[..., None], axis=1)
            g = jnp.einsum('th,ehi->tei', xt, Wg_r)
            u = jnp.einsum('th,ehi->tei', xt, Wu_r)
            hmid = silu(g) * u
            combined = jnp.einsum('tei,eih,te->th', hmid, Wd_r, wts)
            return (shared + combined).reshape(B, S, H)
        x = x + mla(rmsnorm(x, w_ln1), W_kvd, W_qd, W_ku, W_qu, W_vu, W_ropeq, W_ropek, W_o)
        x = x + moe(rmsnorm(x, w_ln2), Wg_s, Wu_s, Wd_s, Wg_r, Wu_r, Wd_r, W_router, routing_bias)
        return x

    def _L3_attn_ref(query, in_proj_weight, in_proj_bias, out_proj_weight, out_proj_bias):
        import jax, jax.numpy as jnp
        import numpy as np
        NUM_HEADS = 16
        S, B, E = query.shape
        H = NUM_HEADS
        hd = E // H
        scale = hd ** (-0.5)
        lin = jnp.einsum('sbe,fe->sbf', query, in_proj_weight) + in_proj_bias
        lin = lin.reshape(S, B * H, 3, hd)
        q = lin[:, :, 0, :]
        k = lin[:, :, 1, :]
        v = lin[:, :, 2, :]
        scores = jnp.einsum('sbd,tbd->bst', q, k) * scale
        attn = jax.nn.softmax(scores.astype(jnp.float32), axis=-1).astype(scores.dtype)
        ctx = jnp.einsum('bst,tbd->sbd', attn, v).reshape(S, B, E)
        out = jnp.einsum('sbe,fe->sbf', ctx, out_proj_weight) + out_proj_bias
        return out

    def _L3_ffn_ref(x, router_w, w1, w2):
        import jax, jax.numpy as jnp
        import numpy as np
        B, T, D, FF, E, TOP_K = (4, 512, 256, 1024, 8, 2)
        b, t, d = x.shape
        e, k = (router_w.shape[0], TOP_K)
        xf = x.reshape(-1, d)
        n = xf.shape[0]
        logits = xf @ router_w.T
        topv, topi = jax.lax.top_k(logits, k)
        topw = jax.nn.softmax(topv.astype(jnp.float32), axis=-1).astype(x.dtype)
        idx_flat = topi.reshape(-1)
        w_flat = topw.reshape(-1)
        sort_idx = jnp.argsort(idx_flat)
        src = jnp.repeat(jnp.arange(n), k)
        rev = src[sort_idx]
        sw = w_flat[sort_idx]
        perm = xf[rev]
        chunks = perm.reshape(e, n * k // e, d)
        h = jax.nn.gelu(jnp.einsum('ecd,edf->ecf', chunks, w1), approximate=False)
        y = jnp.einsum('ecf,efd->ecd', h, w2).reshape(n * k, d)
        y = y * sw[:, None]
        out = jnp.zeros((n, d), dtype=x.dtype).at[rev].add(y)
        return out.reshape(b, t, d)
    h = _L0_tok_ref(x, L0_tok_cls_token, L0_tok_cls_pos_embedding, L0_tok_ln1_g, L0_tok_ln1_b, L0_tok_W, L0_tok_bias, L0_tok_ln2_g, L0_tok_ln2_b)
    h = h + _L0_attn_ref(_layernorm(h, axis=-1), L0_attn_Wq, L0_attn_bq, L0_attn_Wk, L0_attn_bk, L0_attn_Wv, L0_attn_bv, L0_attn_Wo, L0_attn_bo, L0_attn_Weq, L0_attn_beq, L0_attn_Wek, L0_attn_bek, L0_attn_amp_w, L0_attn_amp_b, L0_attn_ph_w, L0_attn_ph_b, L0_attn_mix_w, L0_attn_mix_b, L0_attn_ln_g, L0_attn_ln_b)
    h = h + _L0_ffn_ref(_layernorm(h, axis=-1), L0_ffn_router_weight, L0_ffn_router_bias, L0_ffn_gate_up_proj, L0_ffn_gate_up_bias, L0_ffn_down_proj, L0_ffn_down_bias)
    h = h + _L1_attn_ref(_layernorm(h, axis=-1), L1_attn_wq, L1_attn_wk, L1_attn_wv, L1_attn_wo)
    h = h + _L1_ffn_ref(_layernorm(h, axis=-1), L1_ffn_Wr, L1_ffn_W1, L1_ffn_W2, L1_ffn_W3)
    h = h + _L2_attn_ref(_layernorm(h, axis=-1), L2_attn_Wq, L2_attn_bq, L2_attn_Wk, L2_attn_bk, L2_attn_Wv, L2_attn_bv, L2_attn_Wo, L2_attn_bo)
    h = h + _L2_ffn_ref(_layernorm(h, axis=-1), L2_ffn_w_ln1, L2_ffn_w_ln2, L2_ffn_W_kvd, L2_ffn_W_qd, L2_ffn_W_ku, L2_ffn_W_qu, L2_ffn_W_vu, L2_ffn_W_ropeq, L2_ffn_W_ropek, L2_ffn_W_o, L2_ffn_Wg_s, L2_ffn_Wu_s, L2_ffn_Wd_s, L2_ffn_Wg_r, L2_ffn_Wu_r, L2_ffn_Wd_r, L2_ffn_W_router, L2_ffn_routing_bias)
    h = h + _L3_attn_ref(_layernorm(h, axis=-1), L3_attn_in_proj_weight, L3_attn_in_proj_bias, L3_attn_out_proj_weight, L3_attn_out_proj_bias)
    h = h + _L3_ffn_ref(_layernorm(h, axis=-1), L3_ffn_router_w, L3_ffn_w1, L3_ffn_w2)
    return h

_drawn_inputs = setup_inputs


def setup_inputs(seed=0):
    import zlib

    import numpy as np

    out = dict(_drawn_inputs(seed))
    spreads = {'L0_tok_ln1_g': (1.0, 0.2),
     'L0_tok_ln1_b': (0.0, 0.1),
     'L0_tok_bias': (0.0, 0.1),
     'L0_tok_ln2_g': (1.0, 0.2),
     'L0_tok_ln2_b': (0.0, 0.1),
     'L0_attn_bq': (0.0, 0.8),
     'L0_attn_bk': (0.0, 2.0),
     'L0_attn_bv': (0.0, 0.1),
     'L0_attn_bo': (0.0, 0.1),
     'L0_attn_beq': (0.0, 0.8),
     'L0_attn_bek': (0.0, 0.8),
     'L0_attn_amp_b': (0.0, 0.8),
     'L0_attn_ph_b': (0.0, 0.8),
     'L0_attn_mix_b': (0.0, 0.8),
     'L0_attn_ln_g': (1.0, 0.2),
     'L0_attn_ln_b': (0.0, 0.1),
     'L0_ffn_router_bias': (0.0, 0.339),
     'L0_ffn_gate_up_bias': (0.0, 0.8),
     'L0_ffn_down_bias': (0.0, 0.298),
     'L2_attn_bq': (0.0, 0.8),
     'L2_attn_bk': (0.0, 0.8),
     'L2_attn_bv': (0.0, 0.1),
     'L2_attn_bo': (0.0, 0.1),
     'L2_ffn_w_ln1': (1.0, 0.6),
     'L2_ffn_w_ln2': (1.0, 0.6),
     'L2_ffn_routing_bias': (0.0, 0.8),
     'L3_attn_in_proj_bias': (0.0, 0.61),
     'L3_attn_out_proj_bias': (0.0, 0.718)}
    factors = {'L0_attn_Wq': 8.0,
     'L0_attn_Wk': 8.0,
     'L0_attn_Weq': 8.0,
     'L0_attn_Wek': 8.0,
     'L0_attn_amp_w': 8.0,
     'L0_attn_ph_w': 8.0,
     'L0_attn_mix_w': 5.296,
     'L0_ffn_router_weight': 2.689,
     'L0_ffn_gate_up_proj': 3.104,
     'L0_ffn_down_proj': 8.0,
     'L1_attn_wk': 3.097,
     'L1_ffn_Wr': 6.535,
     'L1_ffn_W1': 4.328,
     'L1_ffn_W2': 5.44,
     'L1_ffn_W3': 7.266,
     'L2_attn_Wq': 8.0,
     'L2_attn_Wk': 8.0,
     'L2_ffn_W_kvd': 7.361,
     'L2_ffn_W_qd': 8.0,
     'L2_ffn_W_ku': 8.0,
     'L2_ffn_W_qu': 8.0,
     'L2_ffn_W_vu': 8.0,
     'L2_ffn_W_ropeq': 8.0,
     'L2_ffn_W_ropek': 8.0,
     'L2_ffn_W_o': 5.554,
     'L2_ffn_Wg_s': 4.154,
     'L2_ffn_Wu_s': 4.236,
     'L2_ffn_Wd_s': 4.469,
     'L2_ffn_Wg_r': 4.522,
     'L2_ffn_Wu_r': 7.694,
     'L2_ffn_Wd_r': 5.031,
     'L2_ffn_W_router': 7.094}
    for name, (base, spread) in spreads.items():
        noise = np.random.default_rng([zlib.crc32(name.encode()), seed]).standard_normal(out[name].shape)
        drawn = base * np.exp(spread * noise) if base else spread * noise
        out[name] = jnp.asarray(drawn.astype(out[name].dtype))
    for name, factor in factors.items():
        out[name] = (out[name] * factor).astype(out[name].dtype)
    return out
```

```python
from contextlib import ExitStack

import numpy as np

import concourse.bass as bass
from concourse import mybir

F32 = mybir.dt.float32
U32 = mybir.dt.uint32
ALU = mybir.AluOpType
ACT = mybir.ActivationFunctionType
AX = mybir.AxisListType

P = 128
IMAGES, SEQ, D = 16, 37, 256
GRID, PATCH, CHANNELS = 6, 16, 3
PATCH_DIM = CHANNELS * PATCH * PATCH
TOKENS = IMAGES * SEQ
TILES = -(-TOKENS // P)
PADDED = TILES * P
LAST = TOKENS - (TILES - 1) * P
HALF = TOKENS // 2
Q_COLS = PADDED + 64
KT = D // P
PK = PATCH_DIM // P
HEADS, HD = 16, 16
HPT = P // HD
EPS = 1e-5
REP = 3
BLOCKS = -(-HEADS // REP)
PAIR = 64 + SEQ

L0_E, L0_TOP, L0_ALPHA, L0_LIMIT = 16, 4, 1.702, 7.0
L1_E, L1_HID, L1_PAD = 8, 352, 384
L2_E = 8
L3_E, L3_FF, L3_TOP = 8, 1024, 2
CHUNK = TOKENS * L3_TOP // L3_E
HCH = CHUNK // 2
L3_GROUPS = -(-SEQ // 4)


def offsets(parts):
    at, out = 0, {}
    for name, width in parts:
        out[name] = (at, width)
        at += width
    return out, at


WEIGHTS = {
    "tok": [("tok_w", PK * D)],
    "l0": [(n, KT * D) for n in ("l0_q", "l0_k", "l0_v", "l0_eq", "l0_ek", "l0_o", "l0_mix")]
    + [("l0_ampph", KT * 2 * HEADS), ("l0_router", KT * L0_E), ("l0_down_b", D)],
    "l1": [(n, KT * D) for n in ("l1_q", "l1_qrot", "l1_k", "l1_krot", "l1_v", "l1_o")] + [("l1_router", KT * L1_E)],
    "l2": [(n, KT * D) for n in ("l2_q", "l2_k", "l2_v", "l2_o")],
    "mla": [("mla_lat", KT * P), ("mla_q", D), ("mla_qrot", D), ("mla_k_lat", D), ("mla_k", KT * D),
            ("mla_krot", KT * D), ("mla_v", D), ("mla_o", KT * D), ("mla_router", KT * 8)],
    "l3": [(n, KT * D) for n in ("l3_q", "l3_k", "l3_v", "l3_o")] + [("l3_router", KT * L3_E)],
}
WEIGHT_AT, WEIGHT_COLS = offsets([p for parts in WEIGHTS.values() for p in parts])
COL_AT, COL_COLS = offsets([
    ("ln1_g", PK), ("ln1_b", PK), ("l0_bq", 2), ("l0_bk", 2), ("l0_beq", 2), ("l0_bek", 2), ("l0_bv", 2),
    ("l2_bq", 2), ("l2_bk", 2), ("w_ln1", 2), ("w_ln2", 2), ("l3_bq", 2), ("l3_bk", 2),
    ("l0_gub", L0_E * 4)])
ROW_AT, ROW_COLS = offsets([
    ("cls", D), ("cls_pos", D), ("tok_b", D), ("ln2_g", D), ("ln2_b", D), ("l0_bv", D), ("l0_bo", D),
    ("l0_ln_g", D), ("l0_ln_b", D), ("l0_mixb", 2 * D), ("l0_ampphb", 2 * HEADS), ("l0_rb", L0_E),
    ("l2_bv", D), ("l2_bo", D), ("mla_rb", 8), ("l3_bv", D), ("l3_bo", D)])
CONST_AT, CONST_COLS = offsets([
    ("ident", P), ("ones", P), ("before", P), ("headmask", HPT), ("vmask37", HEADS), ("vmask16", HEADS),
    ("decay", SEQ), ("sparse", SEQ), ("causal", SEQ), ("cos1", SEQ), ("sin1", SEQ), ("cos2", SEQ),
    ("sin2", SEQ), ("pe", TILES * D), ("is_patch", TILES), ("is_cls", TILES), ("valid", TILES),
    ("earlier16", 256), ("earlier8", 64), ("earlier7", 49)])


def constants():
    f = np.float32
    c = {}
    i128 = np.arange(P)
    c["ident"] = np.eye(P, dtype=f)
    c["ones"] = np.ones((P, P), f)
    c["before"] = (i128[:, None] < i128[None, :]).astype(f)
    c["headmask"] = (i128[:, None] // HD == np.arange(HPT)[None]).astype(f)
    c["vmask37"] = (i128[:, None] // SEQ == np.arange(HEADS)[None] % REP).astype(f)
    c["vmask16"] = (i128[:, None] // HD == np.arange(HEADS)[None] % HPT).astype(f)
    q = np.where(i128 % 64 < SEQ, i128 % 64, 0)
    j = np.arange(SEQ)
    c["decay"] = (f(0.5) * np.exp(f(-0.1) * np.abs(q[:, None] - j[None]).astype(f))).astype(f)
    sparse = np.zeros((SEQ, SEQ), f)
    for r in range(SEQ):
        sparse[r, r] = 1
        k = 0
        while 2 ** k <= r + 1:
            if r - 2 ** k >= 0:
                sparse[r, r - 2 ** k] = 1
            k += 1
    c["sparse"] = sparse[q]
    c["causal"] = np.where(q[:, None] >= j[None], 0, -1e30).astype(f)
    half = 64
    freq = np.power(f(10000.0), -(np.arange(half, dtype=f) / f(half))).astype(f)
    rad = (j.astype(f)[:, None] * freq[None]).astype(f)
    c["cos1"] = np.concatenate([np.cos(rad), np.cos(rad)], 1).T.astype(f)
    c["sin1"] = np.concatenate([-np.sin(rad), np.sin(rad)], 1).T.astype(f)
    inv = (f(1.0) / np.power(f(10000.0), np.arange(0, 8, 2, dtype=f) / f(8))).astype(f)
    ang = (j.astype(f)[:, None] * inv[None]).astype(f)
    cos8, sin8 = np.concatenate([np.cos(ang)] * 2, 1), np.concatenate([-np.sin(ang), np.sin(ang)], 1)
    head_cos = np.concatenate([np.ones((SEQ, 8)), cos8], 1)
    head_sin = np.concatenate([np.zeros((SEQ, 8)), sin8], 1)
    c["cos2"] = np.tile(head_cos, (1, HPT)).T.astype(f)
    c["sin2"] = np.tile(head_sin, (1, HPT)).T.astype(f)
    omega = (f(1.0) / np.power(f(10000.0), np.arange(D // 4, dtype=f) / f(D // 4 - 1))).astype(f)
    yy, xx = np.meshgrid(np.arange(GRID), np.arange(GRID), indexing="ij")
    ya, xa = yy.reshape(-1, 1) * omega[None], xx.reshape(-1, 1) * omega[None]
    pe = np.concatenate([np.sin(xa), np.cos(xa), np.sin(ya), np.cos(ya)], 1).astype(f)
    rows = np.zeros((PADDED, D), f)
    patch, cls, valid = (np.zeros(PADDED, f) for _ in range(3))
    for b in range(IMAGES):
        rows[b * SEQ + 1:(b + 1) * SEQ] = pe
        patch[b * SEQ + 1:(b + 1) * SEQ] = 1
        cls[b * SEQ] = 1
    valid[:TOKENS] = 1
    c["pe"] = tiled(rows)
    for name, v in (("is_patch", patch), ("is_cls", cls), ("valid", valid)):
        c[name] = np.ascontiguousarray(v.reshape(TILES, P).T)
    for e in (16, 8, 7):
        lower = (np.arange(e)[None] < np.arange(e)[:, None]).astype(f)
        c[f"earlier{e}"] = np.tile(lower.reshape(1, -1), (P, 1))
    return np.concatenate([c[n].reshape(P, -1) for n in CONST_AT], 1).astype(f)


def tiled(rows):
    n = rows.shape[1]
    return np.ascontiguousarray(rows.reshape(-1, P, n).transpose(1, 0, 2)).reshape(P, -1)


def ordered(eng, sem, start=0):
    count = [0]

    def signal(ins):
        ins.then_inc(sem, 1)
        count[0] += 1

    def wait():
        eng.wait_ge(sem, start + count[0])

    def link(ins):
        signal(ins)
        wait()
    return link, signal, wait, count


def spread(ap, pattern, shape, **sizes):
    return ap.rearrange(pattern, **sizes).broadcast_to(shape)


def pipeline(eng, total, late, step):
    def has(m):
        return not isinstance(m, int) or 0 <= m < total

    for n in range(2):
        step(n, n % 2, n // 2, has)
    with eng.Fori(1, total // 2) as i:
        for u in range(2):
            step(i * 2 + u, u, i, has)
    for n in range(total - total % 2, total + late):
        step(n, n % 2, n // 2, has)


def build(nc, a, out):
    with ExitStack() as ctx:
        names = set()
        retired = []

        def sb(name, shape, dt=F32, where=ctx):
            return where.enter_context(nc.sbuf_tensor(name, shape, dt))

        def sem(name, where=None):
            assert name not in names
            names.add(name)
            if where is None:
                return ctx.enter_context(nc.semaphore(name))
            retired.append(nc.alloc_semaphore(name))
            return retired[-1]

        def recycle():
            nc.clear_and_free_semaphores(retired)
            del retired[:]
            nc.all_engine_barrier()

        ps = ctx.enter_context(nc.psum_tensor("ps", [P, 8, 512], F32))
        w_sb = sb("w_sb", [P, WEIGHT_COLS])
        col_sb = sb("col_sb", [P, COL_COLS])
        row_sb = sb("row_sb", [P, ROW_COLS])
        const_sb = sb("const_sb", [P, CONST_COLS])
        h = sb("h", [P, TILES, D])
        xn = sb("xn", [P, TILES, D])
        x_fm = sb("x_fm", [P, KT, PADDED])
        v_dram = nc.dram_tensor("v_scratch", [PADDED, D], F32).ap()
        perm_dram = nc.dram_tensor("perm_scratch", [TOKENS * L3_TOP, D], F32).ap()
        y_dram = nc.dram_tensor("y_scratch", [TOKENS * L3_TOP, D], F32).ap()

        def weight(name, k=KT):
            at, width = WEIGHT_AT[name]
            return w_sb[:, at:at + width].rearrange("p (k n) -> p k n", k=k)

        def col(name, i=0, n=1):
            at = COL_AT[name][0] + i
            return col_sb[:, at:at + n]

        def row(name, n=None):
            at, width = ROW_AT[name]
            return row_sb[:, at:at + (n or width)]

        def const(name):
            at, width = CONST_AT[name]
            return const_sb[:, at:at + width]

        ident = const("ident")
        loaded = {n: sem(f"loaded_{n}") for n in [*WEIGHTS, "cols", "rows", "consts", "patches"]}

        norm = {n: sem(f"norm_{n}") for n in ("chain", "var", "rstd", "normed", "turned", "copied_a", "copied_v")}
        norm_stats = sb("norm_stats", [P, TILES, 6])
        norm_mv = sb("norm_mv", [P, TILES, 2])
        norm_ve = sb("norm_ve", [P, TILES])
        norm_pow = sb("norm_pow", [P, TILES])
        norm_r = sb("norm_r", [P, TILES])
        done = {"norms": 0, "chain": 0}

        def normalise(src, dst, rms=False, scale=None):
            n = done["norms"]
            done["norms"] += 1
            with nc.Block() as block:
                @block.vector
                def _(dve):
                    link, signal, wait, count = ordered(dve, norm["chain"], done["chain"])
                    for t in range(TILES):
                        signal(dve.bn_stats(norm_stats[:, t, :], src[:, t, :]))
                    wait()
                    for t in range(TILES):
                        signal(dve.bn_aggr(norm_mv[:, t, :], norm_stats[:, t, :]))
                    wait()
                    if rms:
                        link(dve.tensor_tensor(norm_ve[:, :], norm_mv[:, :, 0], norm_mv[:, :, 0], ALU.mult))
                        dve.tensor_tensor(norm_ve[:, :], norm_ve[:, :], norm_mv[:, :, 1], ALU.add)\
                            .then_inc(norm["var"], 1)
                    else:
                        dve.tensor_scalar(norm_ve[:, :], norm_mv[:, :, 1], EPS, None, ALU.add)\
                            .then_inc(norm["var"], 1)
                    dve.wait_ge(norm["rstd"], 2 * (n + 1))
                    if rms:
                        link(dve.tensor_scalar(norm_r[:, :], norm_r[:, :], EPS, None, ALU.add))
                        link(dve.reciprocal(norm_r[:, :], norm_r[:, :]))
                    for t in range(TILES):
                        if rms:
                            ins = dve.tensor_scalar(dst[:, t, :], src[:, t, :], norm_r[:, t:t + 1], None, ALU.mult)
                        else:
                            ins = dve.tensor_scalar(dst[:, t, :], src[:, t, :], norm_mv[:, t, 0:1],
                                                    norm_r[:, t:t + 1], ALU.subtract, ALU.mult)
                        ins.then_inc(norm["normed"], 1)
                    done["chain"] += count[0]
                    for part, (c0, c1) in enumerate(((0, 512), (512, PADDED))):
                        dve.wait_ge(norm["turned"], 2 * n + part + 1)
                        o, i = x_fm[:, 1, c0:c1], ps[:, 2 + part, 0:c1 - c0]
                        if scale is None:
                            dve.tensor_copy(o, i).then_inc(norm["copied_v"], 1)
                        else:
                            dve.tensor_scalar(o, i, col(scale, 1), None, ALU.mult).then_inc(norm["copied_v"], 1)

                @block.gpsimd
                def _(pool):
                    pool.memset(norm_pow[:, :], 0.5 if rms else -0.5).then_inc(norm["rstd"], 1)
                    pool.wait_ge(norm["rstd"], 2 * n + 1)
                    pool.wait_ge(norm["var"], n + 1)
                    pool.tensor_tensor(norm_r[:, :], norm_ve[:, :], norm_pow[:, :], ALU.pow)\
                        .then_inc(norm["rstd"], 1)

                @block.tensor
                def _(pe):
                    for t in range(TILES):
                        pe.wait_ge(norm["normed"], TILES * n + t + 1)
                        for k in range(KT):
                            o = ps[:, 2 * k + t // 4, (t % 4) * P:(t % 4 + 1) * P]
                            mm = pe.transpose(o, dst[:, t, k * P:(k + 1) * P], ident)
                        if t >= 3:
                            mm.then_inc(norm["turned"], 1)

                @block.scalar
                def _(act):
                    for part, (c0, c1) in enumerate(((0, 512), (512, PADDED))):
                        act.wait_ge(norm["turned"], 2 * n + part + 1)
                        act.activation(x_fm[:, 0, c0:c1], ps[:, part, 0:c1 - c0], ACT.Copy,
                                       scale=1.0 if scale is None else col(scale, 0))\
                            .then_inc(norm["copied_a"], 1)

        def tokens():
            with ExitStack() as st:
                pat = sb("pat", [P, TILES, PATCH_DIM], where=st)
                pat_n = sb("pat_n", [P, TILES, PATCH_DIM], where=st)
                pat_fm = sb("pat_fm", [P, PK, PADDED], where=st)
                stats = sb("tok_stats", [P, TILES, 2, 6], where=st)
                mv = sb("tok_mv", [P, TILES, 2], where=st)
                ve = sb("tok_ve", [P, TILES], where=st)
                pw = sb("tok_pow", [P, TILES], where=st)
                r = sb("tok_r", [P, TILES], where=st)
                s_chain, s_var, s_rstd, s_normed, s_turned, s_fm, s_mm = (
                    sem(f"tok_{n}") for n in ("chain", "var", "rstd", "normed", "turned", "fm", "mm"))

                with nc.Block() as block:
                    @block.sync
                    def _(sp):
                        for t in range(TILES):
                            sp.dma_start(pat[:, t, :], a["patches"][:, t * PATCH_DIM:(t + 1) * PATCH_DIM])\
                                .then_inc(loaded["patches"], 16)
                        for n, parts in WEIGHTS.items():
                            c0 = WEIGHT_AT[parts[0][0]][0]
                            c1 = sum(WEIGHT_AT[parts[-1][0]])
                            sp.dma_start(w_sb[:, c0:c1], a["weights"][:, c0:c1]).then_inc(loaded[n], 16)

                    @block.scalar
                    def _(act):
                        act.dma_start(const_sb[:, :], a["consts"]).then_inc(loaded["consts"], 16)
                        act.dma_start(col_sb[:, :], a["cols"]).then_inc(loaded["cols"], 16)
                        act.dma_start(row_sb[:, :], a["rows"].broadcast_to([P, ROW_COLS])).then_inc(loaded["rows"], 16)
                        act.wait_ge(loaded["cols"], 16)
                        for k in range(PK):
                            act.wait_ge(s_turned, k + 1)
                            for part, (c0, c1) in enumerate(((0, 512), (512, PADDED))):
                                act.activation(pat_fm[:, k, c0:c1], ps[:, 2 * (k % 2) + part, 0:c1 - c0],
                                               ACT.Identity, scale=col("ln1_g", k), bias=col("ln1_b", k))\
                                    .then_inc(s_fm, 1)

                    @block.gpsimd
                    def _(pool):
                        pool.memset(pw[:, :], -0.5).then_inc(s_rstd, 1)
                        pool.wait_ge(s_rstd, 1)
                        for i in range(2):
                            pool.wait_ge(s_var, i + 1)
                            pool.tensor_tensor(r[:, :], ve[:, :], pw[:, :], ALU.pow).then_inc(s_rstd, 1)

                    @block.tensor
                    def _(pe):
                        pe.wait_ge(loaded["consts"], 16)
                        pe.wait_ge(s_normed, TILES)
                        for k in range(PK):
                            if k >= 2:
                                pe.wait_ge(s_fm, 2 * (k - 1))
                            for t in range(TILES):
                                o = ps[:, 2 * (k % 2) + t // 4, (t % 4) * P:(t % 4 + 1) * P]
                                mm = pe.transpose(o, pat_n[:, t, k * P:(k + 1) * P], ident)
                            mm.then_inc(s_turned, 1)
                        pe.wait_ge(s_fm, 2 * PK)
                        pe.wait_ge(loaded["tok"], 16)
                        for t in range(TILES):
                            for k in range(PK):
                                mm = pe.matmul(ps[:, 4 + t // 2, (t % 2) * D:(t % 2 + 1) * D],
                                               pat_fm[:, k, t * P:(t + 1) * P], weight("tok_w", PK)[:, k, :],
                                               start=(k == 0), stop=(k == PK - 1))
                            if t % 2 or t == TILES - 1:
                                mm.then_inc(s_mm, 1)

                    @block.vector
                    def _(dve):
                        link, signal, wait, count = ordered(dve, s_chain)

                        def moments(width):
                            for t in range(TILES):
                                for q in range(2):
                                    n = width // 2
                                    src = pat if width == PATCH_DIM else h
                                    signal(dve.bn_stats(stats[:, t, q, :], src[:, t, q * n:(q + 1) * n]))
                            wait()
                            for t in range(TILES):
                                signal(dve.bn_aggr(mv[:, t, :], stats[:, t, :, :]))
                            wait()
                            dve.tensor_scalar(ve[:, :], mv[:, :, 1], EPS, None, ALU.add).then_inc(s_var, 1)

                        dve.wait_ge(loaded["patches"], 16 * TILES)
                        moments(PATCH_DIM)
                        dve.wait_ge(s_rstd, 2)
                        for t in range(TILES):
                            dve.tensor_scalar(pat_n[:, t, :], pat[:, t, :], mv[:, t, 0:1], r[:, t:t + 1],
                                              ALU.subtract, ALU.mult).then_inc(s_normed, 1)
                        dve.wait_ge(loaded["rows"], 16)
                        for t in range(TILES):
                            dve.wait_ge(s_mm, t // 2 + 1)
                            signal(dve.tensor_tensor(h[:, t, :], ps[:, 4 + t // 2, (t % 2) * D:(t % 2 + 1) * D],
                                                           row("tok_b"), ALU.add))
                        wait()
                        moments(D)
                        link(dve.tensor_tensor(row("cls"), row("cls"), row("cls_pos"), ALU.add))
                        dve.wait_ge(s_rstd, 3)
                        dve.wait_ge(loaded["consts"], 16)
                        pe_rows = const("pe").rearrange("p (t d) -> p t d", t=TILES)
                        for t in range(TILES):
                            x = h[:, t, :]
                            link(dve.tensor_scalar(x, x, mv[:, t, 0:1], r[:, t:t + 1],
                                                         ALU.subtract, ALU.mult))
                            link(dve.tensor_tensor(x, x, row("ln2_g"), ALU.mult))
                            link(dve.tensor_tensor(x, x, row("ln2_b"), ALU.add))
                            link(dve.scalar_tensor_tensor(out=x, in0=x, scalar=const("is_patch")[:, t:t + 1],
                                                                in1=pe_rows[:, t, :], op0=ALU.mult, op1=ALU.add))
                            link(dve.scalar_tensor_tensor(out=x, in0=row("cls"),
                                                                scalar=const("is_cls")[:, t:t + 1],
                                                                in1=x, op0=ALU.mult, op1=ALU.add))

        def attend(tag, ctx_fm, q_fm, k_fm, eq_fm=None, ek_fm=None, mask=None, mask_op=None, scale=1.0):
            pairs = IMAGES // 2
            second = eq_fm is not None
            NMM = 2 if second else 1
            with ExitStack() as st:
                q_st = sb(f"{tag}_q_st", [P, 2, NMM, KT, PAIR], where=st)
                k_bd = sb(f"{tag}_k_bd", [P, 2, 2, NMM, KT, HPT, SEQ], where=st)
                v_rep = sb(f"{tag}_v_rep", [P, 2, 2, D], where=st)
                v_bd = sb(f"{tag}_v_bd", [P, 2, 2, HEADS, HD + 1], where=st)
                e_sc = sb(f"{tag}_e_sc", [P, KT, HPT, SEQ], where=st)
                shifted = sb(f"{tag}_shifted", [P, 2, HEADS, SEQ], where=st)
                top = sb(f"{tag}_top", [P, 2, HEADS], where=st)
                probs = sb(f"{tag}_probs", [P, 2, HEADS * SEQ], where=st)
                p_fm = sb(f"{tag}_p_fm", [P, 2, BLOCKS, PAIR], where=st)
                recip = sb(f"{tag}_recip", [P, 2, HEADS], where=st)
                ctx_tm = sb(f"{tag}_ctx_tm", [P, 2, HEADS, HD], where=st)
                s_vrep0, s_vrep1, s_vbd, s_stage, s_kbd, s_scores, s_shift, s_probs, s_pt, s_pfm, s_av, s_ctx, s_ct, \
                    s_ctfm, s_soft, s_norm, s_vmask = (sem(f"{tag}_{n}", st) for n in (
                        "vrep0", "vrep1", "vbd", "stage", "kbd", "scores", "shift", "probs", "pt", "pfm", "av", "ctx",
                        "ct", "ctfm", "soft", "norm", "vmask"))
                s_vrep = (s_vrep0, s_vrep1)

                with nc.Block() as block:
                    @block.sync
                    def _(sp):
                        def step(n, u, r, has):
                            if has(n):
                                if has(n - 2):
                                    sp.wait_ge(s_vbd, n * 2 - 2)
                                src = v_dram[bass.ds(n * (2 * SEQ), 2 * SEQ), :].rearrange("(s j) d -> j s d", s=2)
                                for q in range(REP):
                                    sp.dma_start(v_rep[q * SEQ:(q + 1) * SEQ, u, :, :], src).then_inc(s_vrep[u], 16)
                        pipeline(sp, pairs, 0, step)

                    @block.gpsimd
                    def _(pool):
                        vm = const("vmask37")
                        for u in range(2):
                            for s in range(2):
                                pool.tensor_copy(v_bd[:, u, s, :, HD], vm).then_inc(s_vmask, 1)
                        vm = spread(vm[0:REP * SEQ], "p (h o) -> p h o", [REP * SEQ, HEADS, HD], o=1)
                        hm = spread(const("headmask"), "p (a h o) -> p a h o", [P, KT, HPT, SEQ], a=1, o=1)

                        def step(n, u, r, has):
                            if not has(n):
                                return
                            if has(n - 2):
                                pool.wait_ge(s_scores, n - 1)
                                pool.wait_ge(s_av, n - 1)
                            for m, fm in enumerate((k_fm, ek_fm)[:NMM]):
                                for s in range(2):
                                    src = fm[:, :, bass.ds(n * (2 * SEQ) + s * SEQ, SEQ)]
                                    pool.tensor_tensor(
                                        k_bd[:, u, s, m, :, :, :],
                                        spread(src, "p k (o j) -> p k o j", [P, KT, HPT, SEQ], o=1),
                                        hm, ALU.mult).then_inc(s_kbd, 1)
                            pool.wait_ge(s_vrep[u], (r + 1) * (16 * REP))
                            for s in range(2):
                                src = v_rep[0:REP * SEQ, u, s, :].rearrange("p (h d) -> p h d", h=HEADS)
                                pool.tensor_tensor(v_bd[0:REP * SEQ, u, s, :, 0:HD], src, vm, ALU.mult)\
                                    .then_inc(s_vbd, 1)
                        pipeline(pool, pairs, 0, step)

                    @block.scalar
                    def _(act):
                        act.preload_act_table(ACT.Exp)
                        act.sem_inc(s_ctfm, 1)

                        def stage(n, u):
                            for m, fm in enumerate((q_fm, eq_fm)[:NMM]):
                                act.activation(q_st[:, u, m, :, :], fm[:, :, bass.ds(n * (2 * SEQ), PAIR)],
                                               ACT.Copy).then_inc(s_stage, 1)

                        def step(n, u, r, has):
                            if isinstance(n, int) and n == 0:
                                stage(0, 0)
                            if has(n):
                                if has(n - 1):
                                    act.wait_ge(s_scores, n)
                                stage(n + 1, 1 - u)
                            if has(n - 2):
                                act.wait_ge(s_ct, n - 1)
                                src = ps[:, 7, 0:KT * P].rearrange("p (k s j) -> p k s j", k=KT, s=2)
                                dst = ctx_fm[:, :, bass.ds((n - 2) * (2 * SEQ), 2 * SEQ)]
                                act.activation(dst.rearrange("p k (s j) -> p k s j", s=2), src[:, :, :, 0:SEQ],
                                               ACT.Copy).then_inc(s_ctfm, 1)
                            if has(n - 1):
                                act.wait_ge(s_pt, n)
                                act.activation(
                                    p_fm[0:REP * SEQ, 1 - u, 0:4, :],
                                    ps[0:REP * SEQ, 4, :].rearrange("p (b r) -> p b r", b=4)[:, :, 0:PAIR],
                                    ACT.Copy).then_inc(s_pfm, 1)
                                act.activation(p_fm[0:REP * SEQ, 1 - u, 4, :], ps[0:REP * SEQ, 5, 0:PAIR],
                                               ACT.Copy).then_inc(s_pfm, 1)
                                act.activation(p_fm[0:SEQ, 1 - u, 5, :], ps[0:SEQ, 5, P:P + PAIR],
                                               ACT.Copy).then_inc(s_pfm, 1)
                            if has(n):
                                act.wait_ge(s_shift, n + 1)
                                act.activation(probs[:, u, :], shifted[:, u, :, :].rearrange("p h j -> p (h j)"),
                                               ACT.Exp, scale=scale).then_inc(s_probs, 1)
                        pipeline(act, pairs, 2, step)

                    @block.tensor
                    def _(pe):
                        def step(n, u, r, has):
                            v = 1 - u
                            if has(n):
                                pe.wait_ge(s_stage, (n + 1) * NMM)
                                pe.wait_ge(s_kbd, (n + 1) * (2 * NMM))
                                if has(n - 1):
                                    pe.wait_ge(s_shift, n)
                                for m in range(NMM):
                                    for s in range(2):
                                        for k in range(KT):
                                            mm = pe.matmul(
                                                ps[64 * s:64 * s + 64, 2 * m + k, 0:HPT * SEQ],
                                                q_st[:, u, m, k, SEQ * s:SEQ * s + 64],
                                                k_bd[:, u, s, m, k, :, :].rearrange("p h j -> p (h j)"),
                                                start=True, stop=True)
                                mm.then_inc(s_scores, 1)
                            if has(n - 2):
                                pe.wait_ge(s_ctx, n - 1)
                                pe.wait_ge(s_ctfm, n - 1)
                                for k in range(KT):
                                    mm = pe.transpose(ps[:, 7, k * P:k * P + PAIR],
                                                      ctx_tm[0:PAIR, u, k * HPT:(k + 1) * HPT, :]
                                                      .rearrange("p h d -> p (h d)"), ident[0:PAIR, 0:PAIR])
                                mm.then_inc(s_ct, 1)
                            if has(n - 1):
                                pe.wait_ge(s_probs, n)
                                if has(n - 2):
                                    pe.wait_ge(s_pfm, n * 3 - 3)
                                for b in range(BLOCKS):
                                    w = min(REP, HEADS - REP * b) * SEQ
                                    mm = pe.transpose(ps[0:w, 4 + b // 4, (b % 4) * P:(b % 4 + 1) * P],
                                                      probs[:, v, b * REP * SEQ:b * REP * SEQ + w], ident)
                                mm.then_inc(s_pt, 1)
                                pe.wait_ge(s_pfm, n * 3)
                                pe.wait_ge(s_vbd, n * 2)
                                pe.wait_ge(s_vmask, 4)
                                for s in range(2):
                                    rows = 64 if s == 0 else SEQ
                                    for b in range(BLOCKS):
                                        nh = min(REP, HEADS - REP * b)
                                        mm = pe.matmul(
                                            ps[64 * s:64 * s + rows, 6,
                                               b * REP * (HD + 1):(b * REP + nh) * (HD + 1)],
                                            p_fm[0:nh * SEQ, v, b, 64 * s:64 * s + rows],
                                            v_bd[0:nh * SEQ, v, s, b * REP:b * REP + nh, :]
                                            .rearrange("p h d -> p (h d)"),
                                            start=True, stop=True)
                                mm.then_inc(s_av, 1)
                        pipeline(pe, pairs, 2, step)

                    @block.vector
                    def _(dve):
                        soft_links = 3 if second else 2
                        m4 = spread(mask, "p (a b j) -> p a b j", [P, KT, HPT, SEQ], a=1, b=1)
                        scores = ps[:, 0:2, 0:HPT * SEQ].rearrange("p k (h j) -> p k h j", h=HPT)
                        scores2 = ps[:, 2:4, 0:HPT * SEQ].rearrange("p k (h j) -> p k h j", h=HPT)
                        out3 = ps[0:PAIR, 6, 0:HEADS * (HD + 1)].rearrange("p (h d) -> p h d", h=HEADS)

                        def step(n, u, r, has):
                            if has(n):
                                link, signal, wait, count = ordered(dve, s_soft, n * soft_links)
                                dve.wait_ge(s_scores, n + 1)
                                if second:
                                    link(dve.tensor_tensor(e_sc[:, :, :, :], scores2, m4, ALU.mult))
                                    link(dve.tensor_tensor(scores, scores, e_sc[:, :, :, :], ALU.add))
                                else:
                                    link(dve.tensor_tensor(scores, scores, m4, mask_op))
                                t3 = top[:, u, :].rearrange("p (k h) -> p k h", k=KT)
                                link(dve.tensor_reduce(t3, scores, AX.X, ALU.max))
                                dve.tensor_tensor(shifted[:, u, :, :].rearrange("p (k h) j -> p k h j", k=KT), scores,
                                                  spread(t3, "p k (h o) -> p k h o", [P, KT, HPT, SEQ], o=1),
                                                  ALU.subtract).then_inc(s_shift, 1)
                            if has(n - 1):
                                dve.wait_ge(s_av, n)
                                dve.reciprocal(recip[0:PAIR, u, :], out3[:, :, HD]).then_inc(s_norm, 1)
                                dve.wait_ge(s_norm, n)
                                dve.tensor_tensor(ctx_tm[0:PAIR, 1 - u, :, :], out3[:, :, 0:HD],
                                                  spread(recip[0:PAIR, u, :], "p (h o) -> p h o",
                                                         [PAIR, HEADS, HD], o=1), ALU.mult).then_inc(s_ctx, 1)
                        pipeline(dve, pairs, 2, step)


        def project(tag, layer, jobs, v_terms, v_bias=None, v_tm=None, pads=()):
            rot = jobs[0][1] is not None
            slots = 2 if rot else 4
            units = [(job, half) for job in jobs for half in range(2)]
            with ExitStack() as st:
                own_v = v_tm is None
                v_tm = v_tm if v_tm is not None else sb(f"{tag}_v_tm", [P, TILES, D], where=st)
                t1 = sb(f"{tag}_rot_a", [P, 2, HALF], where=st)
                t2 = sb(f"{tag}_rot_b", [P, 2, HALF], where=st)
                s_unit, s_v, s_vout, s_vd, s_pads, s_t, s_sum = (
                    sem(f"{tag}_{n}", st) for n in ("unit", "v", "vout", "vd", "pads", "t", "sum"))
                s_free = [sem(f"{tag}_free{i}", st) for i in range(slots)]

                with nc.Block() as block:
                    @block.tensor
                    def _(pe):
                        pe.wait_ge(loaded[layer], 16)
                        for t in range(TILES):
                            if t >= 4:
                                pe.wait_ge(s_vout, t - 3)
                            for k, (w, src) in enumerate(v_terms):
                                mm = pe.matmul(ps[:, 4 + t % 4, 0:D], src[:, t * P:(t + 1) * P], w,
                                               start=(k == 0), stop=(k == len(v_terms) - 1))
                            mm.then_inc(s_v, 1)
                        for i, ((terms, rterms, _, _, _, _), half) in enumerate(units):
                            slot = i % slots
                            if i >= slots:
                                pe.wait_ge(s_free[slot], i // slots)
                            c0 = half * HALF
                            for b, part in enumerate((terms, rterms) if rot else (terms,)):
                                for k, (w, src) in enumerate(part):
                                    mm = pe.matmul(ps[:, slot * (2 if rot else 1) + b, 0:HALF], w,
                                                   src[:, c0:c0 + HALF], start=(k == 0), stop=(k == len(part) - 1))
                            mm.then_inc(s_unit, 1)

                    @block.vector
                    def _(dve):
                        for t in range(TILES):
                            dve.wait_ge(s_v, t + 1)
                            src = ps[:, 4 + t % 4, 0:D]
                            if v_bias is None:
                                dve.tensor_copy(v_tm[:, t, :], src).then_inc(s_vout, 1)
                            else:
                                dve.tensor_tensor(v_tm[:, t, :], src, v_bias, ALU.add).then_inc(s_vout, 1)
                        for i, ((_, _, dst, bias, cos, sin), half) in enumerate(units):
                            slot, c0 = i % slots, half * HALF
                            if rot:
                                dve.wait_ge(s_unit, i + 1)
                                if i >= 2:
                                    dve.wait_ge(s_sum, i - 1)
                                shape = [P, HALF // SEQ, SEQ]
                                for b, (table, t) in enumerate(((cos, t1), (sin, t2))):
                                    ins = dve.tensor_tensor(
                                        t[:, i % 2, :].rearrange("p (i j) -> p i j", j=SEQ),
                                        ps[:, slot * 2 + b, 0:HALF].rearrange("p (i j) -> p i j", j=SEQ),
                                        spread(table, "p (a j) -> p a j", shape, a=1), ALU.mult)
                                    ins.then_inc(s_free[slot] if b else s_t, 1)
                            elif slot % 2:
                                dve.wait_ge(s_unit, i + 1)
                                dst, src = dst[:, c0:c0 + HALF], ps[:, slot, 0:HALF]
                                if bias is None:
                                    dve.tensor_copy(dst, src).then_inc(s_free[slot], 1)
                                else:
                                    dve.tensor_scalar(dst, src, bias, None, ALU.add).then_inc(s_free[slot], 1)

                    @block.scalar
                    def _(act):
                        if not rot:
                            for i, ((_, _, dst, bias, _, _), half) in enumerate(units):
                                slot, c0 = i % slots, half * HALF
                                if slot % 2 == 0:
                                    act.wait_ge(s_unit, i + 1)
                                    act.activation(dst[:, c0:c0 + HALF], ps[:, slot, 0:HALF], ACT.Identity,
                                                   bias=0.0 if bias is None else bias).then_inc(s_free[slot], 1)

                    @block.gpsimd
                    def _(pool):
                        for p in pads:
                            pool.memset(p, 0.0).then_inc(s_pads, 1)
                        if rot:
                            for i, ((_, _, dst, _, _, _), half) in enumerate(units):
                                c0 = half * HALF
                                pool.wait_ge(s_t, i + 1)
                                pool.wait_ge(s_free[i % slots], i // slots + 1)
                                pool.tensor_tensor(dst[:, c0:c0 + HALF], t1[:, i % 2, :], t2[:, i % 2, :],
                                                   ALU.add).then_inc(s_sum, 1)

                    @block.sync
                    def _(sp):
                        if own_v:
                            for t in range(TILES):
                                sp.wait_ge(s_vout, t + 1)
                                sp.dma_start(v_dram[t * P:(t + 1) * P, :], v_tm[:, t, :]).then_inc(s_vd, 16)
                            sp.wait_ge(s_vd, 16 * TILES)

        def plain(w_name, dst, bias=None):
            w = weight(w_name)
            return [([(w[:, k, m * P:(m + 1) * P], x_fm[:, k, :]) for k in range(KT)], None, dst[:, m, :],
                     None if bias is None else col(bias, m), None, None) for m in range(KT)]

        def value_terms(w_name):
            return [(weight(w_name)[:, k, :], x_fm[:, k, :]) for k in range(KT)]

        def project_out(tag, ctx_fm, w_name, bias, target, prefetch=None):
            with ExitStack() as st:
                s_mm, s_add, s_bias = (sem(f"{tag}_{n}", st) for n in ("omm", "oadd", "obias"))
                with nc.Block() as block:
                    @block.tensor
                    def _(pe):
                        for t in range(TILES):
                            for k in range(KT):
                                mm = pe.matmul(ps[:, t, 0:D], ctx_fm[:, k, t * P:(t + 1) * P],
                                               weight(w_name)[:, k, :], start=(k == 0), stop=(k == KT - 1))
                            mm.then_inc(s_mm, 1)

                    @block.gpsimd
                    def _(pool):
                        if bias is not None:
                            for t in range(TILES):
                                pool.tensor_tensor(target[:, t, :], target[:, t, :], bias, ALU.add)\
                                    .then_inc(s_bias, 1)

                    @block.vector
                    def _(dve):
                        for t in range(TILES):
                            dve.wait_ge(s_mm, t + 1)
                            if bias is not None:
                                dve.wait_ge(s_bias, t + 1)
                            dve.tensor_tensor(target[:, t, :], ps[:, t, 0:D], target[:, t, :], ALU.add)\
                                .then_inc(s_add, 1)

                    if prefetch is not None:
                        @block.sync
                        def _(sp):
                            prefetch(sp)

        def mix_values(v_fm, v_tm):
            PI = 3.1415925
            with ExitStack() as st:
                ap_ = sb("mix_ap", [P, TILES, 2 * HEADS], where=st)
                amp = sb("mix_amp", [P, TILES, HEADS], where=st)
                ph = sb("mix_ph", [P, TILES, HEADS], where=st)
                sn = sb("mix_sin", [P, TILES, HEADS], where=st)
                hs = sb("mix_half_sin", [P, TILES, HEADS], where=st)
                coef = sb("mix_coef", [P, TILES, KT, 2, HPT], where=st)
                sup = sb("mix_sup", [P, 2, KT, 2, HPT, HD], where=st)
                s_ap, s_mm, s_chain, s_act, s_sup, s_pool, s_vd = (
                    sem(f"mix_{n}", st) for n in ("ap", "mm", "chain", "act", "sup", "pool", "vd"))
                with nc.Block() as block:
                    @block.tensor
                    def _(pe):
                        for t in range(TILES):
                            for k in range(KT):
                                mm = pe.matmul(ps[:, 7, t * 32:(t + 1) * 32], x_fm[:, k, t * P:(t + 1) * P],
                                               weight("l0_ampph")[:, k, :], start=(k == 0), stop=(k == KT - 1))
                        mm.then_inc(s_ap, 1)
                        for t in range(TILES):
                            for k in range(KT):
                                mm = pe.matmul(ps[:, t, k * D:(k + 1) * D], v_fm[:, k, t * P:(t + 1) * P],
                                               weight("l0_mix")[:, k, :], start=True, stop=True)
                            mm.then_inc(s_mm, 1)

                    @block.scalar
                    def _(act):
                        act.wait_ge(s_chain, 1)
                        act.activation(amp[:, :, :], ap_[:, :, 0:HEADS], ACT.Sigmoid).then_inc(s_act, 1)
                        act.activation(ph[:, :, :], ap_[:, :, HEADS:], ACT.Tanh).then_inc(s_act, 1)
                        act.wait_ge(s_act, 2)
                        act.activation(sn[:, :, :], ph[:, :, :], ACT.Sin, scale=PI).then_inc(s_act, 1)
                        act.activation(hs[:, :, :], ph[:, :, :], ACT.Sin, scale=PI / 2).then_inc(s_act, 1)

                    @block.vector
                    def _(dve):
                        link, signal, wait, count = ordered(dve, s_chain)
                        dve.wait_ge(s_ap, 1)
                        link(dve.tensor_tensor(
                            ap_[:, :, :], ps[:, 7, 0:TILES * 32].rearrange("p (t n) -> p t n", t=TILES),
                            spread(row("l0_ampphb"), "p (a n) -> p a n", [P, TILES, 32], a=1), ALU.add))
                        dve.wait_ge(s_act, 4)
                        link(dve.tensor_tensor(hs[:, :, :], hs[:, :, :], hs[:, :, :], ALU.mult))
                        link(dve.tensor_scalar(hs[:, :, :], hs[:, :, :], -2.0, 1.0, ALU.mult, ALU.add))
                        link(dve.tensor_scalar(amp[:, :, :], amp[:, :, :], 0.3, None, ALU.mult))
                        for i, trig in enumerate((hs, sn)):
                            for k in range(KT):
                                link(dve.tensor_tensor(coef[:, :, k, i, :], amp[:, :, k * HPT:(k + 1) * HPT],
                                                             trig[:, :, k * HPT:(k + 1) * HPT], ALU.mult))
                        for t in range(TILES):
                            dve.wait_ge(s_mm, t + 1)
                            if t >= 2:
                                dve.wait_ge(s_pool, 4 * (t - 1))
                            link(dve.tensor_tensor(ps[:, t, :], ps[:, t, :], row("l0_mixb"), ALU.add))
                            dve.tensor_tensor(
                                sup[:, t % 2, :, :, :, :].rearrange("p k i h d -> p (k i h) d"),
                                ps[:, t, :].rearrange("p (n d) -> p n d", d=HD),
                                spread(coef[:, t, :, :, :].rearrange("p k i h -> p (k i h)"), "p (n o) -> p n o",
                                       [P, 2 * HEADS, HD], o=1), ALU.mult).then_inc(s_sup, 1)

                    @block.gpsimd
                    def _(pool):
                        for t in range(TILES):
                            pool.wait_ge(s_sup, t + 1)
                            for i in range(2):
                                if i:
                                    pool.wait_ge(s_pool, 4 * t + 2)
                                for k in range(KT):
                                    v = v_tm[:, t, k * P:(k + 1) * P]
                                    pool.tensor_tensor(v, v, sup[:, t % 2, k, i, :, :].rearrange("p h d -> p (h d)"),
                                                       ALU.add).then_inc(s_pool, 1)

                    @block.sync
                    def _(sp):
                        for t in range(TILES):
                            sp.wait_ge(s_pool, 4 * (t + 1))
                            sp.dma_start(v_dram[t * P:(t + 1) * P, :], v_tm[:, t, :]).then_inc(s_vd, 16)
                        sp.wait_ge(s_vd, 16 * TILES)

        def add_normed():
            with ExitStack() as st:
                s_chain, s_var, s_rstd = (sem(f"l0n_{n}", st) for n in ("chain", "var", "rstd"))
                with nc.Block() as block:
                    @block.gpsimd
                    def _(pool):
                        pool.memset(norm_pow[:, :], -0.5).then_inc(s_rstd, 1)
                        pool.wait_ge(s_rstd, 1)
                        pool.wait_ge(s_var, 1)
                        pool.tensor_tensor(norm_r[:, :], norm_ve[:, :], norm_pow[:, :], ALU.pow).then_inc(s_rstd, 1)

                    @block.vector
                    def _(dve):
                        link, signal, wait, count = ordered(dve, s_chain)
                        for t in range(TILES):
                            signal(dve.bn_stats(norm_stats[:, t, :], xn[:, t, :]))
                        wait()
                        for t in range(TILES):
                            signal(dve.bn_aggr(norm_mv[:, t, :], norm_stats[:, t, :]))
                        wait()
                        dve.tensor_scalar(norm_ve[:, :], norm_mv[:, :, 1], EPS, None, ALU.add).then_inc(s_var, 1)
                        for t in range(TILES):
                            signal(dve.tensor_tensor(h[:, t, :], h[:, t, :], row("l0_ln_b"), ALU.add))
                            signal(dve.scalar_tensor_tensor(
                                out=xn[:, t, :], in0=xn[:, t, :], scalar=norm_mv[:, t, 0:1], in1=row("l0_ln_g"),
                                op0=ALU.subtract, op1=ALU.mult))
                        wait()
                        dve.wait_ge(s_rstd, 2)
                        for t in range(TILES):
                            link(dve.scalar_tensor_tensor(
                                out=h[:, t, :], in0=xn[:, t, :], scalar=norm_r[:, t:t + 1], in1=h[:, t, :],
                                op0=ALU.mult, op1=ALU.add))

        def attend_wide(ctx_fm, q_fm, k_fm, scale):
            pairs = IMAGES // 2
            units = pairs * KT
            with ExitStack() as st:
                v_img = sb("l1_v_img", [P, IMAGES, D], where=st)
                shifted = sb("l1_shifted", [P, 2, units // 2, SEQ], where=st)
                top = sb("l1_top", [P, 2, units // 2], where=st)
                total = sb("l1_total", [P, units], where=st)
                p_fm = sb("l1_p_fm", [P, units, PAIR], where=st)
                ctx_tm = sb("l1_ctx_tm", [P, pairs, D], where=st)
                s_v, s_scores, s_chain, s_probs, s_pt, s_pfm, s_av, s_ctx, s_ct, s_ctfm, s_total = (
                    sem(f"l1_{n}", st) for n in ("vimg", "scores", "chain", "probs", "pt", "pfm", "av", "ctx",
                                                 "ct", "ctfm", "total"))
                with nc.Block() as block:
                    @block.sync
                    def _(sp):
                        sp.dma_start(v_img[0:SEQ, :, :], v_dram[0:TOKENS, :].rearrange("(b j) d -> j b d", j=SEQ))\
                            .then_inc(s_v, 16)

                    @block.tensor
                    def _(pe):
                        for q in range(2):
                            for p in range(4 * q, 4 * q + 4):
                                for hd in range(KT):
                                    for s in range(2):
                                        c = (2 * p + s) * SEQ
                                        mm = pe.matmul(
                                            ps[64 * s:64 * s + 64, q, ((p % 4) * 2 + hd) * SEQ:((p % 4) * 2 + hd + 1) * SEQ],
                                            q_fm[:, hd, c:c + 64], k_fm[:, hd, c:c + SEQ], start=True, stop=True)
                            mm.then_inc(s_scores, 1)
                        for b in range(4):
                            pe.wait_ge(s_probs, b // 2 + 1)
                            for i in range(4):
                                n = 4 * b + i
                                mm = pe.transpose(ps[0:SEQ, 2 + b, i * P:(i + 1) * P],
                                                  shifted[:, n // 8, n % 8, :], ident)
                            mm.then_inc(s_pt, 1)
                        pe.wait_ge(s_v, 16)
                        for b in range(4):
                            pe.wait_ge(s_pfm, b + 1)
                            for i in range(4):
                                n = 4 * b + i
                                for s in range(2):
                                    rows = 64 if s == 0 else SEQ
                                    mm = pe.matmul(ps[64 * s:64 * s + rows, (6 + b) % 8, i * P:(i + 1) * P],
                                                   p_fm[0:SEQ, n, 64 * s:64 * s + rows],
                                                   v_img[0:SEQ, 2 * (n // 2) + s, (n % 2) * P:(n % 2 + 1) * P],
                                                   start=True, stop=True)
                            mm.then_inc(s_av, 1)
                        for b in range(4):
                            pe.wait_ge(s_ctx, b + 1)
                            for i in range(4):
                                n = 4 * b + i
                                mm = pe.transpose(ps[:, 2 + b, i * P:i * P + PAIR],
                                                  ctx_tm[0:PAIR, n // 2, (n % 2) * P:(n % 2 + 1) * P],
                                                  ident[0:PAIR, 0:PAIR])
                            mm.then_inc(s_ct, 1)

                    @block.vector
                    def _(dve):
                        link, signal, wait, count = ordered(dve, s_chain)
                        for q in range(2):
                            dve.wait_ge(s_scores, q + 1)
                            sc = ps[:, q, 0:8 * SEQ].rearrange("p (n j) -> p n j", j=SEQ)
                            link(dve.tensor_tensor(sc, sc, spread(const("causal"), "p (a j) -> p a j",
                                                                        [P, 8, SEQ], a=1), ALU.add))
                            link(dve.tensor_reduce(top[:, q, :], sc, AX.X, ALU.max))
                            signal(dve.tensor_tensor(shifted[:, q, :, :], sc,
                                                           spread(top[:, q, :], "p (n o) -> p n o", [P, 8, SEQ], o=1),
                                                           ALU.subtract))
                        for q in range(2):
                            dve.wait_ge(s_probs, q + 1)
                            signal(dve.tensor_reduce(total[:, 8 * q:8 * q + 8], shifted[:, q, :, :], AX.X, ALU.add))
                        wait()
                        link(dve.reciprocal(total[:, :], total[:, :]))
                        for b in range(4):
                            dve.wait_ge(s_av, b + 1)
                            dve.tensor_tensor(
                                ctx_tm[0:PAIR, 2 * b:2 * b + 2, :].rearrange("p a (h d) -> p (a h) d", h=KT),
                                ps[0:PAIR, (6 + b) % 8, :].rearrange("p (n d) -> p n d", n=4),
                                spread(total[0:PAIR, 4 * b:4 * b + 4], "p (n o) -> p n o", [PAIR, 4, P], o=1),
                                ALU.mult).then_inc(s_ctx, 1)

                    @block.scalar
                    def _(act):
                        for q in range(2):
                            act.wait_ge(s_chain, 3 * (q + 1))
                            act.activation(shifted[:, q, :, :], shifted[:, q, :, :], ACT.Exp, scale=scale)\
                                .then_inc(s_probs, 1)
                        for b in range(4):
                            act.wait_ge(s_pt, b + 1)
                            act.activation(p_fm[0:SEQ, 4 * b:4 * b + 4, :],
                                           ps[0:SEQ, 2 + b, :].rearrange("p (n r) -> p n r", n=4)[:, :, 0:PAIR],
                                           ACT.Copy).then_inc(s_pfm, 1)
                        for b in range(4):
                            act.wait_ge(s_ct, b + 1)
                            for p in range(2):
                                src = ps[:, 2 + b, p * 2 * P:(p + 1) * 2 * P].rearrange("p (k s j) -> p k s j", k=KT, s=2)
                                c = (2 * b + p) * 2 * SEQ
                                act.activation(ctx_fm[:, :, c:c + 2 * SEQ].rearrange("p k (s j) -> p k s j", s=2),
                                               src[:, :, :, 0:SEQ], ACT.Copy).then_inc(s_ctfm, 1)

        def attend_across(ctx_fm, q_fm, k_fm, scale):
            groups, S = L3_GROUPS, IMAGES
            tag = "l3a"
            with ExitStack() as st:
                q_st = sb(f"{tag}_q_st", [P, 2, KT, 4, 32], where=st)
                k_bd = sb(f"{tag}_k_bd", [P, 2, 4, KT, HPT, S], where=st)
                v_rep = sb(f"{tag}_v_rep", [P, 2, 4, D], where=st)
                v_bd = sb(f"{tag}_v_bd", [P, 2, 4, HEADS, HD + 1], where=st)
                shifted = sb(f"{tag}_shifted", [P, 2, HEADS, S], where=st)
                top = sb(f"{tag}_top", [P, 2, HEADS], where=st)
                probs = sb(f"{tag}_probs", [P, 2, HEADS * S], where=st)
                p_fm = sb(f"{tag}_p_fm", [P, 2, KT, P], where=st)
                recip = sb(f"{tag}_recip", [P, 2, HEADS], where=st)
                ctx_tm = sb(f"{tag}_ctx_tm", [P, 2, HEADS, HD], where=st)
                s_vrep0, s_vrep1, s_vbd, s_stage, s_kbd, s_scores, s_shift, s_probs, s_pt, s_pfm, s_av, s_ctx, \
                    s_ct, s_ctfm, s_soft, s_norm, s_vmask, s_zero = (sem(f"{tag}_{n}", st) for n in (
                        "vrep0", "vrep1", "vbd", "stage", "kbd", "scores", "shift", "probs", "pt", "pfm", "av",
                        "ctx", "ct", "ctfm", "soft", "norm", "vmask", "zero"))
                s_vrep = (s_vrep0, s_vrep1)

                def positions(fm, g, n=4):
                    cols = fm[:, :, bass.ds(g * 4, TOKENS)]
                    return cols.rearrange("p k (s b) -> p k b s", b=SEQ)[:, :, 0:n, :]

                with nc.Block() as block:
                    @block.sync
                    def _(sp):
                        def step(n, u, r, has):
                            if has(n):
                                if has(n - 2):
                                    sp.wait_ge(s_vbd, n * 4 - 4)
                                src = v_dram[bass.ds(n * 4, TOKENS), :].rearrange("(s b) d -> s b d", b=SEQ)[:, 0:4, :]
                                for q in range(HPT):
                                    sp.dma_start(v_rep[q * S:(q + 1) * S, u, :, :], src).then_inc(s_vrep[u], 16)
                        pipeline(sp, groups, 0, step)

                    @block.gpsimd
                    def _(pool):
                        vm = const("vmask16")
                        for u in range(2):
                            for c in range(4):
                                pool.tensor_copy(v_bd[:, u, c, :, HD], vm).then_inc(s_vmask, 1)
                        vm = spread(vm, "p (h o) -> p h o", [P, HEADS, HD], o=1)
                        hm = spread(const("headmask"), "p (a h o) -> p a h o", [P, KT, HPT, S], a=1, o=1)

                        def step(n, u, r, has):
                            if not has(n):
                                return
                            if has(n - 2):
                                pool.wait_ge(s_scores, n - 1)
                                pool.wait_ge(s_av, n - 1)
                            for c in range(4):
                                src = k_fm[:, :, bass.ds(n * 4 + c, TOKENS)]
                                src = src.rearrange("p k (s b) -> p k b s", b=SEQ)[:, :, 0:1, :]
                                pool.tensor_tensor(k_bd[:, u, c, :, :, :], src.broadcast_to([P, KT, HPT, S]), hm,
                                                   ALU.mult).then_inc(s_kbd, 1)
                            pool.wait_ge(s_vrep[u], (r + 1) * (16 * HPT))
                            for c in range(4):
                                pool.tensor_tensor(v_bd[:, u, c, :, 0:HD],
                                                   v_rep[:, u, c, :].rearrange("p (h d) -> p h d", h=HEADS),
                                                   vm, ALU.mult).then_inc(s_vbd, 1)
                        pipeline(pool, groups, 0, step)

                    @block.scalar
                    def _(act):
                        act.preload_act_table(ACT.Exp)
                        act.sem_inc(s_ctfm, 1)

                        def stage(n, u):
                            act.activation(q_st[:, u, :, :, 0:S], positions(q_fm, n), ACT.Copy).then_inc(s_stage, 1)

                        def step(n, u, r, has):
                            if isinstance(n, int) and n == 0:
                                act.wait_ge(s_zero, 2)
                                stage(0, 0)
                            if has(n) and has(n + 1):
                                if has(n - 1):
                                    act.wait_ge(s_scores, n)
                                stage(n + 1, 1 - u)
                            if has(n - 2):
                                act.wait_ge(s_ct, n - 1)
                                real = 4 if not isinstance(n, int) or n - 2 < groups - 1 else SEQ - 4 * (groups - 1)
                                src = ps[:, 7, 0:KT * P].rearrange("p (k c s) -> p k c s", k=KT, c=4)
                                act.activation(positions(ctx_fm, n - 2, real), src[:, :, 0:real, 0:S],
                                               ACT.Copy).then_inc(s_ctfm, 1)
                            if has(n - 1):
                                act.wait_ge(s_pt, n)
                                act.activation(p_fm[:, 1 - u, :, :].rearrange("p k r -> p (k r)"),
                                               ps[:, 4, 0:KT * P], ACT.Copy).then_inc(s_pfm, 1)
                            if has(n):
                                act.wait_ge(s_shift, n + 1)
                                act.activation(probs[:, u, :], shifted[:, u, :, :].rearrange("p h j -> p (h j)"),
                                               ACT.Exp, scale=scale).then_inc(s_probs, 1)
                        pipeline(act, groups, 2, step)

                    @block.tensor
                    def _(pe):
                        def step(n, u, r, has):
                            v = 1 - u
                            if has(n):
                                pe.wait_ge(s_stage, n + 1)
                                pe.wait_ge(s_kbd, (n + 1) * 4)
                                if has(n - 1):
                                    pe.wait_ge(s_shift, n)
                                for c in range(4):
                                    for k in range(KT):
                                        mm = pe.matmul(ps[32 * c:32 * c + 32, k, 0:HPT * S], q_st[:, u, k, c, :],
                                                       k_bd[:, u, c, k, :, :].rearrange("p h j -> p (h j)"),
                                                       start=True, stop=True)
                                mm.then_inc(s_scores, 1)
                            if has(n - 2):
                                pe.wait_ge(s_ctx, n - 1)
                                pe.wait_ge(s_ctfm, n - 1)
                                for k in range(KT):
                                    mm = pe.transpose(ps[:, 7, k * P:(k + 1) * P],
                                                      ctx_tm[:, u, k * HPT:(k + 1) * HPT, :]
                                                      .rearrange("p h d -> p (h d)"), ident)
                                mm.then_inc(s_ct, 1)
                            if has(n - 1):
                                pe.wait_ge(s_probs, n)
                                if has(n - 2):
                                    pe.wait_ge(s_pfm, n - 1)
                                for k in range(KT):
                                    mm = pe.transpose(ps[:, 4, k * P:(k + 1) * P],
                                                      probs[:, v, k * P:(k + 1) * P], ident)
                                mm.then_inc(s_pt, 1)
                                pe.wait_ge(s_pfm, n)
                                pe.wait_ge(s_vbd, n * 4)
                                pe.wait_ge(s_vmask, 8)
                                for c in range(4):
                                    for k in range(KT):
                                        mm = pe.matmul(
                                            ps[32 * c:32 * c + 32, 6, k * HPT * (HD + 1):(k + 1) * HPT * (HD + 1)],
                                            p_fm[:, v, k, 32 * c:32 * c + 32],
                                            v_bd[:, v, c, k * HPT:(k + 1) * HPT, :].rearrange("p h d -> p (h d)"),
                                            start=True, stop=True)
                                mm.then_inc(s_av, 1)
                        pipeline(pe, groups, 2, step)

                    @block.vector
                    def _(dve):
                        scores = ps[:, 0:2, 0:HPT * S].rearrange("p k (h j) -> p k h j", h=HPT)
                        out3 = ps[:, 6, 0:HEADS * (HD + 1)].rearrange("p (h d) -> p h d", h=HEADS)
                        for u in range(2):
                            dve.memset(q_st[:, u, :, :, :], 0.0).then_inc(s_zero, 1)

                        def step(n, u, r, has):
                            if has(n):
                                dve.wait_ge(s_scores, n + 1)
                                t3 = top[:, u, :].rearrange("p (k h) -> p k h", k=KT)
                                dve.tensor_reduce(t3, scores, AX.X, ALU.max).then_inc(s_soft, 1)
                                dve.wait_ge(s_soft, n + 1)
                                dve.tensor_tensor(shifted[:, u, :, :].rearrange("p (k h) j -> p k h j", k=KT), scores,
                                                  spread(t3, "p k (h o) -> p k h o", [P, KT, HPT, S], o=1),
                                                  ALU.subtract).then_inc(s_shift, 1)
                            if has(n - 1):
                                dve.wait_ge(s_av, n)
                                dve.reciprocal(recip[:, u, :], out3[:, :, HD]).then_inc(s_norm, 1)
                                dve.wait_ge(s_norm, n)
                                dve.tensor_tensor(ctx_tm[:, 1 - u, :, :], out3[:, :, 0:HD],
                                                  spread(recip[:, u, :], "p (h o) -> p h o", [P, HEADS, HD], o=1),
                                                  ALU.mult).then_inc(s_ctx, 1)
                        pipeline(dve, groups, 2, step)

        def zero_pads(tag, fm):
            with ExitStack() as st:
                s_zero = sem(tag, st)
                with nc.Block() as block:
                    @block.gpsimd
                    def _(pool):
                        pool.memset(fm[:, :, TOKENS:], 0.0).then_inc(s_zero, 1)

        def latents(tag, lat, terms):
            with ExitStack() as st:
                s_mm, s_cp = sem(f"{tag}_mm", st), sem(f"{tag}_cp", st)
                with nc.Block() as block:
                    @block.tensor
                    def _(pe):
                        pe.wait_ge(loaded["mla"], 16)
                        for half in range(2):
                            for k, (w, src) in enumerate(terms):
                                mm = pe.matmul(ps[:, half, 0:HALF], w, src[:, half * HALF:(half + 1) * HALF],
                                               start=(k == 0), stop=(k == KT - 1))
                            mm.then_inc(s_mm, 1)

                    @block.scalar
                    def _(act):
                        for half in range(2):
                            act.wait_ge(s_mm, half + 1)
                            act.activation(lat[:, half * HALF:(half + 1) * HALF], ps[:, half, 0:HALF], ACT.Copy)\
                                .then_inc(s_cp, 1)

                    @block.gpsimd
                    def _(pool):
                        pool.memset(lat[:, TOKENS:], 0.0).then_inc(s_cp, 1)

        def add_rows(tag, gates):
            with ExitStack() as st:
                s_add = sem(tag, st)
                with nc.Block() as block:
                    @block.gpsimd
                    def _(pool):
                        for t in range(TILES):
                            pool.tensor_tensor(h[:, t, :], h[:, t, :], xn[:, t, :], ALU.add).then_inc(s_add, 1)
                        pool.memset(gates[:, :, 0:1], 1.0).then_inc(s_add, 1)

        expert_w = sb("expert_w", [P, 2, 4096])
        s_w = [sem("expert_w0"), sem("expert_w1")]
        fetched = [0, 0]

        def fetch(sp, name, width, e, u):
            sp.dma_start(expert_w[:, u, 0:width], a[name][bass.ds(e, 1), :, :].rearrange("e p n -> p (e n)"))\
                .then_inc(s_w[u], 16)

        def fetch_first(name, width):
            def run(sp):
                for e in range(2):
                    fetch(sp, name, width, e, e)
            return run

        def ranks(tag, st, link, signal, dve, score, E):
            above = sb(f"{tag}_above", [P, TILES, E, E], where=st)
            same = sb(f"{tag}_same", [P, TILES, E, E], where=st)
            rank = sb(f"{tag}_rank", [P, TILES, E], where=st)
            shape = [P, TILES, E, E]
            other, own = (spread(score, pattern, shape, o=1) for pattern in ("p t (o e) -> p t o e", "p t (e o) -> p t e o"))
            earlier = spread(const(f"earlier{E}"), "p (t e f) -> p t e f", shape, t=1, f=E)
            signal(dve.tensor_tensor(above[:, :, :, :], other, own, ALU.is_gt))
            link(dve.tensor_tensor(same[:, :, :, :], other, own, ALU.is_equal))
            link(dve.tensor_tensor(same[:, :, :, :], same[:, :, :, :], earlier, ALU.mult))
            link(dve.tensor_tensor(above[:, :, :, :], above[:, :, :, :], same[:, :, :, :], ALU.add))
            link(dve.tensor_reduce(rank[:, :, :], above[:, :, :, :], AX.X, ALU.add))
            return rank

        def route(tag, E, top, router, bias, gates, kind, down_b=None):
            with ExitStack() as st:
                lg = sb(f"{tag}_lg", [P, TILES, E], where=st)
                red = sb(f"{tag}_red", [P, TILES], where=st)
                gate_fm = sb(f"{tag}_gate_fm", [E, PADDED], where=st) if down_b is not None else None
                s_mm, s_chain, s_exp, s_gate, s_gt, s_gfm, s_bias = (
                    sem(f"{tag}_r{n}", st) for n in ("mm", "chain", "exp", "gate", "gt", "gfm", "bias"))
                red3 = spread(red[:, :], "p (t o) -> p t o", [P, TILES, E], o=1)
                width = router.shape[2]
                with nc.Block() as block:
                    @block.tensor
                    def _(pe):
                        for t in range(TILES):
                            for k in range(KT):
                                mm = pe.matmul(ps[:, 0, t * width:(t + 1) * width], x_fm[:, k, t * P:(t + 1) * P],
                                               router[:, k, :], start=(k == 0), stop=(k == KT - 1))
                        mm.then_inc(s_mm, 1)
                        if down_b is not None:
                            pe.wait_ge(s_gate, 1)
                            for t in range(TILES):
                                mm = pe.transpose(ps[0:E, 1 + t // 4, (t % 4) * P:(t % 4 + 1) * P], gates[:, t, :], ident)
                            mm.then_inc(s_gt, 1)
                            pe.wait_ge(s_gfm, 2)
                            for t in range(TILES):
                                pe.matmul(ps[:, 3 + t, 0:D], gate_fm[:, t * P:(t + 1) * P], down_b,
                                          start=True, stop=True).then_inc(s_bias, 1)

                    @block.scalar
                    def _(act):
                        act.wait_ge(s_chain, 3 if kind == "softmax" else 1)
                        func = ACT.Exp if kind == "softmax" else ACT.Sigmoid
                        act.activation(lg[:, :, :], lg[:, :, :], func).then_inc(s_exp, 1)
                        if down_b is not None:
                            act.wait_ge(s_gt, 1)
                            for b, (c0, c1) in enumerate(((0, 512), (512, PADDED))):
                                act.activation(gate_fm[:, c0:c1], ps[0:E, 1 + b, 0:c1 - c0], ACT.Copy)\
                                    .then_inc(s_gfm, 1)

                    @block.vector
                    def _(dve):
                        link, signal, wait, count = ordered(dve, s_chain)
                        dve.wait_ge(s_mm, 1)
                        src = ps[:, 0, 0:TILES * width].rearrange("p (t e) -> p t e", t=TILES)[:, :, 0:E]
                        if bias is None:
                            link(dve.tensor_copy(lg[:, :, :], src))
                        else:
                            link(dve.tensor_tensor(lg[:, :, :], src, spread(bias, "p (a e) -> p a e", [P, TILES, E], a=1),
                                                         ALU.add))
                        if kind == "softmax":
                            link(dve.tensor_reduce(red[:, :], lg[:, :, :], AX.X, ALU.max))
                            link(dve.tensor_tensor(lg[:, :, :], lg[:, :, :], red3, ALU.subtract))
                            dve.wait_ge(s_exp, 1)
                            link(dve.tensor_reduce(red[:, :], lg[:, :, :], AX.X, ALU.add))
                            link(dve.reciprocal(red[:, :], red[:, :]))
                            link(dve.tensor_tensor(lg[:, :, :], lg[:, :, :], red3, ALU.mult))
                        dve.wait_ge(s_exp, 1)
                        rank = ranks(tag, st, link, signal, dve, lg[:, :, :], E)
                        link(dve.tensor_scalar(rank[:, :, :], rank[:, :, :], float(top), None, ALU.is_lt))
                        link(dve.tensor_tensor(gates, rank[:, :, :], lg[:, :, :], ALU.mult))
                        if kind == "sigmoid":
                            link(dve.tensor_reduce(red[:, :], gates, AX.X, ALU.add))
                            link(dve.reciprocal(red[:, :], red[:, :]))
                            link(dve.tensor_tensor(gates, gates, red3, ALU.mult))
                        dve.sem_inc(s_gate, 1)
                        if down_b is not None:
                            for t in range(TILES):
                                dve.wait_ge(s_bias, t + 1)
                                signal(dve.tensor_tensor(h[:, t, :], ps[:, 3 + t, 0:D], h[:, t, :], ALU.add))

        def experts(tag, w_in, E, mt, gates, clipped=False, first_open=False):
            units = 2 * mt
            up_w, down_w = KT * mt * P, mt * D
            width = 2 * up_w + down_w
            base = list(fetched)
            with ExitStack() as st:
                act_fm = sb(f"{tag}_act_fm", [P, 2, mt, PADDED], where=st)
                up_sb = sb(f"{tag}_up_sb", [P, 2, HALF], where=st)
                s_pads, s_up, s_free0, s_free1, s_glu, s_sil, s_chain, s_act, s_down, s_acc = (
                    sem(f"{tag}_{n}", st) for n in ("pads", "up", "free0", "free1", "glu", "sil", "chain", "act",
                                                    "down", "acc"))
                s_free = (s_free0, s_free1)

                def wa(u, which, k, m):
                    at = which * up_w + k * mt * P + m * P
                    return expert_w[:, u, at:at + P]

                def wd(u, m):
                    return expert_w[:, u, 2 * up_w + m * D:2 * up_w + (m + 1) * D]

                with nc.Block() as block:
                    @block.sync
                    def _(sp):
                        def step(n, u, r, has):
                            if has(n) and has(n - 2):
                                sp.wait_ge(s_down, n * 3 - 3)
                                fetch(sp, w_in, width, n, u)
                        pipeline(sp, E, 0, step)

                    @block.gpsimd
                    def _(pool):
                        pool.memset(act_fm[:, :, :, TOKENS:], 0.0).then_inc(s_pads, 1)

                    @block.tensor
                    def _(pe):
                        pe.wait_ge(s_pads, 1)

                        def step(n, u, r, has):
                            if has(n):
                                pe.wait_ge(s_w[u], (r + (1 + base[u])) * 16)
                                for j in range(units):
                                    m, half, slot = j // 2, j % 2, j % 2
                                    if has(n - 1) or j >= 2:
                                        pe.wait_ge(s_free[slot], n * mt + j // 2)
                                    for which in range(2):
                                        for k in range(KT):
                                            mm = pe.matmul(ps[:, 2 * slot + which, 0:HALF], wa(u, which, k, m),
                                                           x_fm[:, k, half * HALF:(half + 1) * HALF],
                                                           start=(k == 0), stop=(k == KT - 1))
                                    mm.then_inc(s_up, 1)
                            if has(n - 1):
                                v = 1 - u
                                pe.wait_ge(s_free0, n * mt)
                                pe.wait_ge(s_free1, n * mt)
                                for b in range(3):
                                    if has(n - 2):
                                        pe.wait_ge(s_acc, n * 3 - 5 + b)
                                    for t in range(2 * b, min(2 * b + 2, TILES)):
                                        for m in range(mt):
                                            mm = pe.matmul(ps[:, 4 + b, (t % 2) * D:(t % 2 + 1) * D],
                                                           act_fm[:, v, m, t * P:(t + 1) * P], wd(v, m),
                                                           start=(m == 0), stop=(m == mt - 1))
                                    mm.then_inc(s_down, 1)
                        pipeline(pe, E, 1, step)

                    @block.scalar
                    def _(act):
                        act.preload_act_table(ACT.Silu)

                        def step(n, u, r, has):
                            if has(n):
                                for j in range(units):
                                    slot = j % 2
                                    if clipped:
                                        act.wait_ge(s_glu, n * units + (j + 1))
                                        g = ps[:, 2 * slot, 0:HALF]
                                        act.activation(g, g, ACT.Silu, scale=L0_ALPHA).then_inc(s_sil, 1)
                                    else:
                                        act.wait_ge(s_up, n * units + (j + 1))
                                        if has(n - 1) or j >= 2:
                                            act.wait_ge(s_free[slot], n * mt + j // 2)
                                        act.activation(up_sb[:, slot, :], ps[:, 2 * slot, 0:HALF], ACT.Silu)\
                                            .then_inc(s_sil, 1)
                        pipeline(act, E, 0, step)

                    @block.vector
                    def _(dve):
                        def step(n, u, r, has):
                            if has(n):
                                for j in range(units):
                                    m, half, slot = j // 2, j % 2, j % 2
                                    out = act_fm[:, u, m, half * HALF:(half + 1) * HALF]
                                    g, up = ps[:, 2 * slot, 0:HALF], ps[:, 2 * slot + 1, 0:HALF]
                                    dve.wait_ge(s_up, n * units + (j + 1))
                                    if clipped:
                                        at = COL_AT["l0_gub"][0]
                                        bias = [col_sb[:, bass.ds(n * 4 + (at + 2 * w + m), 1)] for w in range(2)]
                                        link, signal, wait, count = ordered(dve, s_chain, (n * units + j) * 2)
                                        dve.tensor_scalar(g, g, bias[0], L0_LIMIT, ALU.add, ALU.min).then_inc(s_glu, 1)
                                        link(dve.tensor_scalar(up_sb[:, slot, :], up, bias[1], L0_LIMIT,
                                                                     ALU.add, ALU.min))
                                        link(dve.tensor_scalar(up_sb[:, slot, :], up_sb[:, slot, :], -L0_LIMIT, 1.0,
                                                                     ALU.max, ALU.add))
                                        dve.wait_ge(s_sil, n * units + (j + 1))
                                        dve.scalar_tensor_tensor(out=out, in0=g, scalar=1.0 / L0_ALPHA,
                                                                 in1=up_sb[:, slot, :], op0=ALU.mult, op1=ALU.mult)\
                                            .then_inc(s_free[slot], 1)
                                    else:
                                        dve.wait_ge(s_sil, n * units + (j + 1))
                                        dve.tensor_tensor(out, up, up_sb[:, slot, :], ALU.mult).then_inc(s_free[slot], 1)
                            if has(n - 1):
                                for b in range(3):
                                    dve.wait_ge(s_down, n * 3 - 2 + b)
                                    if has(n - 2):
                                        dve.wait_ge(s_acc, n * 3 - 5 + b)
                                    for t in range(2 * b, min(2 * b + 2, TILES)):
                                        ins = dve.scalar_tensor_tensor(
                                            out=h[:, t, :], in0=ps[:, 4 + b, (t % 2) * D:(t % 2 + 1) * D],
                                            scalar=gates[:, t, bass.ds(n - 1, 1)], in1=h[:, t, :],
                                            op0=ALU.mult, op1=ALU.add)
                                    ins.then_inc(s_acc, 1)
                        pipeline(dve, E, 1, step)
            fetched[0] += E // 2
            fetched[1] += E // 2

        def chunked_experts():
            E = L3_E
            base = list(fetched)
            with ExitStack() as st:
                lg = sb("l3_lg", [P, TILES, E], where=st)
                cnt = sb("l3_cnt", [P, TILES, E], where=st)
                pick = sb("l3_pick", [P, 2, TILES, E], where=st)
                tmp = sb("l3_tmp", [P, TILES, E], where=st)
                chosen = sb("l3_chosen", [P, TILES, E], where=st)
                offs = sb("l3_offs", [P, E, E], where=st)
                off = sb("l3_off", [P, E], where=st)
                tot = sb("l3_tot", [P, E], where=st)
                place = sb("l3_place", [P, 2, TILES], where=st)
                place_u = sb("l3_place_u", [P, 2, TILES], U32, where=st)
                best = sb("l3_best", [P, 2, TILES], where=st)
                share = sb("l3_share", [P, 2, TILES], where=st)
                s_mm, s_chain, s_m, s_cnt, s_e, s_idx, s_sc = (
                    sem(f"l3r_{n}", st) for n in ("mm", "chain", "m", "cnt", "e", "idx", "sc"))
                with nc.Block() as block:
                    @block.tensor
                    def _(pe):
                        router = weight("l3_router")
                        for t in range(TILES):
                            for k in range(KT):
                                mm = pe.matmul(ps[:, 0, t * E:(t + 1) * E], x_fm[:, k, t * P:(t + 1) * P],
                                               router[:, k, :], start=(k == 0), stop=(k == KT - 1))
                        mm.then_inc(s_mm, 1)
                        pe.wait_ge(s_m, 1)
                        for t in range(TILES):
                            for q in range(t + 1):
                                mm = pe.matmul(ps[:, 1, t * E:(t + 1) * E], const("before" if q == t else "ones"),
                                               chosen[:, q, :], start=(q == 0), stop=(q == t))
                        for q in range(TILES):
                            mm = pe.matmul(ps[:, 2, 0:E], const("ones"), chosen[:, q, :], start=(q == 0),
                                           stop=(q == TILES - 1))
                        mm.then_inc(s_cnt, 1)

                    @block.scalar
                    def _(act):
                        act.wait_ge(s_idx, 1)
                        act.activation(share[:, 1, :], share[:, 1, :], ACT.Exp).then_inc(s_e, 1)

                    @block.vector
                    def _(dve):
                        link, signal, wait, count = ordered(dve, s_chain)
                        dve.wait_ge(s_mm, 1)
                        link(dve.tensor_copy(lg[:, :, :], ps[:, 0, 0:TILES * E].rearrange("p (t e) -> p t e", t=TILES)))
                        rank = ranks("l3", st, link, signal, dve, lg[:, :, :], E)
                        valid = spread(const("valid"), "p (t o) -> p t o", [P, TILES, E], o=1)
                        link(dve.tensor_scalar(chosen[:, :, :], rank[:, :, :], float(L3_TOP), None, ALU.is_lt))
                        link(dve.tensor_tensor(chosen[:, :, :], chosen[:, :, :], valid, ALU.mult))
                        dve.sem_inc(s_m, 1)
                        for i in range(2):
                            link(dve.tensor_scalar(pick[:, i, :, :], rank[:, :, :], float(i), None, ALU.is_equal))
                            link(dve.tensor_tensor(tmp[:, :, :], pick[:, i, :, :], lg[:, :, :], ALU.mult))
                            link(dve.tensor_reduce(best[:, i, :], tmp[:, :, :], AX.X, ALU.add))
                        link(dve.tensor_tensor(share[:, 1, :], best[:, 1, :], best[:, 0, :], ALU.subtract))
                        dve.sem_inc(s_idx, 1)
                        dve.wait_ge(s_e, 1)
                        link(dve.tensor_scalar(share[:, 0, :], share[:, 1, :], 1.0, None, ALU.add))
                        link(dve.reciprocal(share[:, 0, :], share[:, 0, :]))
                        link(dve.tensor_tensor(share[:, 1, :], share[:, 1, :], share[:, 0, :], ALU.mult))
                        dve.wait_ge(s_cnt, 1)
                        link(dve.tensor_copy(tot[:, :], ps[:, 2, 0:E]))
                        link(dve.tensor_tensor(offs[:, :, :], spread(tot[:, :], "p (o e) -> p o e", [P, E, E], o=1),
                                                     const("earlier8").rearrange("p (e f) -> p e f", e=E), ALU.mult))
                        link(dve.tensor_reduce(off[:, :], offs[:, :, :], AX.X, ALU.add))
                        link(dve.tensor_tensor(cnt[:, :, :], ps[:, 1, 0:TILES * E].rearrange("p (t e) -> p t e", t=TILES),
                                                     spread(off[:, :], "p (o e) -> p o e", [P, TILES, E], o=1), ALU.add))
                        for i in range(2):
                            link(dve.tensor_tensor(tmp[:, :, :], pick[:, i, :, :], cnt[:, :, :], ALU.mult))
                            link(dve.tensor_reduce(place[:, i, :], tmp[:, :, :], AX.X, ALU.add))
                            link(dve.tensor_copy(place_u[:, i, :], place[:, i, :]))
                        dve.sem_inc(s_idx, 1)

                    @block.gpsimd
                    def _(pool):
                        pool.wait_ge(s_idx, 2)
                        for t in range(TILES):
                            rows = P if t < TILES - 1 else LAST
                            for i in range(2):
                                pool.indirect_dma_start(
                                    perm_dram, bass.IndirectOffsetOnAxis(ap=place_u[0:rows, i, t:t + 1], axis=0),
                                    xn[0:rows, t, :], None).then_inc(s_sc, 16)
                        pool.wait_ge(s_sc, 16 * 2 * TILES)

                width = KT * L3_FF + L3_FF // P * D
                MT = L3_FF // P
                xp_tm = sb("l3_xp_tm", [HCH, 2, 2, D], where=st)
                xp_fm = sb("l3_xp_fm", [P, 2, KT, CHUNK], where=st)
                hid = sb("l3_hid", [P, 2, MT, CHUNK], where=st)
                y_fm = sb("l3_y_fm", [P, 2, KT, CHUNK], where=st)
                y_tm = sb("l3_y_tm", [HCH, 2, 2, D], where=st)
                s_x = [sem(f"l3c_x{u}", st) for u in range(2)]
                s_y = [sem(f"l3c_y{u}", st) for u in range(2)]
                s_xt, s_xfm, s_up, s_hid, s_down, s_yfm, s_yt, s_ytm = (
                    sem(f"l3c_{n}", st) for n in ("xt", "xfm", "up", "hid", "down", "yfm", "yt", "ytm"))

                def chunk_rows(dram, n):
                    return dram[bass.ds(n * CHUNK, CHUNK), :].rearrange("(q p) d -> p q d", q=2)

                with nc.Block() as block:
                    @block.sync
                    def _(sp):
                        def step(n, u, r, has):
                            if has(n):
                                if has(n - 2):
                                    sp.wait_ge(s_xt, n - 1)
                                sp.dma_start(xp_tm[:, u, :, :], chunk_rows(perm_dram, n)).then_inc(s_x[u], 16)
                            if has(n) and has(n - 2):
                                sp.wait_ge(s_down, n * 2 - 2)
                                fetch(sp, "l3_experts", width, n, u)
                            if has(n - 2):
                                sp.wait_ge(s_ytm, n)
                                sp.dma_start(chunk_rows(y_dram, n - 2), y_tm[:, u, :, :]).then_inc(s_y[u], 16)
                        for u in range(2):
                            sp.sem_inc(s_y[u], 16)
                        pipeline(sp, E, 2, step)
                        for u in range(2):
                            sp.wait_ge(s_y[u], 16 * (E // 2 + 1))

                    @block.tensor
                    def _(pe):
                        def step(n, u, r, has):
                            v = 1 - u
                            if has(n - 1):
                                pe.wait_ge(s_w[v], (r + base[v] + (1 if v == 0 else 0)) * 16)
                                pe.wait_ge(s_xfm, n)
                                for j in range(MT // 2):
                                    if has(n - 2):
                                        pe.wait_ge(s_hid, n * 4 - 7 + j)
                                    for i in range(2):
                                        for k in range(KT):
                                            at = k * L3_FF + (2 * j + i) * P
                                            mm = pe.matmul(ps[:, 1 + j, i * CHUNK:(i + 1) * CHUNK],
                                                           expert_w[:, v, at:at + P], xp_fm[:, v, k, :],
                                                           start=(k == 0), stop=(k == KT - 1))
                                    mm.then_inc(s_up, 1)
                            if has(n):
                                pe.wait_ge(s_x[u], (r + 1) * 16)
                                if has(n - 1):
                                    pe.wait_ge(s_xfm, n)
                                for k in range(KT):
                                    for q in range(2):
                                        mm = pe.transpose(ps[:, 0, k * CHUNK + q * HCH:k * CHUNK + (q + 1) * HCH],
                                                          xp_tm[:, u, q, k * P:(k + 1) * P], ident[0:HCH, 0:HCH])
                                mm.then_inc(s_xt, 1)
                            if has(n - 2):
                                pe.wait_ge(s_yfm, n * 2 - 2)
                                pe.wait_ge(s_ytm, n - 1)
                                for q in range(2):
                                    for m in range(KT):
                                        mm = pe.transpose(ps[0:HCH, 7, q * D + m * P:q * D + (m + 1) * P],
                                                          y_fm[:, u, m, q * HCH:(q + 1) * HCH], ident)
                                mm.then_inc(s_yt, 1)
                            if has(n - 1):
                                for m in range(KT):
                                    if has(n - 2):
                                        pe.wait_ge(s_yfm, n * 2 - 3 + m)
                                    for k in range(MT):
                                        if m == 0 and k % 2 == 0:
                                            pe.wait_ge(s_hid, n * 4 - 3 + k // 2)
                                        at = KT * L3_FF + k * D + m * P
                                        mm = pe.matmul(ps[:, 5 + m, 0:CHUNK], expert_w[:, v, at:at + P],
                                                       hid[:, v, k, :], start=(k == 0), stop=(k == MT - 1))
                                    mm.then_inc(s_down, 1)
                        pipeline(pe, E, 2, step)

                    @block.scalar
                    def _(act):
                        act.preload_act_table(ACT.Gelu)

                        def step(n, u, r, has):
                            if has(n - 1):
                                for j in range(MT // 2):
                                    act.wait_ge(s_up, n * 4 - 3 + j)
                                    act.activation(hid[:, 1 - u, 2 * j:2 * j + 2, :].rearrange("p i c -> p (i c)"),
                                                   ps[:, 1 + j, 0:2 * CHUNK], ACT.Gelu).then_inc(s_hid, 1)
                        pipeline(act, E, 1, step)

                    @block.vector
                    def _(dve):
                        dve.sem_inc(s_ytm, 1)

                        def step(n, u, r, has):
                            if has(n):
                                dve.wait_ge(s_xt, n + 1)
                                dve.tensor_copy(xp_fm[:, u, :, :].rearrange("p k c -> p (k c)"), ps[:, 0, 0:KT * CHUNK])\
                                    .then_inc(s_xfm, 1)
                            if has(n - 2):
                                dve.wait_ge(s_yt, n - 1)
                                dve.wait_ge(s_y[u], r * 16)
                                dve.tensor_copy(y_tm[:, u, :, :].rearrange("p q d -> p (q d)"), ps[0:HCH, 7, :])\
                                    .then_inc(s_ytm, 1)
                            if has(n - 1):
                                for m in range(KT):
                                    dve.wait_ge(s_down, n * 2 - 1 + m)
                                    dve.tensor_copy(y_fm[:, 1 - u, m, :], ps[:, 5 + m, 0:CHUNK]).then_inc(s_yfm, 1)
                        pipeline(dve, E, 2, step)

                back = sb("l3_back", [P, 2, TILES, D], where=st)
                s_back = [sem(f"l3b_back{t}", st) for t in range(TILES)]
                s_add, s_out = sem("l3b_add", st), sem("l3b_out", st)
                with nc.Block() as block:
                    @block.gpsimd
                    def _(pool):
                        for t in range(TILES):
                            rows = P if t < TILES - 1 else LAST
                            for i in range(2):
                                pool.indirect_dma_start(
                                    back[0:rows, i, t, :], None, y_dram,
                                    bass.IndirectOffsetOnAxis(ap=place_u[0:rows, i, t:t + 1], axis=0))\
                                    .then_inc(s_back[t], 16)

                    @block.vector
                    def _(dve):
                        for t in range(TILES):
                            rows = P if t < TILES - 1 else LAST
                            dve.wait_ge(s_back[t], 32)
                            for i in range(2):
                                if i:
                                    dve.wait_ge(s_add, 2 * t + 1)
                                x = h[0:rows, t, :]
                                dve.scalar_tensor_tensor(out=x, in0=back[0:rows, i, t, :],
                                                         scalar=share[0:rows, i, t:t + 1], in1=x,
                                                         op0=ALU.mult, op1=ALU.add).then_inc(s_add, 1)

                    @block.sync
                    def _(sp):
                        for t in range(TILES):
                            rows = P if t < TILES - 1 else LAST
                            sp.wait_ge(s_add, 2 * t + 2)
                            sp.dma_start(out[t * P:t * P + rows, :], h[0:rows, t, :]).then_inc(s_out, 16)
                        sp.wait_ge(s_out, 16 * TILES)

        l0_width, l1_width, l3_width = 3 * KT * D, 2 * KT * L1_PAD + L1_PAD // P * D, 4096

        tokens()
        normalise(h, xn)
        with ExitStack() as st:
            q_fm, eq_fm = (sb(f"l0_{n}", [P, KT, Q_COLS], where=st) for n in ("q_fm", "eq_fm"))
            k_fm, ek_fm = (sb(f"l0_{n}", [P, KT, PADDED], where=st) for n in ("k_fm", "ek_fm"))
            with ExitStack() as st2:
                v_fm = sb("l0_v_fm", [P, KT, PADDED], where=st2)
                v_tm = sb("l0_v_tm", [P, TILES, D], where=st2)
                project("l0p", "l0", plain("l0_v", v_fm, "l0_bv") + plain("l0_q", q_fm, "l0_bq")
                        + plain("l0_k", k_fm, "l0_bk") + plain("l0_eq", eq_fm, "l0_beq")
                        + plain("l0_ek", ek_fm, "l0_bek"), value_terms("l0_v"), row("l0_bv"), v_tm,
                        pads=(q_fm[:, :, TOKENS:], eq_fm[:, :, TOKENS:], v_fm[:, :, TOKENS:]))
                mix_values(v_fm, v_tm)
            ctx_fm = sb("l0_ctx_fm", [P, KT, PADDED], where=st)
            zero_pads("l0z", ctx_fm)
            attend("l0a", ctx_fm, q_fm, k_fm, eq_fm, ek_fm, mask=const("decay"), scale=0.25)
            project_out("l0o", ctx_fm, "l0_o", row("l0_bo"), xn, fetch_first("l0_experts", l0_width))
            add_normed()
        normalise(h, xn)
        with ExitStack() as st:
            gates = sb("l0_gates", [P, TILES, L0_E], where=st)
            at = WEIGHT_AT["l0_down_b"][0]
            route("l0", L0_E, L0_TOP, weight("l0_router"), row("l0_rb"), gates[:, :, :], "softmax",
                  down_b=w_sb[0:L0_E, at:at + D])
            experts("l0e", "l0_experts", L0_E, 2, gates, clipped=True)

        recycle()
        normalise(h, xn)
        with ExitStack() as st:
            q_fm, k_fm, ctx_fm = (sb(f"l1_{n}", [P, KT, PADDED], where=st) for n in ("q_fm", "k_fm", "ctx_fm"))
            jobs = []
            for w, wr, dst in (("l1_q", "l1_qrot", q_fm), ("l1_k", "l1_krot", k_fm)):
                for (terms, _, d, _, _, _), (rterms, *_) in zip(plain(w, dst), plain(wr, dst)):
                    jobs.append((terms, rterms, d, None, const("cos1"), const("sin1")))
            project("l1p", "l1", jobs, value_terms("l1_v"), pads=(q_fm[:, :, TOKENS:], ctx_fm[:, :, TOKENS:]))
            attend_wide(ctx_fm, q_fm, k_fm, 1.0 / P)
            project_out("l1o", ctx_fm, "l1_o", None, h, fetch_first("l1_experts", l1_width))
        normalise(h, xn)
        with ExitStack() as st:
            gates = sb("l1_gates", [P, TILES, L1_E], where=st)
            route("l1", L1_E, 2, weight("l1_router"), None, gates[:, :, :], "softmax")
            experts("l1e", "l1_experts", L1_E, L1_PAD // P, gates)

        recycle()
        normalise(h, xn)
        with ExitStack() as st:
            q_fm = sb("l2_q_fm", [P, KT, Q_COLS], where=st)
            k_fm, ctx_fm = (sb(f"l2_{n}", [P, KT, PADDED], where=st) for n in ("k_fm", "ctx_fm"))
            project("l2p", "l2", plain("l2_q", q_fm, "l2_bq") + plain("l2_k", k_fm, "l2_bk"), value_terms("l2_v"),
                    row("l2_bv"), pads=(q_fm[:, :, TOKENS:], ctx_fm[:, :, TOKENS:]))
            attend("l2a", ctx_fm, q_fm, k_fm, mask=const("sparse"), mask_op=ALU.mult, scale=0.25)
            project_out("l2o", ctx_fm, "l2_o", row("l2_bo"), h)
        normalise(h, xn)
        with ExitStack() as st:
            x0n = sb("mla_x0n", [P, TILES, D], where=st)
            normalise(xn, x0n, rms=True, scale="w_ln1")
            lat = sb("mla_lat_fm", [P, PADDED], where=st)
            q_fm = sb("mla_q_fm", [P, KT, Q_COLS], where=st)
            k_fm, ctx_fm = (sb(f"mla_{n}", [P, KT, PADDED], where=st) for n in ("k_fm", "ctx_fm"))
            wl = weight("mla_lat")
            latents("mlal", lat, [(wl[:, k, :], x_fm[:, k, :]) for k in range(KT)])
            one = {n: weight(f"mla_{n}", 1)[:, 0, :] for n in ("q", "qrot", "k_lat", "v")}
            jobs = []
            for m in range(KT):
                f = slice(m * P, (m + 1) * P)
                jobs.append(([(one["q"][:, f], lat)], [(one["qrot"][:, f], lat)], q_fm[:, m, :], None,
                             const("cos2"), const("sin2")))
                jobs.append(([(one["k_lat"][:, f], lat)] + [(weight("mla_k")[:, k, f], x_fm[:, k, :]) for k in range(KT)],
                             [(weight("mla_krot")[:, k, f], x_fm[:, k, :]) for k in range(KT)], k_fm[:, m, :], None,
                             const("cos2"), const("sin2")))
            project("mlap", "mla", jobs, [(one["v"], lat)], pads=(q_fm[:, :, TOKENS:], ctx_fm[:, :, TOKENS:]))
            attend("mlaa", ctx_fm, q_fm, k_fm, mask=const("causal"), mask_op=ALU.add, scale=0.25)
            project_out("mlao", ctx_fm, "mla_o", None, xn, fetch_first("l2_experts", l0_width))
            normalise(xn, x0n, rms=True, scale="w_ln2")
            gates = sb("l2_gates", [P, TILES, L2_E], where=st)
            add_rows("l2h", gates)
            route("l2", L2_E - 1, 2, weight("mla_router"), row("mla_rb", 7), gates[:, :, 1:], "sigmoid")
            experts("l2e", "l2_experts", L2_E, 2, gates)

        recycle()
        normalise(h, xn)
        with ExitStack() as st:
            q_fm = sb("l3_q_fm", [P, KT, Q_COLS], where=st)
            k_fm, ctx_fm = (sb(f"l3_{n}", [P, KT, PADDED], where=st) for n in ("k_fm", "ctx_fm"))
            project("l3p", "l3", plain("l3_q", q_fm, "l3_bq") + plain("l3_k", k_fm, "l3_bk"), value_terms("l3_v"),
                    row("l3_bv"), pads=(q_fm[:, :, TOKENS:], k_fm[:, :, TOKENS:], ctx_fm[:, :, TOKENS:]))
            attend_across(ctx_fm, q_fm, k_fm, 0.25)
            project_out("l3o", ctx_fm, "l3_o", row("l3_bo"), h, fetch_first("l3_experts", l3_width))
        normalise(h, xn)
        chunked_experts()


def rows_of(w):
    w = np.asarray(w)
    return np.ascontiguousarray(w.reshape(-1, P, w.shape[1]).transpose(1, 0, 2)).reshape(P, -1)


def under(w, above=0, total=P):
    out = np.zeros((total, w.shape[1]), w.dtype)
    out[above:above + w.shape[0]] = w
    return out


def layout(i):
    z = np.float32
    x = np.asarray(i["x"]).reshape(IMAGES, CHANNELS, GRID, PATCH, GRID, PATCH).transpose(0, 2, 4, 3, 5, 1)
    patches = np.zeros((PADDED, PATCH_DIM), z)
    for b in range(IMAGES):
        patches[b * SEQ + 1:(b + 1) * SEQ] = x[b].reshape(GRID * GRID, PATCH_DIM)

    w = {"tok_w": rows_of(i["L0_tok_W"])}
    for n, k in (("q", "Wq"), ("k", "Wk"), ("v", "Wv"), ("eq", "Weq"), ("ek", "Wek"), ("o", "Wo")):
        w[f"l0_{n}"] = rows_of(i[f"L0_attn_{k}"].T)
    mix = np.zeros((D, 2, P), z)
    for hd in range(HEADS):
        m = i["L0_attn_mix_w"][hd].T
        c = (hd % HPT) * HD
        mix[hd * HD:(hd + 1) * HD, 0, c:c + HD] = m
        mix[hd * HD:(hd + 1) * HD, 1, c:c + HD] = np.roll(m, 1, axis=1)
    w["l0_mix"] = rows_of(mix.reshape(D, 2 * P))
    w["l0_ampph"] = rows_of(np.concatenate([i["L0_attn_amp_w"].T, i["L0_attn_ph_w"].T], 1))
    w["l0_router"] = rows_of(i["L0_ffn_router_weight"].T)
    w["l0_down_b"] = under(i["L0_ffn_down_bias"])
    swap = np.concatenate([np.arange(64, 128), np.arange(64)])
    for n, k in (("q", "wq"), ("k", "wk"), ("v", "wv")):
        m = i[f"L1_attn_{k}"]
        w[f"l1_{n}"] = rows_of(m.transpose(1, 0, 2).reshape(D, D))
        if n != "v":
            w[f"l1_{n}rot"] = rows_of(m[:, :, swap].transpose(1, 0, 2).reshape(D, D))
    w["l1_o"] = rows_of(i["L1_attn_wo"].reshape(D, D))
    w["l1_router"] = rows_of(i["L1_ffn_Wr"])
    for n, k in (("q", "Wq"), ("k", "Wk"), ("v", "Wv"), ("o", "Wo")):
        w[f"l2_{n}"] = rows_of(i[f"L2_attn_{k}"].T)
    w["mla_lat"] = rows_of(np.concatenate([i["L2_ffn_W_qd"], i["L2_ffn_W_kvd"]], 1))
    half_swap = np.concatenate([np.arange(4, 8), np.arange(4)])

    def heads(m, rope, rot=False):
        m = m.reshape(m.shape[0], HEADS, 8)
        if rot:
            m = m[:, :, half_swap]
        out = np.zeros((m.shape[0], HEADS, HD), z)
        out[:, :, 8 * rope:8 * rope + 8] = m
        return out.reshape(m.shape[0], D)

    qu, qr = heads(i["L2_ffn_W_qu"], 0), heads(i["L2_ffn_W_ropeq"], 1)
    both = np.where(np.arange(D)[None] % HD < 8, qu, qr)
    w["mla_q"] = under(both)
    w["mla_qrot"] = under(heads(i["L2_ffn_W_ropeq"], 1, True))
    w["mla_k_lat"] = under(heads(i["L2_ffn_W_ku"], 0), 64)
    w["mla_k"] = rows_of(heads(i["L2_ffn_W_ropek"], 1))
    w["mla_krot"] = rows_of(heads(i["L2_ffn_W_ropek"], 1, True))
    w["mla_v"] = under(i["L2_ffn_W_vu"], 64)
    w["mla_o"] = rows_of(i["L2_ffn_W_o"])
    w["mla_router"] = rows_of(np.concatenate([i["L2_ffn_W_router"], np.zeros((D, 1), z)], 1))
    ipw = i["L3_attn_in_proj_weight"].reshape(HEADS, 3, HD, D)
    ipb = i["L3_attn_in_proj_bias"].reshape(HEADS, 3, HD)
    for n, k in (("q", 0), ("k", 1), ("v", 2)):
        w[f"l3_{n}"] = rows_of(ipw[:, k].reshape(D, D).T)
    w["l3_o"] = rows_of(i["L3_attn_out_proj_weight"].T)
    w["l3_router"] = rows_of(i["L3_ffn_router_w"].T)
    weights = np.concatenate([w[n] for n in WEIGHT_AT], 1)

    def cols(v):
        return np.asarray(v).reshape(-1, P).T
    c = {"ln1_g": cols(i["L0_tok_ln1_g"]), "ln1_b": cols(i["L0_tok_ln1_b"])}
    for n in ("bq", "bk", "beq", "bek", "bv"):
        c[f"l0_{n}"] = cols(i[f"L0_attn_{n}"])
    for n in ("bq", "bk"):
        c[f"l2_{n}"] = cols(i[f"L2_attn_{n}"])
    c["w_ln1"], c["w_ln2"] = cols(i["L2_ffn_w_ln1"]), cols(i["L2_ffn_w_ln2"])
    c["l3_bq"], c["l3_bk"] = cols(ipb[:, 0].reshape(-1)), cols(ipb[:, 1].reshape(-1))
    c["l0_gub"] = cols(i["L0_ffn_gate_up_bias"].reshape(-1))

    mb = i["L0_attn_mix_b"]
    mixb = np.stack([mb.reshape(2, P), np.roll(mb, 1, axis=1).reshape(2, P)], 1)
    r = {"cls": i["L0_tok_cls_token"], "cls_pos": i["L0_tok_cls_pos_embedding"], "tok_b": i["L0_tok_bias"],
         "ln2_g": i["L0_tok_ln2_g"], "ln2_b": i["L0_tok_ln2_b"], "l0_bv": i["L0_attn_bv"],
         "l0_bo": i["L0_attn_bo"], "l0_ln_g": i["L0_attn_ln_g"], "l0_ln_b": i["L0_attn_ln_b"], "l0_mixb": mixb,
         "l0_ampphb": np.concatenate([i["L0_attn_amp_b"], i["L0_attn_ph_b"]]), "l0_rb": i["L0_ffn_router_bias"],
         "l2_bv": i["L2_attn_bv"], "l2_bo": i["L2_attn_bo"],
         "mla_rb": np.concatenate([i["L2_ffn_routing_bias"], np.zeros(1, z)]), "l3_bv": ipb[:, 2],
         "l3_bo": i["L3_attn_out_proj_bias"]}

    def experts(*parts):
        return np.ascontiguousarray(np.concatenate(
            [p.reshape(p.shape[0], -1, P, p.shape[2]).transpose(0, 2, 1, 3).reshape(p.shape[0], P, -1)
             for p in parts], 2))

    gu = i["L0_ffn_gate_up_proj"]
    pad_out = ((0, 0), (0, 0), (0, L1_PAD - L1_HID))
    pad_in = ((0, 0), (0, L1_PAD - L1_HID), (0, 0))

    def with_shared(shared, routed):
        return np.concatenate([i[f"L2_ffn_{shared}"][None], i[f"L2_ffn_{routed}"]], 0)
    return {
        "patches": tiled(patches), "weights": weights,
        "cols": np.concatenate([c[n] for n in COL_AT], 1),
        "rows": np.concatenate([np.asarray(r[n]).reshape(1, -1) for n in ROW_AT], 1),
        "consts": constants(),
        "l0_experts": experts(gu[:, :, :D], gu[:, :, D:], i["L0_ffn_down_proj"]),
        "l1_experts": experts(np.pad(i["L1_ffn_W2"], pad_out), np.pad(i["L1_ffn_W1"], pad_out),
                              np.pad(i["L1_ffn_W3"], pad_in)),
        "l2_experts": experts(with_shared("Wg_s", "Wg_r"), with_shared("Wu_s", "Wu_r"), with_shared("Wd_s", "Wd_r")),
        "l3_experts": experts(i["L3_ffn_w1"], i["L3_ffn_w2"]),
    }


def kernel(**inputs):
    import concourse.bacc as bacc
    from concourse.bass_utils import run_bass_kernel_spmd

    nc = bacc.Bacc("TRN2", target_bir_lowering=False, num_devices=1)
    arrays, aps = {}, {}
    for name, v in layout({k: np.asarray(v) for k, v in inputs.items()}).items():
        arrays[f"in_{name}"] = np.ascontiguousarray(v)
        aps[name] = nc.dram_tensor(f"in_{name}", v.shape, mybir.dt.from_np(v.dtype), kind="ExternalInput").ap()
    out = nc.dram_tensor("out_dram", (TOKENS, D), F32, kind="ExternalOutput").ap()
    build(nc, aps, out)
    r = run_bass_kernel_spmd(nc, [arrays], core_ids=[0])
    return r.results[0]["out_dram"].reshape(IMAGES, SEQ, D)
```

```python
from contextlib import ExitStack

import numpy as np

import concourse.bass as bass
from concourse import mybir

F32 = mybir.dt.float32
F32R = mybir.dt.float32r
U32 = mybir.dt.uint32
ALU = mybir.AluOpType
ACT = mybir.ActivationFunctionType
AX = mybir.AxisListType

P = 128
IMAGES, SEQ, D = 16, 37, 256
GRID, PATCH, CHANNELS = 6, 16, 3
PATCH_DIM = CHANNELS * PATCH * PATCH
TOKENS = IMAGES * SEQ
TILES = -(-TOKENS // P)
PADDED = TILES * P
LAST = TOKENS - (TILES - 1) * P
HALF = TOKENS // 2
Q_COLS = PADDED + 64
KT = D // P
PK = PATCH_DIM // P
HEADS, HD = 16, 16
HPT = P // HD
EPS = 1e-5
REP = 3
BLOCKS = -(-HEADS // REP)
PAIR = 64 + SEQ

L0_E, L0_TOP, L0_ALPHA, L0_LIMIT = 16, 4, 1.702, 7.0
L0_BIASES = 4
L1_E, L1_HID, L1_PAD = 8, 352, 384
L2_E = 8
L3_E, L3_FF, L3_TOP = 8, 1024, 2
CHUNK = TOKENS * L3_TOP // L3_E
HCH = CHUNK // 2
L3_GROUPS = -(-SEQ // 4)


def offsets(parts):
    at, out = 0, {}
    for name, width in parts:
        out[name] = (at, width)
        at += width
    return out, at


WEIGHTS = {
    "tok": [("tok_w", PK * D)],
    "l0": [(n, KT * D) for n in ("l0_q", "l0_k", "l0_v", "l0_eq", "l0_ek", "l0_o", "l0_mix")]
    + [("l0_ampph", KT * 2 * HEADS), ("l0_router", KT * L0_E), ("l0_down_b", D)],
    "l1": [(n, KT * D) for n in ("l1_q", "l1_qrot", "l1_k", "l1_krot", "l1_v", "l1_o")] + [("l1_router", KT * L1_E)],
    "l2": [(n, KT * D) for n in ("l2_q", "l2_k", "l2_v", "l2_o")],
    "mla": [("mla_lat", KT * P), ("mla_q", D), ("mla_qrot", D), ("mla_k_lat", D), ("mla_k", KT * D),
            ("mla_krot", KT * D), ("mla_v", D), ("mla_o", KT * D), ("mla_router", KT * 8)],
    "l3": [(n, KT * D) for n in ("l3_q", "l3_k", "l3_v", "l3_o")] + [("l3_router", KT * L3_E)],
}
WEIGHT_FROM, WEIGHT_COLS = offsets([p for parts in WEIGHTS.values() for p in parts])
WEIGHT_AT, FIRST_COLS = offsets(WEIGHTS["tok"] + WEIGHTS["l0"])
LATER_AT, LATER_COLS = offsets(WEIGHTS["l2"] + WEIGHTS["mla"])
FIRST_COLS = max(FIRST_COLS, LATER_COLS)
WEIGHT_AT.update(LATER_AT)
for layer in ("l1", "l3"):
    WEIGHT_AT.update({n: (FIRST_COLS + at, width) for n, (at, width) in offsets(WEIGHTS[layer])[0].items()})
WEIGHT_ROOM = FIRST_COLS + max(offsets(WEIGHTS[layer])[1] for layer in ("l1", "l3"))
COL_AT, COL_COLS = offsets([
    ("ln1_g", PK), ("ln1_b", PK), ("l0_bq", 2), ("l0_bk", 2), ("l0_beq", 2), ("l0_bek", 2), ("l0_bv", 2),
    ("l2_bq", 2), ("l2_bk", 2), ("w_ln1", 2), ("w_ln2", 2), ("l3_bq", 2), ("l3_bk", 2)])
ROW_AT, ROW_COLS = offsets([
    ("cls", D), ("cls_pos", D), ("tok_b", D), ("ln2_g", D), ("ln2_b", D), ("l0_bv", D), ("l0_bo", D),
    ("l0_ln_g", D), ("l0_ln_b", D), ("l0_mixb", 2 * D), ("l0_ampphb", 2 * HEADS), ("l0_rb", L0_E),
    ("l2_bv", D), ("l2_bo", D), ("mla_rb", 8), ("l3_bv", D), ("l3_bo", D)])
CONST_AT, CONST_COLS = offsets([
    ("ident", P), ("half", 2), ("minus_half", 2), ("ones", P), ("before", P), ("headmask", HPT), ("vmask37", HEADS), ("vmask16", HEADS),
    ("decay", SEQ), ("sparse", SEQ), ("causal", SEQ), ("cos1", SEQ), ("sin1", SEQ), ("cos2", SEQ),
    ("sin2", SEQ), ("pe", TILES * D), ("is_patch", TILES), ("is_cls", TILES), ("valid", TILES),
    ("earlier16", 256), ("earlier8", 64), ("earlier7", 49)])


FIRST_CONST = CONST_AT["ones"][0]
FIRST_ROW = ROW_AT["l0_bv"][0]


def constants():
    f = np.float32
    c = {}
    i128 = np.arange(P)
    c["ident"] = np.eye(P, dtype=f)
    c["ones"] = np.ones((P, P), f)
    c["before"] = (i128[:, None] < i128[None, :]).astype(f)
    c["headmask"] = (i128[:, None] // HD == np.arange(HPT)[None]).astype(f)
    c["vmask37"] = (i128[:, None] // SEQ == np.arange(HEADS)[None] % REP).astype(f)
    c["vmask16"] = (i128[:, None] // HD == np.arange(HEADS)[None] % HPT).astype(f)
    q = np.where(i128 % 64 < SEQ, i128 % 64, 0)
    j = np.arange(SEQ)
    c["decay"] = (f(0.5) * np.exp(f(-0.1) * np.abs(q[:, None] - j[None]).astype(f))).astype(f)
    sparse = np.zeros((SEQ, SEQ), f)
    for r in range(SEQ):
        sparse[r, r] = 1
        k = 0
        while 2 ** k <= r + 1:
            if r - 2 ** k >= 0:
                sparse[r, r - 2 ** k] = 1
            k += 1
    c["sparse"] = sparse[q]
    c["causal"] = np.where(q[:, None] >= j[None], 0, -1e30).astype(f)
    half = 64
    freq = np.power(f(10000.0), -(np.arange(half, dtype=f) / f(half))).astype(f)
    rad = (j.astype(f)[:, None] * freq[None]).astype(f)
    c["cos1"] = np.concatenate([np.cos(rad), np.cos(rad)], 1).T.astype(f)
    c["sin1"] = np.concatenate([-np.sin(rad), np.sin(rad)], 1).T.astype(f)
    inv = (f(1.0) / np.power(f(10000.0), np.arange(0, 8, 2, dtype=f) / f(8))).astype(f)
    ang = (j.astype(f)[:, None] * inv[None]).astype(f)
    cos8, sin8 = np.concatenate([np.cos(ang)] * 2, 1), np.concatenate([-np.sin(ang), np.sin(ang)], 1)
    head_cos = np.concatenate([np.ones((SEQ, 8)), cos8], 1)
    head_sin = np.concatenate([np.zeros((SEQ, 8)), sin8], 1)
    c["cos2"] = np.tile(head_cos, (1, HPT)).T.astype(f)
    c["sin2"] = np.tile(head_sin, (1, HPT)).T.astype(f)
    omega = (f(1.0) / np.power(f(10000.0), np.arange(D // 4, dtype=f) / f(D // 4 - 1))).astype(f)
    yy, xx = np.meshgrid(np.arange(GRID), np.arange(GRID), indexing="ij")
    ya, xa = yy.reshape(-1, 1) * omega[None], xx.reshape(-1, 1) * omega[None]
    pe = np.concatenate([np.sin(xa), np.cos(xa), np.sin(ya), np.cos(ya)], 1).astype(f)
    rows = np.zeros((PADDED, D), f)
    patch, cls, valid = (np.zeros(PADDED, f) for _ in range(3))
    for b in range(IMAGES):
        rows[b * SEQ + 1:(b + 1) * SEQ] = pe
        patch[b * SEQ + 1:(b + 1) * SEQ] = 1
        cls[b * SEQ] = 1
    valid[:TOKENS] = 1
    c["pe"] = tiled(rows)
    for name, v in (("is_patch", patch), ("is_cls", cls), ("valid", valid)):
        c[name] = np.ascontiguousarray(v.reshape(TILES, P).T)
    c["half"], c["minus_half"] = np.full((P, 2), 0.5, f), np.full((P, 2), -0.5, f)
    for e in (16, 8, 7):
        lower = (np.arange(e)[None] < np.arange(e)[:, None]).astype(f)
        c[f"earlier{e}"] = np.tile(lower.reshape(1, -1), (P, 1))
    return np.concatenate([c[n].reshape(P, -1) for n in CONST_AT], 1).astype(f)


def tiled(rows):
    n = rows.shape[1]
    return np.ascontiguousarray(rows.reshape(-1, P, n).transpose(1, 0, 2)).reshape(P, -1)


def ordered(eng, sem, start=0):
    count = [0]

    def signal(ins):
        ins.then_inc(sem, 1)
        count[0] += 1

    def wait():
        eng.wait_ge(sem, start + count[0])

    def link(ins):
        signal(ins)
        wait()
    return link, signal, wait, count


def spread(ap, pattern, shape, **sizes):
    return ap.rearrange(pattern, **sizes).broadcast_to(shape)


def pipeline(eng, total, late, step):
    def has(m):
        return not isinstance(m, int) or 0 <= m < total

    for n in range(2):
        step(n, n % 2, n // 2, has)
    with eng.Fori(1, total // 2) as i:
        for u in range(2):
            step(i * 2 + u, u, i, has)
    for n in range(total - total % 2, total + late):
        step(n, n % 2, n // 2, has)


def build(nc, a, out):
    with ExitStack() as ctx:
        names = set()
        retired = []

        def sb(name, shape, dt=F32, where=ctx):
            return where.enter_context(nc.sbuf_tensor(name, shape, dt))

        def sem(name, where=None):
            assert name not in names
            names.add(name)
            if where is None:
                return ctx.enter_context(nc.semaphore(name))
            retired.append(nc.alloc_semaphore(name))
            return retired[-1]

        def recycle():
            nc.clear_and_free_semaphores(retired)
            del retired[:]
            nc.all_engine_barrier()

        ps = ctx.enter_context(nc.psum_tensor("ps", [P, 8, 512], F32))
        w_sb = sb("w_sb", [P, WEIGHT_ROOM])
        col_sb = sb("col_sb", [P, COL_COLS])
        row_sb = sb("row_sb", [P, ROW_COLS])
        const_sb = sb("const_sb", [P, CONST_COLS])
        h = sb("h", [P, TILES, D])
        xn = sb("xn", [P, TILES, D])
        x_fm = sb("x_fm", [P, KT, PADDED])
        v_dram = nc.dram_tensor("v_scratch", [PADDED, D], F32).ap()
        perm_dram = nc.dram_tensor("perm_scratch", [TOKENS * L3_TOP, D], F32).ap()
        y_dram = nc.dram_tensor("y_scratch", [TOKENS * L3_TOP, D], F32).ap()

        def weight(name, k=KT):
            at, width = WEIGHT_AT[name]
            return w_sb[:, at:at + width].rearrange("p (k n) -> p k n", k=k)

        def col(name, i=0, n=1):
            at = COL_AT[name][0] + i
            return col_sb[:, at:at + n]

        def row(name, n=None):
            at, width = ROW_AT[name]
            return row_sb[:, at:at + (n or width)]

        def const(name):
            at, width = CONST_AT[name]
            return const_sb[:, at:at + width]

        ident = const("ident")
        loaded = {n: sem(f"loaded_{n}") for n in [*WEIGHTS, "cols", "tok_rows", "rows", "ident", "consts"]}

        norm = {n: sem(f"norm_{n}") for n in ("chain", "var", "rstd", "normed", "turned", "copied_a", "copied_v")}
        stat_bufs = {n: (sb(f"{n}_stats", [P, TILES, 2, 6]), sb(f"{n}_mv", [P, TILES, 2]), sb(f"{n}_ve", [P, TILES]),
                         sb(f"{n}_r", [P, TILES])) for n in ("norm", "affine")}
        done = {"norms": 0, "chain": 0}
        GROUPS = ((0, 2), (2, 4), (4, TILES))

        def group_stats(dve, link, signal, wait, bufs, src, tiles, s_var, rms=False, parts=1):
            stats, mv, ve, _ = bufs
            t0, t1 = tiles
            n = src.shape[2] // parts
            for t in range(t0, t1):
                for q in range(parts):
                    signal(dve.bn_stats(stats[:, t, q, :], src[:, t, q * n:(q + 1) * n]))
            wait()
            for t in range(t0, t1):
                signal(dve.bn_aggr(mv[:, t, :], stats[:, t, 0:parts, :]))
            wait()
            ve = ve[:, t0:t1]
            if rms:
                link(dve.tensor_tensor(ve, mv[:, t0:t1, 0], mv[:, t0:t1, 0], ALU.mult))
                dve.tensor_tensor(ve, ve, mv[:, t0:t1, 1], ALU.add).then_inc(s_var, 1)
            else:
                dve.tensor_scalar(ve, mv[:, t0:t1, 1], EPS, None, ALU.add).then_inc(s_var, 1)

        def group_power(pool, bufs, tiles, root, s_rstd):
            _, _, ve, r = bufs
            t0, t1 = tiles
            power = const("half" if root else "minus_half")[:, 0:t1 - t0]
            pool.tensor_tensor(r[:, t0:t1], ve[:, t0:t1], power, ALU.pow).then_inc(s_rstd, 1)

        def norm_parts(src, dst, rms=False, scale=None):
            n = done["norms"]
            done["norms"] += 1
            bufs = stat_bufs["norm"]
            _, mv, _, r = bufs
            base = n * len(GROUPS)

            def vector(dve, ready=lambda dve, g: None):
                link, signal, wait, count = ordered(dve, norm["chain"], done["chain"])

                def scaled(g):
                    t0, t1 = GROUPS[g]
                    dve.wait_ge(norm["rstd"], base + g + 1)
                    if rms:
                        link(dve.tensor_scalar(r[:, t0:t1], r[:, t0:t1], EPS, None, ALU.add))
                        link(dve.reciprocal(r[:, t0:t1], r[:, t0:t1]))
                    for t in range(t0, t1):
                        if rms:
                            ins = dve.tensor_scalar(dst[:, t, :], src[:, t, :], r[:, t:t + 1], None, ALU.mult)
                        else:
                            ins = dve.tensor_scalar(dst[:, t, :], src[:, t, :], mv[:, t, 0:1], r[:, t:t + 1],
                                                    ALU.subtract, ALU.mult)
                        ins.then_inc(norm["normed"], 1)

                for g, tiles in enumerate(GROUPS):
                    ready(dve, g)
                    group_stats(dve, link, signal, wait, bufs, src, tiles, norm["var"], rms)
                    if g:
                        scaled(g - 1)
                scaled(len(GROUPS) - 1)
                done["chain"] += count[0]
                for part, (c0, c1) in enumerate(((0, 512), (512, PADDED))):
                    dve.wait_ge(norm["turned"], 2 * n + part + 1)
                    o, i = x_fm[:, 1, c0:c1], ps[:, 2 + part, 0:c1 - c0]
                    if scale is None:
                        dve.tensor_copy(o, i).then_inc(norm["copied_v"], 1)
                    else:
                        dve.tensor_scalar(o, i, col(scale, 1), None, ALU.mult).then_inc(norm["copied_v"], 1)

            def gpsimd(pool):
                for g, tiles in enumerate(GROUPS):
                    pool.wait_ge(norm["var"], base + g + 1)
                    group_power(pool, bufs, tiles, rms, norm["rstd"])

            def tensor(pe):
                for t in range(TILES):
                    pe.wait_ge(norm["normed"], TILES * n + t + 1)
                    for k in range(KT):
                        o = ps[:, 2 * k + t // 4, (t % 4) * P:(t % 4 + 1) * P]
                        mm = pe.transpose(o, dst[:, t, k * P:(k + 1) * P], ident)
                    if t >= 3:
                        mm.then_inc(norm["turned"], 1)

            def scalar(act):
                for part, (c0, c1) in enumerate(((0, 512), (512, PADDED))):
                    act.wait_ge(norm["turned"], 2 * n + part + 1)
                    act.activation(x_fm[:, 0, c0:c1], ps[:, part, 0:c1 - c0], ACT.Copy,
                                   scale=1.0 if scale is None else col(scale, 0)).then_inc(norm["copied_a"], 1)
            return vector, gpsimd, tensor, scalar

        def normalise(src, dst, rms=False, scale=None):
            vector, gpsimd, tensor, scalar = norm_parts(src, dst, rms, scale)
            with nc.Block() as block:
                @block.vector
                def _(dve):
                    vector(dve)

                @block.gpsimd
                def _(pool):
                    gpsimd(pool)

                @block.tensor
                def _(pe):
                    tensor(pe)

                @block.scalar
                def _(act):
                    scalar(act)

        def load(sp, layer):
            parts = WEIGHTS[layer]
            to, at = WEIGHT_AT[parts[0][0]][0], WEIGHT_FROM[parts[0][0]][0]
            width = sum(WEIGHT_FROM[parts[-1][0]]) - at
            sp.dma_start(w_sb[:, to:to + width], a["weights"][:, at:at + width]).then_inc(loaded[layer], 16)

        def load_next(layers):
            with nc.Block() as block:
                @block.sync
                def _(sp):
                    for layer in layers:
                        load(sp, layer)

        def tokens():
            with ExitStack() as st:
                pat = sb("pat", [P, TILES, PATCH_DIM], where=st)
                pat_n = sb("pat_n", [P, TILES, PATCH_DIM], where=st)
                pat_fm = sb("pat_fm", [P, PK, PADDED], where=st)
                fixed = sb("tok_fixed", [P, TILES, D], where=st)
                s_pat = [sem(f"tok_pat{t}") for t in range(TILES)]
                s_chain, s_var, s_rstd, s_normed, s_turned, s_fm, s_fm_v, s_mm, s_fix, s_var2, s_rstd2, s_gain = (
                    sem(f"tok_{n}") for n in ("chain", "var", "rstd", "normed", "turned", "fm", "fm_v", "mm", "fix",
                                              "var2", "rstd2", "gain"))
                vector, gpsimd, tensor, scalar = norm_parts(h, xn)
                ACT_K = 4

                with nc.Block() as block:
                    @block.sync
                    def _(sp):
                        for t in range(TILES):
                            sp.dma_start(pat[:, t, :], a["patches"][:, t * PATCH_DIM:(t + 1) * PATCH_DIM])\
                                .then_inc(s_pat[t], 16)
                        load(sp, "l0")
                        sp.dma_start(row_sb[:, FIRST_ROW:], a["rows"][:, FIRST_ROW:]
                                     .broadcast_to([P, ROW_COLS - FIRST_ROW])).then_inc(loaded["rows"], 16)
                        load(sp, "l1")

                    @block.scalar
                    def _(act):
                        act.dma_start(const_sb[:, 0:FIRST_CONST], a["consts"][:, 0:FIRST_CONST])\
                            .then_inc(loaded["ident"], 16)
                        act.dma_start(col_sb[:, :], a["cols"]).then_inc(loaded["cols"], 16)
                        load(act, "tok")
                        act.dma_start(row_sb[:, 0:FIRST_ROW], a["rows"][:, 0:FIRST_ROW].broadcast_to([P, FIRST_ROW]))\
                            .then_inc(loaded["tok_rows"], 16)
                        act.dma_start(const_sb[:, FIRST_CONST:], a["consts"][:, FIRST_CONST:])\
                            .then_inc(loaded["consts"], 16)
                        act.wait_ge(loaded["cols"], 16)
                        for t in range(TILES):
                            act.wait_ge(s_turned, t + 1)
                            for k in range(ACT_K):
                                act.activation(pat_fm[:, k, t * P:(t + 1) * P],
                                               ps[:, 2 * (t % 2), k * P:(k + 1) * P],
                                               ACT.Identity, scale=col("ln1_g", k), bias=col("ln1_b", k))\
                                    .then_inc(s_fm, 1)
                        scalar(act)

                    @block.gpsimd
                    def _(pool):
                        def powers(g):
                            pool.wait_ge(s_var, g + 1)
                            group_power(pool, stat_bufs["norm"], GROUPS[g], False, s_rstd)

                        pool.wait_ge(loaded["ident"], 16)
                        powers(0)
                        powers(1)
                        powers(2)
                        pool.wait_ge(loaded["tok_rows"], 16)
                        pool.tensor_tensor(row("cls"), row("cls"), row("cls_pos"), ALU.add).then_inc(s_fix, 1)
                        pool.wait_ge(loaded["consts"], 16)
                        for g, (t0, t1) in enumerate(GROUPS):
                            pool.wait_ge(s_var2, g + 1)
                            group_power(pool, stat_bufs["affine"], GROUPS[g], False, s_rstd2)
                            pool.wait_ge(s_rstd2, 2 * g + 1)
                            r = stat_bufs["affine"][3][:, t0:t1]
                            pool.tensor_tensor(r, r, const("is_patch")[:, t0:t1], ALU.mult).then_inc(s_rstd2, 1)
                        gpsimd(pool)

                    @block.tensor
                    def _(pe):
                        def turn(t):
                            if t == 0:
                                pe.wait_ge(loaded["ident"], 16)
                            pe.wait_ge(s_normed, t + 1)
                            if t >= 2:
                                pe.wait_ge(s_fm, ACT_K * (t - 1))
                                pe.wait_ge(s_fm_v, (PK - ACT_K) * (t - 1))
                            for k in range(PK):
                                o = ps[:, 2 * (t % 2) + k // ACT_K, (k % ACT_K) * P:(k % ACT_K + 1) * P]
                                mm = pe.transpose(o, pat_n[:, t, k * P:(k + 1) * P], ident)
                            mm.then_inc(s_turned, 1)

                        turn(0)
                        for t in range(TILES):
                            if t + 1 < TILES:
                                turn(t + 1)
                            if t == 0:
                                pe.wait_ge(loaded["tok"], 16)
                            pe.wait_ge(s_fm, ACT_K * (t + 1))
                            pe.wait_ge(s_fm_v, (PK - ACT_K) * (t + 1))
                            for k in range(PK):
                                mm = pe.matmul(ps[:, 4 + t // 2, (t % 2) * D:(t % 2 + 1) * D],
                                               pat_fm[:, k, t * P:(t + 1) * P], weight("tok_w", PK)[:, k, :],
                                               start=(k == 0), stop=(k == PK - 1))
                            if t % 2 or t == TILES - 1:
                                mm.then_inc(s_mm, 1)
                        tensor(pe)

                    @block.vector
                    def _(dve):
                        link, signal, wait, count = ordered(dve, s_chain)
                        _, mv, _, r = stat_bufs["norm"]

                        def normed(g):
                            dve.wait_ge(s_rstd, g + 1)
                            for t in range(*GROUPS[g]):
                                dve.tensor_scalar(pat_n[:, t, :], pat[:, t, :], mv[:, t, 0:1], r[:, t:t + 1],
                                                  ALU.subtract, ALU.mult).then_inc(s_normed, 1)

                        def copied(t):
                            dve.wait_ge(s_turned, t + 1)
                            for k in range(ACT_K, PK):
                                dve.tensor_scalar(pat_fm[:, k, t * P:(t + 1) * P],
                                                  ps[:, 2 * (t % 2) + 1, (k - ACT_K) * P:(k - ACT_K + 1) * P],
                                                  col("ln1_g", k), col("ln1_b", k), ALU.mult, ALU.add)\
                                    .then_inc(s_fm_v, 1)

                        def fix(t):
                            if t == 0:
                                dve.wait_ge(s_fix, 1)
                                dve.wait_ge(loaded["consts"], 16)
                            positions = const("pe").rearrange("p (t d) -> p t d", t=TILES)
                            for name, flag, rest in (("cls", "is_cls", positions[:, t, :]),
                                                     ("ln2_b", "is_patch", fixed[:, t, :])):
                                link(dve.scalar_tensor_tensor(out=fixed[:, t, :], in0=row(name),
                                                              scalar=const(flag)[:, t:t + 1], in1=rest,
                                                              op0=ALU.mult, op1=ALU.add))

                        def first(g):
                            affine_first(dve, link, signal, wait, h, s_mm, s_var2, row("ln2_g"),
                                         lambda t: dve.tensor_tensor(h[:, t, :],
                                                                     ps[:, 4 + t // 2, (t % 2) * D:(t % 2 + 1) * D],
                                                                     row("tok_b"), ALU.add), g)

                        for g, (t0, t1) in enumerate(GROUPS):
                            for t in range(t0, t1):
                                dve.wait_ge(s_pat[t], 16)
                            group_stats(dve, link, signal, wait, stat_bufs["norm"], pat, (t0, t1), s_var, parts=2)
                            if g == 0:
                                normed(0)
                            if g == 1:
                                dve.wait_ge(loaded["cols"], 16)
                                copied(0)
                                normed(1)
                                copied(1)
                        normed(2)
                        copied(2)
                        fix(0)
                        copied(3)
                        fix(1)
                        copied(4)
                        first(0)
                        for t in range(2, TILES):
                            fix(t)

                        def ready(dve, g):
                            if g + 1 < len(GROUPS):
                                first(g + 1)
                            wait()
                            dve.wait_ge(s_rstd2, 2 * g + 2)
                            for t in range(*GROUPS[g]):
                                signal(dve.scalar_tensor_tensor(
                                    out=h[:, t, :], in0=h[:, t, :], scalar=stat_bufs["affine"][3][:, t:t + 1],
                                    in1=fixed[:, t, :], op0=ALU.mult, op1=ALU.add))
                            wait()
                        vector(dve, ready)

        def affine_first(dve, link, signal, wait, x, s_mm, s_var, gain, value, g):
            bufs = stat_bufs["affine"]
            t0, t1 = GROUPS[g]
            dve.wait_ge(s_mm, g + 1)
            for t in range(t0, t1):
                signal(value(t))
            wait()
            group_stats(dve, link, signal, wait, bufs, x, (t0, t1), s_var)
            for t in range(t0, t1):
                signal(dve.scalar_tensor_tensor(out=x[:, t, :], in0=x[:, t, :], scalar=bufs[1][:, t, 0:1],
                                                in1=gain, op0=ALU.subtract, op1=ALU.mult))

        def attend(tag, ctx_fm, q_fm, k_fm, eq_fm=None, ek_fm=None, mask=None, mask_op=None, scale=1.0):
            pairs = IMAGES // 2
            second = eq_fm is not None
            NMM = 2 if second else 1
            with ExitStack() as st:
                q_st = sb(f"{tag}_q_st", [P, 2, NMM, KT, PAIR], where=st)
                k_bd = sb(f"{tag}_k_bd", [P, 2, 2, NMM, KT, HPT, SEQ], where=st)
                v_rep = sb(f"{tag}_v_rep", [P, 2, 2, D], where=st)
                v_bd = sb(f"{tag}_v_bd", [P, 2, 2, HEADS, HD + 1], where=st)
                e_sc = sb(f"{tag}_e_sc", [P, KT, HPT, SEQ], where=st)
                shifted = sb(f"{tag}_shifted", [P, 2, HEADS, SEQ], where=st)
                top = sb(f"{tag}_top", [P, 2, HEADS], where=st)
                probs = sb(f"{tag}_probs", [P, 2, HEADS * SEQ], where=st)
                p_fm = sb(f"{tag}_p_fm", [P, 2, BLOCKS, PAIR], where=st)
                recip = sb(f"{tag}_recip", [P, 2, HEADS], where=st)
                ctx_tm = sb(f"{tag}_ctx_tm", [P, 2, HEADS, HD], where=st)
                s_vrep0, s_vrep1, s_vbd, s_stage, s_kbd, s_scores, s_shift, s_probs, s_pt, s_pfm, s_av, s_ctx, s_ct, \
                    s_ctfm, s_soft, s_norm, s_vmask, s_kbd_last = (sem(f"{tag}_{n}", st) for n in (
                        "vrep0", "vrep1", "vbd", "stage", "kbd", "scores", "shift", "probs", "pt", "pfm", "av", "ctx",
                        "ct", "ctfm", "soft", "norm", "vmask", "kbd_last"))
                s_vrep = (s_vrep0, s_vrep1)

                hm = spread(const("headmask"), "p (a h o) -> p a h o", [P, KT, HPT, SEQ], a=1, o=1)

                def block_diagonal(eng, n, u, s, m):
                    src = (k_fm, ek_fm)[m][:, :, bass.ds(n * (2 * SEQ) + s * SEQ, SEQ)]
                    return eng.tensor_tensor(k_bd[:, u, s, m, :, :, :],
                                             spread(src, "p k (o j) -> p k o j", [P, KT, HPT, SEQ], o=1), hm, ALU.mult)

                with nc.Block() as block:
                    @block.sync
                    def _(sp):
                        def step(n, u, r, has):
                            if has(n):
                                if has(n - 2):
                                    sp.wait_ge(s_vbd, n * 2 - 2)
                                src = v_dram[bass.ds(n * (2 * SEQ), 2 * SEQ), :].rearrange("(s j) d -> j s d", s=2)
                                for q in range(REP):
                                    sp.dma_start(v_rep[q * SEQ:(q + 1) * SEQ, u, :, :], src).then_inc(s_vrep[u], 16)
                        pipeline(sp, pairs, 0, step)

                    @block.gpsimd
                    def _(pool):
                        vm = const("vmask37")
                        for u in range(2):
                            for s in range(2):
                                pool.tensor_copy(v_bd[:, u, s, :, HD], vm).then_inc(s_vmask, 1)
                        vm = spread(vm[0:REP * SEQ], "p (h o) -> p h o", [REP * SEQ, HEADS, HD], o=1)

                        def step(n, u, r, has):
                            if not has(n):
                                return
                            if has(n - 2):
                                pool.wait_ge(s_scores, n * 2 - 2)
                            for m in range(NMM):
                                for s in range(2):
                                    if (m, s) != (1, 1):
                                        block_diagonal(pool, n, u, s, m).then_inc(s_kbd, 1)
                            if has(n - 2):
                                pool.wait_ge(s_av, n - 1)
                            pool.wait_ge(s_vrep[u], (r + 1) * (16 * REP))
                            for s in range(2):
                                src = v_rep[0:REP * SEQ, u, s, :].rearrange("p (h d) -> p h d", h=HEADS)
                                pool.tensor_tensor(v_bd[0:REP * SEQ, u, s, :, 0:HD], src, vm, ALU.mult)\
                                    .then_inc(s_vbd, 1)
                        pipeline(pool, pairs, 0, step)

                    @block.scalar
                    def _(act):
                        act.preload_act_table(ACT.Exp)
                        act.sem_inc(s_ctfm, 1)

                        def stage(n, u):
                            for m, fm in enumerate((q_fm, eq_fm)[:NMM]):
                                act.activation(q_st[:, u, m, :, :], fm[:, :, bass.ds(n * (2 * SEQ), PAIR)],
                                               ACT.Copy).then_inc(s_stage, 1)

                        def step(n, u, r, has):
                            if isinstance(n, int) and n == 0:
                                stage(0, 0)
                            if has(n - 1):
                                act.wait_ge(s_pt, n)
                                act.activation(
                                    p_fm[0:REP * SEQ, 1 - u, 0:4, :],
                                    ps[0:REP * SEQ, 4, :].rearrange("p (b r) -> p b r", b=4)[:, :, 0:PAIR],
                                    ACT.Copy).then_inc(s_pfm, 1)
                                act.activation(p_fm[0:REP * SEQ, 1 - u, 4, :], ps[0:REP * SEQ, 5, 0:PAIR],
                                               ACT.Copy).then_inc(s_pfm, 1)
                                act.activation(p_fm[0:SEQ, 1 - u, 5, :], ps[0:SEQ, 5, P:P + PAIR],
                                               ACT.Copy).then_inc(s_pfm, 1)
                            if has(n):
                                if has(n - 1):
                                    act.wait_ge(s_scores, n * 2)
                                stage(n + 1, 1 - u)
                            if has(n - 2):
                                act.wait_ge(s_ct, n - 1)
                                src = ps[:, 7, 0:KT * P].rearrange("p (k s j) -> p k s j", k=KT, s=2)
                                dst = ctx_fm[:, :, bass.ds((n - 2) * (2 * SEQ), 2 * SEQ)]
                                act.activation(dst.rearrange("p k (s j) -> p k s j", s=2), src[:, :, :, 0:SEQ],
                                               ACT.Copy).then_inc(s_ctfm, 1)
                            if has(n):
                                act.wait_ge(s_shift, n * 2 + 2)
                                act.activation(probs[:, u, :], shifted[:, u, :, :].rearrange("p h j -> p (h j)"),
                                               ACT.Exp, scale=scale).then_inc(s_probs, 1)
                        pipeline(act, pairs, 2, step)

                    @block.tensor
                    def _(pe):
                        def scores(n, u, k, has):
                            if has(n - 1):
                                pe.wait_ge(s_shift, n * 2 + (k - 1))
                            for m in range(NMM):
                                for s in range(2):
                                    mm = pe.matmul(
                                        ps[64 * s:64 * s + 64, 2 * m + k, 0:HPT * SEQ],
                                        q_st[:, u, m, k, SEQ * s:SEQ * s + 64],
                                        k_bd[:, u, s, m, k, :, :].rearrange("p h j -> p (h j)"),
                                        start=True, stop=True)
                            mm.then_inc(s_scores, 1)

                        def step(n, u, r, has):
                            v = 1 - u
                            if has(n):
                                pe.wait_ge(s_stage, (n + 1) * NMM)
                                pe.wait_ge(s_kbd, (n + 1) * (3 if second else 2))
                                if second:
                                    pe.wait_ge(s_kbd_last, n + 1)
                                scores(n, u, 0, has)
                            if has(n - 1):
                                pe.wait_ge(s_probs, n)
                                if has(n - 2):
                                    pe.wait_ge(s_pfm, n * 3 - 3)
                                for b in range(BLOCKS):
                                    w = min(REP, HEADS - REP * b) * SEQ
                                    mm = pe.transpose(ps[0:w, 4 + b // 4, (b % 4) * P:(b % 4 + 1) * P],
                                                      probs[:, v, b * REP * SEQ:b * REP * SEQ + w], ident)
                                mm.then_inc(s_pt, 1)
                            if has(n):
                                scores(n, u, 1, has)
                            if has(n - 2):
                                pe.wait_ge(s_ctx, n - 1)
                                pe.wait_ge(s_ctfm, n - 1)
                                for k in range(KT):
                                    mm = pe.transpose(ps[:, 7, k * P:k * P + PAIR],
                                                      ctx_tm[0:PAIR, u, k * HPT:(k + 1) * HPT, :]
                                                      .rearrange("p h d -> p (h d)"), ident[0:PAIR, 0:PAIR])
                                mm.then_inc(s_ct, 1)
                            if has(n - 1):
                                pe.wait_ge(s_pfm, n * 3)
                                pe.wait_ge(s_vbd, n * 2)
                                pe.wait_ge(s_vmask, 4)
                                for s in range(2):
                                    rows = 64 if s == 0 else SEQ
                                    for b in range(BLOCKS):
                                        nh = min(REP, HEADS - REP * b)
                                        mm = pe.matmul(
                                            ps[64 * s:64 * s + rows, 6,
                                               b * REP * (HD + 1):(b * REP + nh) * (HD + 1)],
                                            p_fm[0:nh * SEQ, v, b, 64 * s:64 * s + rows],
                                            v_bd[0:nh * SEQ, v, s, b * REP:b * REP + nh, :]
                                            .rearrange("p h d -> p (h d)"),
                                            start=True, stop=True)
                                mm.then_inc(s_av, 1)
                        pipeline(pe, pairs, 2, step)

                    @block.vector
                    def _(dve):
                        soft_links = 3 if second else 2
                        mask3 = spread(mask, "p (b j) -> p b j", [P, HPT, SEQ], b=1)
                        out3 = ps[0:PAIR, 6, 0:HEADS * (HD + 1)].rearrange("p (h d) -> p h d", h=HEADS)

                        def step(n, u, r, has):
                            if second and isinstance(n, int) and n == 0:
                                block_diagonal(dve, 0, 0, 1, 1).then_inc(s_kbd_last, 1)
                            if second and has(n):
                                if has(n - 1):
                                    dve.wait_ge(s_scores, n * 2)
                                block_diagonal(dve, n + 1, 1 - u, 1, 1).then_inc(s_kbd_last, 1)
                            if has(n):
                                for k in range(KT):
                                    link, signal, wait, count = ordered(dve, s_soft, (n * 2 + k) * soft_links)
                                    scores, scores2 = (ps[:, b + k, 0:HPT * SEQ].rearrange("p (h j) -> p h j", h=HPT)
                                                       for b in (0, 2))
                                    heads = slice(k * HPT, (k + 1) * HPT)
                                    dve.wait_ge(s_scores, n * 2 + (k + 1))
                                    if second:
                                        link(dve.tensor_tensor(e_sc[:, k, :, :], scores2, mask3, ALU.mult))
                                        link(dve.tensor_tensor(scores, scores, e_sc[:, k, :, :], ALU.add))
                                    else:
                                        link(dve.tensor_tensor(scores, scores, mask3, mask_op))
                                    link(dve.tensor_reduce(top[:, u, heads], scores, AX.X, ALU.max))
                                    dve.tensor_tensor(shifted[:, u, heads, :], scores,
                                                      spread(top[:, u, heads], "p (h o) -> p h o", [P, HPT, SEQ], o=1),
                                                      ALU.subtract).then_inc(s_shift, 1)
                            if has(n - 1):
                                dve.wait_ge(s_av, n)
                                dve.reciprocal(recip[0:PAIR, u, :], out3[:, :, HD]).then_inc(s_norm, 1)
                                dve.wait_ge(s_norm, n)
                                dve.tensor_tensor(ctx_tm[0:PAIR, 1 - u, :, :], out3[:, :, 0:HD],
                                                  spread(recip[0:PAIR, u, :], "p (h o) -> p h o",
                                                         [PAIR, HEADS, HD], o=1), ALU.mult).then_inc(s_ctx, 1)
                        pipeline(dve, pairs, 2, step)


        def project(tag, layer, jobs, v_terms, v_bias=None, v_tm=None, pads=()):
            rot = jobs[0][1] is not None
            slots = 2 if rot else 4
            units = [(job, half) for job in jobs for half in range(2)]
            with ExitStack() as st:
                own_v = v_tm is None
                v_tm = v_tm if v_tm is not None else sb(f"{tag}_v_tm", [P, TILES, D], where=st)
                t1 = sb(f"{tag}_rot_a", [P, 2, HALF], where=st)
                t2 = sb(f"{tag}_rot_b", [P, 2, HALF], where=st)
                s_unit, s_v, s_vout, s_vd, s_pads, s_t, s_sum = (
                    sem(f"{tag}_{n}", st) for n in ("unit", "v", "vout", "vd", "pads", "t", "sum"))
                s_free = [sem(f"{tag}_free{i}", st) for i in range(slots)]

                with nc.Block() as block:
                    @block.tensor
                    def _(pe):
                        pe.wait_ge(loaded[layer], 16)
                        for t in range(TILES):
                            if t >= 4:
                                pe.wait_ge(s_vout, t - 3)
                            for k, (w, src) in enumerate(v_terms):
                                mm = pe.matmul(ps[:, 4 + t % 4, 0:D], src[:, t * P:(t + 1) * P], w,
                                               start=(k == 0), stop=(k == len(v_terms) - 1))
                            mm.then_inc(s_v, 1)
                        for i, ((terms, rterms, _, _, _, _), half) in enumerate(units):
                            slot = i % slots
                            if i >= slots:
                                pe.wait_ge(s_free[slot], i // slots)
                            c0 = half * HALF
                            for b, part in enumerate((terms, rterms) if rot else (terms,)):
                                for k, (w, src) in enumerate(part):
                                    mm = pe.matmul(ps[:, slot * (2 if rot else 1) + b, 0:HALF], w,
                                                   src[:, c0:c0 + HALF], start=(k == 0), stop=(k == len(part) - 1))
                            mm.then_inc(s_unit, 1)

                    @block.vector
                    def _(dve):
                        dve.wait_ge(loaded["rows"], 16)
                        for t in range(TILES):
                            dve.wait_ge(s_v, t + 1)
                            src = ps[:, 4 + t % 4, 0:D]
                            if v_bias is None:
                                dve.tensor_copy(v_tm[:, t, :], src).then_inc(s_vout, 1)
                            else:
                                dve.tensor_tensor(v_tm[:, t, :], src, v_bias, ALU.add).then_inc(s_vout, 1)
                        for i, ((_, _, dst, bias, cos, sin), half) in enumerate(units):
                            slot, c0 = i % slots, half * HALF
                            if rot:
                                dve.wait_ge(s_unit, i + 1)
                                if i >= 2:
                                    dve.wait_ge(s_sum, i - 1)
                                shape = [P, HALF // SEQ, SEQ]
                                for b, (table, t) in enumerate(((cos, t1), (sin, t2))):
                                    ins = dve.tensor_tensor(
                                        t[:, i % 2, :].rearrange("p (i j) -> p i j", j=SEQ),
                                        ps[:, slot * 2 + b, 0:HALF].rearrange("p (i j) -> p i j", j=SEQ),
                                        spread(table, "p (a j) -> p a j", shape, a=1), ALU.mult)
                                    ins.then_inc(s_free[slot] if b else s_t, 1)
                            elif slot % 2:
                                dve.wait_ge(s_unit, i + 1)
                                dst, src = dst[:, c0:c0 + HALF], ps[:, slot, 0:HALF]
                                if bias is None:
                                    dve.tensor_copy(dst, src).then_inc(s_free[slot], 1)
                                else:
                                    dve.tensor_scalar(dst, src, bias, None, ALU.add).then_inc(s_free[slot], 1)

                    @block.scalar
                    def _(act):
                        if not rot:
                            for i, ((_, _, dst, bias, _, _), half) in enumerate(units):
                                slot, c0 = i % slots, half * HALF
                                if slot % 2 == 0:
                                    act.wait_ge(s_unit, i + 1)
                                    act.activation(dst[:, c0:c0 + HALF], ps[:, slot, 0:HALF], ACT.Identity,
                                                   bias=0.0 if bias is None else bias).then_inc(s_free[slot], 1)

                    @block.gpsimd
                    def _(pool):
                        for p in pads:
                            pool.memset(p, 0.0).then_inc(s_pads, 1)
                        if rot:
                            for i, ((_, _, dst, _, _, _), half) in enumerate(units):
                                c0 = half * HALF
                                pool.wait_ge(s_t, i + 1)
                                pool.wait_ge(s_free[i % slots], i // slots + 1)
                                pool.tensor_tensor(dst[:, c0:c0 + HALF], t1[:, i % 2, :], t2[:, i % 2, :],
                                                   ALU.add).then_inc(s_sum, 1)

                    @block.sync
                    def _(sp):
                        if own_v:
                            for t in range(TILES):
                                sp.wait_ge(s_vout, t + 1)
                                sp.dma_start(v_dram[t * P:(t + 1) * P, :], v_tm[:, t, :]).then_inc(s_vd, 16)
                            sp.wait_ge(s_vd, 16 * TILES)

        def plain(w_name, dst, bias=None):
            w = weight(w_name)
            return [([(w[:, k, m * P:(m + 1) * P], x_fm[:, k, :]) for k in range(KT)], None, dst[:, m, :],
                     None if bias is None else col(bias, m), None, None) for m in range(KT)]

        def value_terms(w_name):
            return [(weight(w_name)[:, k, :], x_fm[:, k, :]) for k in range(KT)]

        def project_out(tag, ctx_fm, w_name, bias, target, norm_args, prefetch=None, affine=None):
            vector, gpsimd, tensor, scalar = norm_parts(*norm_args)
            with ExitStack() as st:
                s_mm, s_add, s_bias, s_var, s_rstd, s_off = (
                    sem(f"{tag}_{n}", st) for n in ("omm", "oadd", "obias", "ovar", "orstd", "ooff"))
                with nc.Block() as block:
                    @block.tensor
                    def _(pe):
                        for t in range(TILES):
                            for k in range(KT):
                                mm = pe.matmul(ps[:, 4 + t // 2, (t % 2) * D:(t % 2 + 1) * D],
                                               ctx_fm[:, k, t * P:(t + 1) * P],
                                               weight(w_name)[:, k, :], start=(k == 0), stop=(k == KT - 1))
                            if t % 2 or t == TILES - 1:
                                mm.then_inc(s_mm, 1)
                        tensor(pe)

                    @block.scalar
                    def _(act):
                        scalar(act)

                    @block.gpsimd
                    def _(pool):
                        if bias is not None:
                            for t in range(TILES):
                                pool.tensor_tensor(target[:, t, :], target[:, t, :], bias, ALU.add)\
                                    .then_inc(s_bias, 1)
                        if affine is not None:
                            for t in range(TILES):
                                pool.tensor_tensor(h[:, t, :], h[:, t, :], affine[1], ALU.add).then_inc(s_off, 1)
                            for g, tiles in enumerate(GROUPS):
                                pool.wait_ge(s_var, g + 1)
                                group_power(pool, stat_bufs["affine"], tiles, False, s_rstd)
                        gpsimd(pool)

                    @block.vector
                    def _(dve):
                        link, signal, wait, count = ordered(dve, s_add)

                        def value(t):
                            if bias is not None:
                                dve.wait_ge(s_bias, t + 1)
                            return dve.tensor_tensor(target[:, t, :], ps[:, 4 + t // 2, (t % 2) * D:(t % 2 + 1) * D],
                                                     target[:, t, :], ALU.add)

                        def ready(dve, g):
                            if affine is None:
                                dve.wait_ge(s_mm, g + 1)
                                for t in range(*GROUPS[g]):
                                    signal(value(t))
                            else:
                                if g + 1 < len(GROUPS):
                                    first(g + 1)
                                wait()
                                dve.wait_ge(s_rstd, g + 1)
                                dve.wait_ge(s_off, TILES)
                                for t in range(*GROUPS[g]):
                                    signal(dve.scalar_tensor_tensor(
                                        out=h[:, t, :], in0=target[:, t, :], scalar=stat_bufs["affine"][3][:, t:t + 1],
                                        in1=h[:, t, :], op0=ALU.mult, op1=ALU.add))
                            wait()

                        def first(g):
                            affine_first(dve, link, signal, wait, target, s_mm, s_var, affine[0], value, g)
                        if affine is not None:
                            first(0)
                        vector(dve, ready)

                    if prefetch is not None:
                        @block.sync
                        def _(sp):
                            prefetch(sp)

        def mix_values(v_fm, v_tm):
            PI = 3.1415925
            with ExitStack() as st:
                ap_ = sb("mix_ap", [P, TILES, 2 * HEADS], where=st)
                amp = sb("mix_amp", [P, TILES, HEADS], where=st)
                ph = sb("mix_ph", [P, TILES, HEADS], where=st)
                sn = sb("mix_sin", [P, TILES, HEADS], where=st)
                hs = sb("mix_half_sin", [P, TILES, HEADS], where=st)
                coef = sb("mix_coef", [P, TILES, KT, 2, HPT], where=st)
                sup = sb("mix_sup", [P, 2, KT, 2, HPT, HD], where=st)
                s_ap, s_mm, s_chain, s_act, s_sup, s_pool, s_vd = (
                    sem(f"mix_{n}", st) for n in ("ap", "mm", "chain", "act", "sup", "pool", "vd"))
                with nc.Block() as block:
                    @block.tensor
                    def _(pe):
                        for t in range(TILES):
                            for k in range(KT):
                                mm = pe.matmul(ps[:, 7, t * 32:(t + 1) * 32], x_fm[:, k, t * P:(t + 1) * P],
                                               weight("l0_ampph")[:, k, :], start=(k == 0), stop=(k == KT - 1))
                        mm.then_inc(s_ap, 1)
                        for t in range(TILES):
                            for k in range(KT):
                                mm = pe.matmul(ps[:, t, k * D:(k + 1) * D], v_fm[:, k, t * P:(t + 1) * P],
                                               weight("l0_mix")[:, k, :], start=True, stop=True)
                            mm.then_inc(s_mm, 1)

                    @block.scalar
                    def _(act):
                        act.wait_ge(s_chain, 1)
                        act.activation(amp[:, :, :], ap_[:, :, 0:HEADS], ACT.Sigmoid).then_inc(s_act, 1)
                        act.activation(ph[:, :, :], ap_[:, :, HEADS:], ACT.Tanh).then_inc(s_act, 1)
                        act.wait_ge(s_act, 2)
                        act.activation(sn[:, :, :], ph[:, :, :], ACT.Sin, scale=PI).then_inc(s_act, 1)
                        act.activation(hs[:, :, :], ph[:, :, :], ACT.Sin, scale=PI / 2).then_inc(s_act, 1)

                    @block.vector
                    def _(dve):
                        link, signal, wait, count = ordered(dve, s_chain)
                        dve.wait_ge(s_ap, 1)
                        link(dve.tensor_tensor(
                            ap_[:, :, :], ps[:, 7, 0:TILES * 32].rearrange("p (t n) -> p t n", t=TILES),
                            spread(row("l0_ampphb"), "p (a n) -> p a n", [P, TILES, 32], a=1), ALU.add))
                        dve.wait_ge(s_act, 4)
                        link(dve.tensor_tensor(hs[:, :, :], hs[:, :, :], hs[:, :, :], ALU.mult))
                        link(dve.tensor_scalar(hs[:, :, :], hs[:, :, :], -2.0, 1.0, ALU.mult, ALU.add))
                        link(dve.tensor_scalar(amp[:, :, :], amp[:, :, :], 0.3, None, ALU.mult))
                        for i, trig in enumerate((hs, sn)):
                            for k in range(KT):
                                link(dve.tensor_tensor(coef[:, :, k, i, :], amp[:, :, k * HPT:(k + 1) * HPT],
                                                             trig[:, :, k * HPT:(k + 1) * HPT], ALU.mult))
                        for t in range(TILES):
                            dve.wait_ge(s_mm, t + 1)
                            if t >= 2:
                                dve.wait_ge(s_pool, 4 * (t - 1))
                            link(dve.tensor_tensor(ps[:, t, :], ps[:, t, :], row("l0_mixb"), ALU.add))
                            dve.tensor_tensor(
                                sup[:, t % 2, :, :, :, :].rearrange("p k i h d -> p (k i h) d"),
                                ps[:, t, :].rearrange("p (n d) -> p n d", d=HD),
                                spread(coef[:, t, :, :, :].rearrange("p k i h -> p (k i h)"), "p (n o) -> p n o",
                                       [P, 2 * HEADS, HD], o=1), ALU.mult).then_inc(s_sup, 1)

                    @block.gpsimd
                    def _(pool):
                        for t in range(TILES):
                            pool.wait_ge(s_sup, t + 1)
                            for i in range(2):
                                if i:
                                    pool.wait_ge(s_pool, 4 * t + 2)
                                for k in range(KT):
                                    v = v_tm[:, t, k * P:(k + 1) * P]
                                    pool.tensor_tensor(v, v, sup[:, t % 2, k, i, :, :].rearrange("p h d -> p (h d)"),
                                                       ALU.add).then_inc(s_pool, 1)

                    @block.sync
                    def _(sp):
                        for t in range(TILES):
                            sp.wait_ge(s_pool, 4 * (t + 1))
                            sp.dma_start(v_dram[t * P:(t + 1) * P, :], v_tm[:, t, :]).then_inc(s_vd, 16)
                        sp.wait_ge(s_vd, 16 * TILES)

        def attend_wide(ctx_fm, q_fm, k_fm, scale):
            pairs = IMAGES // 2
            units = pairs * KT
            with ExitStack() as st:
                v_img = sb("l1_v_img", [P, IMAGES, D], where=st)
                shifted = sb("l1_shifted", [P, 2, units // 2, SEQ], where=st)
                top = sb("l1_top", [P, 2, units // 2], where=st)
                total = sb("l1_total", [P, units], where=st)
                p_fm = sb("l1_p_fm", [P, units, PAIR], where=st)
                ctx_tm = sb("l1_ctx_tm", [P, pairs, D], where=st)
                s_v, s_scores, s_chain, s_probs, s_pt, s_pfm, s_av, s_ctx, s_ct, s_ctfm, s_total = (
                    sem(f"l1_{n}", st) for n in ("vimg", "scores", "chain", "probs", "pt", "pfm", "av", "ctx",
                                                 "ct", "ctfm", "total"))
                with nc.Block() as block:
                    @block.sync
                    def _(sp):
                        sp.dma_start(v_img[0:SEQ, :, :], v_dram[0:TOKENS, :].rearrange("(b j) d -> j b d", j=SEQ))\
                            .then_inc(s_v, 16)

                    @block.tensor
                    def _(pe):
                        for q in range(2):
                            for p in range(4 * q, 4 * q + 4):
                                for hd in range(KT):
                                    for s in range(2):
                                        c = (2 * p + s) * SEQ
                                        mm = pe.matmul(
                                            ps[64 * s:64 * s + 64, q, ((p % 4) * 2 + hd) * SEQ:((p % 4) * 2 + hd + 1) * SEQ],
                                            q_fm[:, hd, c:c + 64], k_fm[:, hd, c:c + SEQ], start=True, stop=True)
                            mm.then_inc(s_scores, 1)
                        for b in range(4):
                            pe.wait_ge(s_probs, b // 2 + 1)
                            for i in range(4):
                                n = 4 * b + i
                                mm = pe.transpose(ps[0:SEQ, 2 + b, i * P:(i + 1) * P],
                                                  shifted[:, n // 8, n % 8, :], ident)
                            mm.then_inc(s_pt, 1)
                        pe.wait_ge(s_v, 16)
                        for b in range(4):
                            pe.wait_ge(s_pfm, b + 1)
                            for i in range(4):
                                n = 4 * b + i
                                for s in range(2):
                                    rows = 64 if s == 0 else SEQ
                                    mm = pe.matmul(ps[64 * s:64 * s + rows, (6 + b) % 8, i * P:(i + 1) * P],
                                                   p_fm[0:SEQ, n, 64 * s:64 * s + rows],
                                                   v_img[0:SEQ, 2 * (n // 2) + s, (n % 2) * P:(n % 2 + 1) * P],
                                                   start=True, stop=True)
                            mm.then_inc(s_av, 1)
                        for b in range(4):
                            pe.wait_ge(s_ctx, b + 1)
                            for i in range(4):
                                n = 4 * b + i
                                mm = pe.transpose(ps[:, 2 + b, i * P:i * P + PAIR],
                                                  ctx_tm[0:PAIR, n // 2, (n % 2) * P:(n % 2 + 1) * P],
                                                  ident[0:PAIR, 0:PAIR])
                            mm.then_inc(s_ct, 1)

                    @block.vector
                    def _(dve):
                        link, signal, wait, count = ordered(dve, s_chain)
                        for q in range(2):
                            dve.wait_ge(s_scores, q + 1)
                            sc = ps[:, q, 0:8 * SEQ].rearrange("p (n j) -> p n j", j=SEQ)
                            link(dve.tensor_tensor(sc, sc, spread(const("causal"), "p (a j) -> p a j",
                                                                        [P, 8, SEQ], a=1), ALU.add))
                            link(dve.tensor_reduce(top[:, q, :], sc, AX.X, ALU.max))
                            signal(dve.tensor_tensor(shifted[:, q, :, :], sc,
                                                           spread(top[:, q, :], "p (n o) -> p n o", [P, 8, SEQ], o=1),
                                                           ALU.subtract))
                        for q in range(2):
                            dve.wait_ge(s_probs, q + 1)
                            signal(dve.tensor_reduce(total[:, 8 * q:8 * q + 8], shifted[:, q, :, :], AX.X, ALU.add))
                        wait()
                        link(dve.reciprocal(total[:, :], total[:, :]))
                        for b in range(4):
                            dve.wait_ge(s_av, b + 1)
                            dve.tensor_tensor(
                                ctx_tm[0:PAIR, 2 * b:2 * b + 2, :].rearrange("p a (h d) -> p (a h) d", h=KT),
                                ps[0:PAIR, (6 + b) % 8, :].rearrange("p (n d) -> p n d", n=4),
                                spread(total[0:PAIR, 4 * b:4 * b + 4], "p (n o) -> p n o", [PAIR, 4, P], o=1),
                                ALU.mult).then_inc(s_ctx, 1)

                    @block.scalar
                    def _(act):
                        for q in range(2):
                            act.wait_ge(s_chain, 3 * (q + 1))
                            act.activation(shifted[:, q, :, :], shifted[:, q, :, :], ACT.Exp, scale=scale)\
                                .then_inc(s_probs, 1)
                        for b in range(4):
                            act.wait_ge(s_pt, b + 1)
                            act.activation(p_fm[0:SEQ, 4 * b:4 * b + 4, :],
                                           ps[0:SEQ, 2 + b, :].rearrange("p (n r) -> p n r", n=4)[:, :, 0:PAIR],
                                           ACT.Copy).then_inc(s_pfm, 1)
                        for b in range(4):
                            act.wait_ge(s_ct, b + 1)
                            for p in range(2):
                                src = ps[:, 2 + b, p * 2 * P:(p + 1) * 2 * P].rearrange("p (k s j) -> p k s j", k=KT, s=2)
                                c = (2 * b + p) * 2 * SEQ
                                act.activation(ctx_fm[:, :, c:c + 2 * SEQ].rearrange("p k (s j) -> p k s j", s=2),
                                               src[:, :, :, 0:SEQ], ACT.Copy).then_inc(s_ctfm, 1)

        def attend_across(ctx_fm, q_fm, k_fm, scale):
            groups, S = L3_GROUPS, IMAGES
            tag = "l3a"
            with ExitStack() as st:
                q_st = sb(f"{tag}_q_st", [P, 2, KT, 4, 32], where=st)
                k_bd = sb(f"{tag}_k_bd", [P, 2, 4, KT, HPT, S], where=st)
                v_rep = sb(f"{tag}_v_rep", [P, 2, 4, D], where=st)
                v_bd = sb(f"{tag}_v_bd", [P, 2, 4, HEADS, HD + 1], where=st)
                shifted = sb(f"{tag}_shifted", [P, 2, HEADS, S], where=st)
                top = sb(f"{tag}_top", [P, 2, HEADS], where=st)
                probs = sb(f"{tag}_probs", [P, 2, HEADS * S], where=st)
                p_fm = sb(f"{tag}_p_fm", [P, 2, KT, P], where=st)
                recip = sb(f"{tag}_recip", [P, 2, HEADS], where=st)
                ctx_tm = sb(f"{tag}_ctx_tm", [P, 2, HEADS, HD], where=st)
                s_vrep0, s_vrep1, s_vbd, s_stage, s_kbd, s_scores, s_shift, s_probs, s_pt, s_pfm, s_av, s_ctx, \
                    s_ct, s_ctfm, s_soft, s_norm, s_vmask, s_zero = (sem(f"{tag}_{n}", st) for n in (
                        "vrep0", "vrep1", "vbd", "stage", "kbd", "scores", "shift", "probs", "pt", "pfm", "av",
                        "ctx", "ct", "ctfm", "soft", "norm", "vmask", "zero"))
                s_vrep = (s_vrep0, s_vrep1)

                def positions(fm, g, n=4):
                    cols = fm[:, :, bass.ds(g * 4, TOKENS)]
                    return cols.rearrange("p k (s b) -> p k b s", b=SEQ)[:, :, 0:n, :]

                with nc.Block() as block:
                    @block.sync
                    def _(sp):
                        def step(n, u, r, has):
                            if has(n):
                                if has(n - 2):
                                    sp.wait_ge(s_vbd, n - 1)
                                src = v_dram[bass.ds(n * 4, TOKENS), :].rearrange("(s b) d -> s b d", b=SEQ)[:, 0:4, :]
                                for q in range(HPT):
                                    sp.dma_start(v_rep[q * S:(q + 1) * S, u, :, :], src).then_inc(s_vrep[u], 16)
                        pipeline(sp, groups, 0, step)

                    @block.gpsimd
                    def _(pool):
                        vm = const("vmask16")
                        for u in range(2):
                            for c in range(4):
                                pool.tensor_copy(v_bd[:, u, c, :, HD], vm).then_inc(s_vmask, 1)
                        hm = spread(const("headmask"), "p (a h o) -> p a h o", [P, KT, HPT, S], a=1, o=1)

                        def step(n, u, r, has):
                            if not has(n):
                                return
                            if has(n - 2):
                                pool.wait_ge(s_scores, n - 1)
                            for c in range(4):
                                src = k_fm[:, :, bass.ds(n * 4 + c, TOKENS)]
                                src = src.rearrange("p k (s b) -> p k b s", b=SEQ)[:, :, 0:1, :]
                                pool.tensor_tensor(k_bd[:, u, c, :, :, :], src.broadcast_to([P, KT, HPT, S]), hm,
                                                   ALU.mult).then_inc(s_kbd, 1)
                        pipeline(pool, groups, 0, step)

                    @block.scalar
                    def _(act):
                        act.preload_act_table(ACT.Exp)
                        act.sem_inc(s_ctfm, 1)

                        def stage(n, u):
                            act.activation(q_st[:, u, :, :, 0:S], positions(q_fm, n), ACT.Copy).then_inc(s_stage, 1)

                        def step(n, u, r, has):
                            if isinstance(n, int) and n == 0:
                                act.wait_ge(s_zero, 2)
                                stage(0, 0)
                            if has(n - 1):
                                act.wait_ge(s_pt, n)
                                act.activation(p_fm[:, 1 - u, :, :].rearrange("p k r -> p (k r)"),
                                               ps[:, 4, 0:KT * P], ACT.Copy).then_inc(s_pfm, 1)
                            if has(n) and has(n + 1):
                                if has(n - 1):
                                    act.wait_ge(s_scores, n)
                                stage(n + 1, 1 - u)
                            if has(n - 2):
                                act.wait_ge(s_ct, n - 1)
                                real = 4 if not isinstance(n, int) or n - 2 < groups - 1 else SEQ - 4 * (groups - 1)
                                src = ps[:, 7, 0:KT * P].rearrange("p (k c s) -> p k c s", k=KT, c=4)
                                act.activation(positions(ctx_fm, n - 2, real), src[:, :, 0:real, 0:S],
                                               ACT.Copy).then_inc(s_ctfm, 1)
                            if has(n):
                                act.wait_ge(s_shift, n + 1)
                                act.activation(probs[:, u, :], shifted[:, u, :, :].rearrange("p h j -> p (h j)"),
                                               ACT.Exp, scale=scale).then_inc(s_probs, 1)
                        pipeline(act, groups, 2, step)

                    @block.tensor
                    def _(pe):
                        def step(n, u, r, has):
                            v = 1 - u
                            if has(n - 1):
                                pe.wait_ge(s_probs, n)
                                if has(n - 2):
                                    pe.wait_ge(s_pfm, n - 1)
                                for k in range(KT):
                                    mm = pe.transpose(ps[:, 4, k * P:(k + 1) * P],
                                                      probs[:, v, k * P:(k + 1) * P], ident)
                                mm.then_inc(s_pt, 1)
                            if has(n):
                                pe.wait_ge(s_stage, n + 1)
                                pe.wait_ge(s_kbd, (n + 1) * 4)
                                if has(n - 1):
                                    pe.wait_ge(s_shift, n)
                                for c in range(4):
                                    for k in range(KT):
                                        mm = pe.matmul(ps[32 * c:32 * c + 32, k, 0:HPT * S], q_st[:, u, k, c, :],
                                                       k_bd[:, u, c, k, :, :].rearrange("p h j -> p (h j)"),
                                                       start=True, stop=True)
                                mm.then_inc(s_scores, 1)
                            if has(n - 2):
                                pe.wait_ge(s_ctx, n - 1)
                                pe.wait_ge(s_ctfm, n - 1)
                                for k in range(KT):
                                    mm = pe.transpose(ps[:, 7, k * P:(k + 1) * P],
                                                      ctx_tm[:, u, k * HPT:(k + 1) * HPT, :]
                                                      .rearrange("p h d -> p (h d)"), ident)
                                mm.then_inc(s_ct, 1)
                            if has(n - 1):
                                pe.wait_ge(s_pfm, n)
                                pe.wait_ge(s_vbd, n)
                                pe.wait_ge(s_vmask, 8)
                                for c in range(4):
                                    for k in range(KT):
                                        mm = pe.matmul(
                                            ps[32 * c:32 * c + 32, 6, k * HPT * (HD + 1):(k + 1) * HPT * (HD + 1)],
                                            p_fm[:, v, k, 32 * c:32 * c + 32],
                                            v_bd[:, v, c, k * HPT:(k + 1) * HPT, :].rearrange("p h d -> p (h d)"),
                                            start=True, stop=True)
                                mm.then_inc(s_av, 1)
                        pipeline(pe, groups, 2, step)

                    @block.vector
                    def _(dve):
                        scores = ps[:, 0:2, 0:HPT * S].rearrange("p k (h j) -> p k h j", h=HPT)
                        out3 = ps[:, 6, 0:HEADS * (HD + 1)].rearrange("p (h d) -> p h d", h=HEADS)
                        vm = spread(const("vmask16"), "p (a h o) -> p a h o", [P, 4, HEADS, HD], a=1, o=1)
                        for u in range(2):
                            dve.memset(q_st[:, u, :, :, :], 0.0).then_inc(s_zero, 1)

                        def step(n, u, r, has):
                            if has(n):
                                dve.wait_ge(s_scores, n + 1)
                                t3 = top[:, u, :].rearrange("p (k h) -> p k h", k=KT)
                                dve.tensor_reduce(t3, scores, AX.X, ALU.max).then_inc(s_soft, 1)
                                dve.wait_ge(s_soft, n + 1)
                                dve.tensor_tensor(shifted[:, u, :, :].rearrange("p (k h) j -> p k h j", k=KT), scores,
                                                  spread(t3, "p k (h o) -> p k h o", [P, KT, HPT, S], o=1),
                                                  ALU.subtract).then_inc(s_shift, 1)
                                dve.wait_ge(s_vrep[u], (r + 1) * (16 * HPT))
                                if has(n - 2):
                                    dve.wait_ge(s_av, n - 1)
                                dve.tensor_tensor(v_bd[:, u, :, :, 0:HD],
                                                  v_rep[:, u, :, :].rearrange("p c (h d) -> p c h d", h=HEADS),
                                                  vm, ALU.mult).then_inc(s_vbd, 1)
                            if has(n - 1):
                                dve.wait_ge(s_av, n)
                                dve.reciprocal(recip[:, u, :], out3[:, :, HD]).then_inc(s_norm, 1)
                                dve.wait_ge(s_norm, n)
                                dve.tensor_tensor(ctx_tm[:, 1 - u, :, :], out3[:, :, 0:HD],
                                                  spread(recip[:, u, :], "p (h o) -> p h o", [P, HEADS, HD], o=1),
                                                  ALU.mult).then_inc(s_ctx, 1)
                        pipeline(dve, groups, 2, step)

        def zero_pads(tag, fm):
            with ExitStack() as st:
                s_zero = sem(tag, st)
                with nc.Block() as block:
                    @block.gpsimd
                    def _(pool):
                        pool.memset(fm[:, :, TOKENS:], 0.0).then_inc(s_zero, 1)

        def latents(tag, lat, terms):
            with ExitStack() as st:
                s_mm, s_cp = sem(f"{tag}_mm", st), sem(f"{tag}_cp", st)
                with nc.Block() as block:
                    @block.tensor
                    def _(pe):
                        pe.wait_ge(loaded["mla"], 16)
                        for half in range(2):
                            for k, (w, src) in enumerate(terms):
                                mm = pe.matmul(ps[:, half, 0:HALF], w, src[:, half * HALF:(half + 1) * HALF],
                                               start=(k == 0), stop=(k == KT - 1))
                            mm.then_inc(s_mm, 1)

                    @block.scalar
                    def _(act):
                        for half in range(2):
                            act.wait_ge(s_mm, half + 1)
                            act.activation(lat[:, half * HALF:(half + 1) * HALF], ps[:, half, 0:HALF], ACT.Copy)\
                                .then_inc(s_cp, 1)

                    @block.gpsimd
                    def _(pool):
                        pool.memset(lat[:, TOKENS:], 0.0).then_inc(s_cp, 1)

        def add_rows(tag, gates):
            with ExitStack() as st:
                s_add = sem(tag, st)
                with nc.Block() as block:
                    @block.gpsimd
                    def _(pool):
                        for t in range(TILES):
                            pool.tensor_tensor(h[:, t, :], h[:, t, :], xn[:, t, :], ALU.add).then_inc(s_add, 1)
                        pool.memset(gates[:, :, 0:1], 1.0).then_inc(s_add, 1)

        expert_w = sb("expert_w", [P, 2, 4096])
        s_w = [sem("expert_w0"), sem("expert_w1")]
        fetched = [0, 0]

        def fetch(sp, name, width, e, u):
            sp.dma_start(expert_w[:, u, 0:width], a[name][bass.ds(e, 1), :, :].rearrange("e p n -> p (e n)"))\
                .then_inc(s_w[u], 16)

        def fetch_first(name, width):
            def run(sp):
                for e in range(2):
                    fetch(sp, name, width, e, e)
            return run

        def ranks(tag, st, link, signal, dve, score, E):
            above = sb(f"{tag}_above", [P, TILES, E, E], where=st)
            same = sb(f"{tag}_same", [P, TILES, E, E], where=st)
            rank = sb(f"{tag}_rank", [P, TILES, E], where=st)
            shape = [P, TILES, E, E]
            other, own = (spread(score, pattern, shape, o=1) for pattern in ("p t (o e) -> p t o e", "p t (e o) -> p t e o"))
            earlier = spread(const(f"earlier{E}"), "p (t e f) -> p t e f", shape, t=1, f=E)
            signal(dve.tensor_tensor(above[:, :, :, :], other, own, ALU.is_gt))
            link(dve.tensor_tensor(same[:, :, :, :], other, own, ALU.is_equal))
            link(dve.tensor_tensor(same[:, :, :, :], same[:, :, :, :], earlier, ALU.mult))
            link(dve.tensor_tensor(above[:, :, :, :], above[:, :, :, :], same[:, :, :, :], ALU.add))
            link(dve.tensor_reduce(rank[:, :, :], above[:, :, :, :], AX.X, ALU.add))
            return rank

        def route(tag, E, top, router, bias, gates, kind, down_b=None, first=None):
            with ExitStack() as st:
                lg = sb(f"{tag}_lg", [P, TILES, E], where=st)
                red = sb(f"{tag}_red", [P, TILES], where=st)
                gate_fm = sb(f"{tag}_gate_fm", [E, PADDED], where=st) if down_b is not None else None
                s_mm, s_chain, s_exp, s_gate, s_gt, s_gfm, s_bias = (
                    sem(f"{tag}_r{n}", st) for n in ("mm", "chain", "exp", "gate", "gt", "gfm", "bias"))
                red3 = spread(red[:, :], "p (t o) -> p t o", [P, TILES, E], o=1)
                width = router.shape[2]
                with nc.Block() as block:
                    @block.tensor
                    def _(pe):
                        for t in range(TILES):
                            for k in range(KT):
                                mm = pe.matmul(ps[:, 0, t * width:(t + 1) * width], x_fm[:, k, t * P:(t + 1) * P],
                                               router[:, k, :], start=(k == 0), stop=(k == KT - 1))
                        mm.then_inc(s_mm, 1)
                        if down_b is not None:
                            pe.wait_ge(s_gate, 1)
                            for t in range(TILES):
                                mm = pe.transpose(ps[0:E, 1 + t // 4, (t % 4) * P:(t % 4 + 1) * P], gates[:, t, :], ident)
                            mm.then_inc(s_gt, 1)
                            pe.wait_ge(s_gfm, 2)
                            for t in range(TILES):
                                pe.matmul(ps[:, 3 + t, 0:D], gate_fm[:, t * P:(t + 1) * P], down_b,
                                          start=True, stop=True).then_inc(s_bias, 1)

                    @block.scalar
                    def _(act):
                        first["act"](act)
                        act.wait_ge(s_chain, 3 if kind == "softmax" else 1)
                        func = ACT.Exp if kind == "softmax" else ACT.Sigmoid
                        act.activation(lg[:, :, :], lg[:, :, :], func).then_inc(s_exp, 1)
                        if down_b is not None:
                            act.wait_ge(s_gt, 1)
                            for b, (c0, c1) in enumerate(((0, 512), (512, PADDED))):
                                act.activation(gate_fm[:, c0:c1], ps[0:E, 1 + b, 0:c1 - c0], ACT.Copy)\
                                    .then_inc(s_gfm, 1)

                    @block.gpsimd
                    def _(pool):
                        first["pool"](pool)

                    @block.vector
                    def _(dve):
                        link, signal, wait, count = ordered(dve, s_chain)
                        dve.wait_ge(s_mm, 1)
                        src = ps[:, 0, 0:TILES * width].rearrange("p (t e) -> p t e", t=TILES)[:, :, 0:E]
                        if bias is None:
                            link(dve.tensor_copy(lg[:, :, :], src))
                        else:
                            link(dve.tensor_tensor(lg[:, :, :], src, spread(bias, "p (a e) -> p a e", [P, TILES, E], a=1),
                                                         ALU.add))
                        if kind == "softmax":
                            link(dve.tensor_reduce(red[:, :], lg[:, :, :], AX.X, ALU.max))
                            link(dve.tensor_tensor(lg[:, :, :], lg[:, :, :], red3, ALU.subtract))
                            dve.wait_ge(s_exp, 1)
                            link(dve.tensor_reduce(red[:, :], lg[:, :, :], AX.X, ALU.add))
                            link(dve.reciprocal(red[:, :], red[:, :]))
                            link(dve.tensor_tensor(lg[:, :, :], lg[:, :, :], red3, ALU.mult))
                        dve.wait_ge(s_exp, 1)
                        rank = ranks(tag, st, link, signal, dve, lg[:, :, :], E)
                        link(dve.tensor_scalar(rank[:, :, :], rank[:, :, :], float(top), None, ALU.is_lt))
                        link(dve.tensor_tensor(gates, rank[:, :, :], lg[:, :, :], ALU.mult))
                        if kind == "sigmoid":
                            link(dve.tensor_reduce(red[:, :], gates, AX.X, ALU.add))
                            link(dve.reciprocal(red[:, :], red[:, :]))
                            link(dve.tensor_tensor(gates, gates, red3, ALU.mult))
                        dve.sem_inc(s_gate, 1)
                        if down_b is not None:
                            for t in range(TILES):
                                dve.wait_ge(s_bias, t + 1)
                                signal(dve.tensor_tensor(h[:, t, :], ps[:, 3 + t, 0:D], h[:, t, :], ALU.add))

        def experts(tag, w_in, E, mt, gates, routing, clipped=False):
            units = 2 * mt
            up_w, down_w = KT * mt * P, mt * D
            width = 2 * up_w + down_w
            fetch_w = width + (L0_BIASES if clipped else 0)
            base = list(fetched)
            with ExitStack() as st:
                x_hi, x_lo = (sb(f"{tag}_x_{n}", [P, KT, PADDED], F32R, where=st) for n in ("hi", "lo"))
                up_hi, up_lo = (sb(f"{tag}_up_{n}", [P, 2, 2 * up_w], F32R, where=st) for n in ("hi", "lo"))
                down_hi, down_lo = (sb(f"{tag}_down_{n}", [P, 2, down_w], F32R, where=st) for n in ("hi", "lo"))
                hid_hi, hid_lo = (sb(f"{tag}_hid_{n}", [P, 2, mt, PADDED], F32R, where=st) for n in ("hi", "lo"))
                bias_sb = sb(f"{tag}_bias_sb", [P, 2, L0_BIASES], where=st) if clipped else None
                gate_sb, up_sb, hid = (sb(f"{tag}_{n}", [P, 2, HALF], where=st) for n in ("gate_sb", "up_sb", "hid"))
                (s_pads, s_whi, s_wlo, s_up, s_gate, s_upb, s_clip, s_silu, s_hid, s_hhi, s_hlo, s_down, s_acc) = (
                    sem(f"{tag}_{n}", st) for n in ("pads", "whi", "wlo", "up", "gate", "upb", "clip", "silu", "hid",
                                                    "hhi", "hlo", "down", "acc"))

                def wa(part, u, which, k, m):
                    at = which * up_w + k * mt * P + m * P
                    return part[:, u, at:at + P]

                def up_high(act, n, u, r, has):
                    act.wait_ge(s_w[u], (r + (1 + base[u])) * 16)
                    if has(n - 2):
                        act.wait_ge(s_up, (n - 1) * units)
                    act.activation(up_hi[:, u, :], expert_w[:, u, 0:2 * up_w], ACT.Copy).then_inc(s_whi, 1)
                    if clipped:
                        act.activation(bias_sb[:, u, :], expert_w[:, u, width:width + L0_BIASES], ACT.Copy)\
                            .then_inc(s_bias, 1)

                def down_high(act, n, u, has):
                    if has(n - 2):
                        act.wait_ge(s_down, n * 3 - 3)
                    act.activation(down_hi[:, u, :], expert_w[:, u, 2 * up_w:width], ACT.Copy).then_inc(s_whi, 1)

                def up_low(pool, n, u):
                    pool.wait_ge(s_whi, 1 if isinstance(n, int) and n == 0 else 2 * n)
                    pool.tensor_tensor(up_lo[:, u, :], expert_w[:, u, 0:2 * up_w], up_hi[:, u, :].bitcast(F32),
                                       ALU.subtract).then_inc(s_wlo, 1)

                def down_low(pool, n, u, E_last):
                    pool.wait_ge(s_whi, n * 2 + (2 if E_last else 3))
                    pool.tensor_tensor(down_lo[:, u, :], expert_w[:, u, 2 * up_w:width], down_hi[:, u, :].bitcast(F32),
                                       ALU.subtract).then_inc(s_wlo, 1)

                s_xhi, s_scaled, s_bias = (sem(f"{tag}_{n}", st) for n in ("xhi", "scaled", "bias"))

                def first_act(act):
                    for k in range(KT):
                        act.activation(x_hi[:, k, :], x_fm[:, k, :], ACT.Copy).then_inc(s_xhi, 1)
                    up_high(act, 0, 0, 0, lambda m: m == 0)

                def first_pool(pool):
                    for k in range(KT):
                        pool.wait_ge(s_xhi, k + 1)
                        pool.tensor_tensor(x_lo[:, k, :], x_fm[:, k, :], x_hi[:, k, :].bitcast(F32), ALU.subtract)\
                            .then_inc(s_pads, 1)
                    up_low(pool, 0, 0)
                routing({"act": first_act, "pool": first_pool})
                vector, gpsimd, tensor, scalar = norm_parts(h, xn)

                with nc.Block() as block:
                    @block.sync
                    def _(sp):
                        def step(n, u, r, has):
                            if has(n - 2):
                                sp.wait_ge(s_wlo, n * 2 - 1)
                                if clipped:
                                    sp.wait_ge(s_bias, n)
                                fetch(sp, w_in, fetch_w, n, u)
                        pipeline(sp, E, 0, step)

                    @block.gpsimd
                    def _(pool):
                        for part in (hid_hi, hid_lo):
                            pool.memset(part[:, :, :, TOKENS:].bitcast(F32), 0.0).then_inc(s_pads, 1)

                        def step(n, u, r, has):
                            if has(n) and not (isinstance(n, int) and n == 0):
                                up_low(pool, n, u)
                            if has(n - 1):
                                v = 1 - u
                                down_low(pool, n - 1, v, not has(n))
                                for j in range(units):
                                    m, half, slot = j // 2, j % 2, j % 2
                                    cols = slice(half * HALF, (half + 1) * HALF)
                                    pool.wait_ge(s_hhi, n * units + (j + 1 - units))
                                    pool.tensor_tensor(hid_lo[:, v, m, cols], hid[:, slot, :],
                                                       hid_hi[:, v, m, cols].bitcast(F32), ALU.subtract)\
                                        .then_inc(s_hlo, 1)
                        pipeline(pool, E, 1, step)
                        gpsimd(pool)

                    @block.tensor
                    def _(pe):
                        pe.wait_ge(s_pads, 4)

                        def products(out, left, right, last):
                            for k in range(last + 1):
                                (lh, ll), (rh, rl) = left(k), right(k)
                                pe.matmul(out, lh, rh, start=(k == 0), stop=False)
                                pe.matmul(out, lh, rl, start=False, stop=False)
                                mm = pe.matmul(out, ll, rh, start=False, stop=(k == last))
                            return mm

                        def step(n, u, r, has):
                            if has(n):
                                pe.wait_ge(s_wlo, 1 if isinstance(n, int) and n == 0 else n * 2)
                                for j in range(units):
                                    m, half, slot = j // 2, j % 2, j % 2
                                    cols = slice(half * HALF, (half + 1) * HALF)
                                    for which in range(2):
                                        if has(n - 1) or j >= 2:
                                            if clipped:
                                                s = s_upb if which else s_gate
                                            else:
                                                s = s_hid if which else s_silu
                                            pe.wait_ge(s, n * units + (j - 1))
                                        mm = products(ps[:, 2 * slot + which, 0:HALF],
                                                      lambda k: (wa(up_hi, u, which, k, m), wa(up_lo, u, which, k, m)),
                                                      lambda k: (x_hi[:, k, cols], x_lo[:, k, cols]), KT - 1)
                                    mm.then_inc(s_up, 1)
                            if has(n - 1):
                                v = 1 - u
                                pe.wait_ge(s_hlo, n * units)
                                pe.wait_ge(s_wlo, n * 2 + 1 if has(n) else n * 2)
                                for b in range(3):
                                    if has(n - 2):
                                        pe.wait_ge(s_acc, n * 3 - 5 + b)
                                    for t in range(2 * b, min(2 * b + 2, TILES)):
                                        rows = slice(t * P, (t + 1) * P)
                                        mm = products(ps[:, 4 + b, (t % 2) * D:(t % 2 + 1) * D],
                                                      lambda m: (hid_hi[:, v, m, rows], hid_lo[:, v, m, rows]),
                                                      lambda m: (down_hi[:, v, m * D:(m + 1) * D],
                                                                 down_lo[:, v, m * D:(m + 1) * D]), mt - 1)
                                    mm.then_inc(s_down, 1)
                        pipeline(pe, E, 1, step)
                        tensor(pe)

                    @block.scalar
                    def _(act):
                        act.preload_act_table(ACT.Silu)

                        def step(n, u, r, has):
                            if has(n) and not (isinstance(n, int) and n == 0):
                                up_high(act, n, u, r, has)
                            if has(n - 1):
                                v, e = 1 - u, n - 1
                                down_high(act, e, v, has)

                                def high(j):
                                    m, half, slot = j // 2, j % 2, j % 2
                                    act.wait_ge(s_hid, e * units + (j + 1))
                                    act.activation(hid_hi[:, v, m, half * HALF:(half + 1) * HALF], hid[:, slot, :],
                                                   ACT.Copy).then_inc(s_hhi, 1)

                                for j in range(units):
                                    m, slot = j // 2, j % 2
                                    if has(n - 2) or j >= 2:
                                        act.wait_ge(s_hid, e * units + (j - 1))
                                    if clipped:
                                        if j == 0:
                                            act.wait_ge(s_bias, n)
                                        act.wait_ge(s_up, e * units + (j + 1))
                                        act.activation(up_sb[:, slot, :], ps[:, 2 * slot + 1, 0:HALF], ACT.Identity,
                                                       bias=bias_sb[:, v, mt + m:mt + m + 1]).then_inc(s_upb, 1)
                                        act.wait_ge(s_gate, e * units + (j + 1))
                                        act.activation(gate_sb[:, slot, :], gate_sb[:, slot, :], ACT.Silu,
                                                       scale=L0_ALPHA).then_inc(s_silu, 1)
                                    else:
                                        act.wait_ge(s_up, e * units + (j + 1))
                                        act.activation(gate_sb[:, slot, :], ps[:, 2 * slot, 0:HALF], ACT.Silu)\
                                            .then_inc(s_silu, 1)
                                    if j:
                                        high(j - 1)
                                high(units - 1)
                        pipeline(act, E, 1, step)
                        scalar(act)

                    @block.vector
                    def _(dve):
                        if clipped:
                            dve.tensor_scalar(gates[:, :, :], gates[:, :, :], 1.0 / L0_ALPHA, None, ALU.mult)\
                                .then_inc(s_scaled, 1)
                            dve.wait_ge(s_scaled, 1)

                        def step(n, u, r, has):
                            if has(n):
                                def hidden(j):
                                    m, slot = j // 2, j % 2
                                    g = n * units + j
                                    dve.wait_ge(s_silu, g + 1)
                                    if has(n - 1) or j >= 2:
                                        dve.wait_ge(s_hlo, g - 1)
                                    if clipped:
                                        dve.wait_ge(s_clip, g + 1)
                                        dve.scalar_tensor_tensor(out=hid[:, slot, :], in0=up_sb[:, slot, :], scalar=1.0,
                                                                 in1=gate_sb[:, slot, :], op0=ALU.add, op1=ALU.mult)\
                                            .then_inc(s_hid, 1)
                                    else:
                                        dve.tensor_tensor(hid[:, slot, :], ps[:, 2 * slot + 1, 0:HALF],
                                                          gate_sb[:, slot, :], ALU.mult).then_inc(s_hid, 1)

                                for j in range(units):
                                    m, slot = j // 2, j % 2
                                    g = n * units + j
                                    if clipped:
                                        if j == 0:
                                            dve.wait_ge(s_bias, n + 1)
                                        dve.wait_ge(s_up, g + 1)
                                        if has(n - 1) or j >= 2:
                                            dve.wait_ge(s_hid, g - 1)
                                        dve.tensor_scalar(gate_sb[:, slot, :], ps[:, 2 * slot, 0:HALF],
                                                          bias_sb[:, u, m:m + 1], L0_LIMIT, ALU.add, ALU.min)\
                                            .then_inc(s_gate, 1)
                                        dve.wait_ge(s_upb, g + 1)
                                        dve.tensor_scalar(up_sb[:, slot, :], up_sb[:, slot, :], L0_LIMIT, -L0_LIMIT,
                                                          ALU.min, ALU.max).then_inc(s_clip, 1)
                                        if j:
                                            hidden(j - 1)
                                        if j == units - 1:
                                            hidden(j)
                                    else:
                                        hidden(j)
                            if has(n - 1) and has(n):
                                for b in range(3):
                                    add(n, b, has)

                        def add(n, b, has=lambda m: True):
                            dve.wait_ge(s_down, n * 3 - 2 + b)
                            if has(n - 2):
                                dve.wait_ge(s_acc, n * 3 - 5 + b)
                            for t in range(*GROUPS[b]):
                                ins = dve.scalar_tensor_tensor(
                                    out=h[:, t, :], in0=ps[:, 4 + b, (t % 2) * D:(t % 2 + 1) * D],
                                    scalar=gates[:, t, bass.ds(n - 1, 1)], in1=h[:, t, :],
                                    op0=ALU.mult, op1=ALU.add)
                            ins.then_inc(s_acc, 1)
                        pipeline(dve, E, 1, step)

                        def ready(dve, g):
                            add(E, g)
                            dve.wait_ge(s_acc, 3 * (E - 1) + g + 1)
                        vector(dve, ready)
            fetched[0] += E // 2
            fetched[1] += E // 2

        def chunked_experts():
            E = L3_E
            base = list(fetched)
            with ExitStack() as st:
                lg = sb("l3_lg", [P, TILES, E], where=st)
                cnt = sb("l3_cnt", [P, TILES, E], where=st)
                pick = sb("l3_pick", [P, 2, TILES, E], where=st)
                tmp = sb("l3_tmp", [P, TILES, E], where=st)
                chosen = sb("l3_chosen", [P, TILES, E], where=st)
                offs = sb("l3_offs", [P, E, E], where=st)
                off = sb("l3_off", [P, E], where=st)
                tot = sb("l3_tot", [P, E], where=st)
                place = sb("l3_place", [P, 2, TILES], where=st)
                place_u = sb("l3_place_u", [P, 2, TILES], U32, where=st)
                best = sb("l3_best", [P, 2, TILES], where=st)
                share = sb("l3_share", [P, 2, TILES], where=st)
                s_mm, s_chain, s_m, s_cnt, s_e, s_idx, s_sc = (
                    sem(f"l3r_{n}", st) for n in ("mm", "chain", "m", "cnt", "e", "idx", "sc"))
                with nc.Block() as block:
                    @block.tensor
                    def _(pe):
                        router = weight("l3_router")
                        for t in range(TILES):
                            for k in range(KT):
                                mm = pe.matmul(ps[:, 0, t * E:(t + 1) * E], x_fm[:, k, t * P:(t + 1) * P],
                                               router[:, k, :], start=(k == 0), stop=(k == KT - 1))
                        mm.then_inc(s_mm, 1)
                        pe.wait_ge(s_m, 1)
                        flat = chosen[:, :, :].rearrange("p t e -> p (t e)")
                        for b, table in ((1, "before"), (2, "ones")):
                            mm = pe.matmul(ps[:, b, 0:TILES * E], const(table), flat, start=True, stop=True)
                        mm.then_inc(s_cnt, 1)

                    @block.scalar
                    def _(act):
                        act.wait_ge(s_idx, 1)
                        act.activation(share[:, 1, :], share[:, 1, :], ACT.Exp).then_inc(s_e, 1)

                    @block.vector
                    def _(dve):
                        link, signal, wait, count = ordered(dve, s_chain)
                        dve.wait_ge(s_mm, 1)
                        link(dve.tensor_copy(lg[:, :, :], ps[:, 0, 0:TILES * E].rearrange("p (t e) -> p t e", t=TILES)))
                        rank = ranks("l3", st, link, signal, dve, lg[:, :, :], E)
                        valid = spread(const("valid"), "p (t o) -> p t o", [P, TILES, E], o=1)
                        link(dve.tensor_scalar(chosen[:, :, :], rank[:, :, :], float(L3_TOP), None, ALU.is_lt))
                        link(dve.tensor_tensor(chosen[:, :, :], chosen[:, :, :], valid, ALU.mult))
                        dve.sem_inc(s_m, 1)
                        for i in range(2):
                            link(dve.tensor_scalar(pick[:, i, :, :], rank[:, :, :], float(i), None, ALU.is_equal))
                            link(dve.tensor_tensor(tmp[:, :, :], pick[:, i, :, :], lg[:, :, :], ALU.mult))
                            link(dve.tensor_reduce(best[:, i, :], tmp[:, :, :], AX.X, ALU.add))
                        link(dve.tensor_tensor(share[:, 1, :], best[:, 1, :], best[:, 0, :], ALU.subtract))
                        dve.sem_inc(s_idx, 1)
                        dve.wait_ge(s_e, 1)
                        link(dve.tensor_scalar(share[:, 0, :], share[:, 1, :], 1.0, None, ALU.add))
                        link(dve.reciprocal(share[:, 0, :], share[:, 0, :]))
                        link(dve.tensor_tensor(share[:, 1, :], share[:, 1, :], share[:, 0, :], ALU.mult))
                        dve.wait_ge(s_cnt, 1)
                        link(dve.tensor_copy(cnt[:, :, :], ps[:, 1, 0:TILES * E].rearrange("p (t e) -> p t e", t=TILES)))
                        link(dve.tensor_copy(tot[:, :], ps[:, 2, 0:E]))
                        for t in range(1, TILES):
                            link(dve.tensor_tensor(cnt[:, t, :], cnt[:, t, :], tot[:, :], ALU.add))
                            link(dve.tensor_tensor(tot[:, :], ps[:, 2, t * E:(t + 1) * E], tot[:, :], ALU.add))
                        link(dve.tensor_tensor(offs[:, :, :], spread(tot[:, :], "p (o e) -> p o e", [P, E, E], o=1),
                                                     const("earlier8").rearrange("p (e f) -> p e f", e=E), ALU.mult))
                        link(dve.tensor_reduce(off[:, :], offs[:, :, :], AX.X, ALU.add))
                        link(dve.tensor_tensor(cnt[:, :, :], cnt[:, :, :],
                                                     spread(off[:, :], "p (o e) -> p o e", [P, TILES, E], o=1), ALU.add))
                        for i in range(2):
                            link(dve.tensor_tensor(tmp[:, :, :], pick[:, i, :, :], cnt[:, :, :], ALU.mult))
                            link(dve.tensor_reduce(place[:, i, :], tmp[:, :, :], AX.X, ALU.add))
                            link(dve.tensor_copy(place_u[:, i, :], place[:, i, :]))
                        dve.sem_inc(s_idx, 1)

                    @block.gpsimd
                    def _(pool):
                        pool.wait_ge(s_idx, 2)
                        for t in range(TILES):
                            rows = P if t < TILES - 1 else LAST
                            for i in range(2):
                                pool.indirect_dma_start(
                                    perm_dram, bass.IndirectOffsetOnAxis(ap=place_u[0:rows, i, t:t + 1], axis=0),
                                    xn[0:rows, t, :], None).then_inc(s_sc, 16)
                        pool.wait_ge(s_sc, 16 * 2 * TILES)

                width = KT * L3_FF + L3_FF // P * D
                MT = L3_FF // P
                xp_tm = sb("l3_xp_tm", [HCH, 2, 2, D], where=st)
                xp_fm = sb("l3_xp_fm", [P, 2, KT, CHUNK], where=st)
                hid = sb("l3_hid", [P, 2, MT, CHUNK], where=st)
                y_fm = sb("l3_y_fm", [P, 2, KT, CHUNK], where=st)
                y_tm = sb("l3_y_tm", [HCH, 2, 2, D], where=st)
                s_x = [sem(f"l3c_x{u}", st) for u in range(2)]
                s_y = [sem(f"l3c_y{u}", st) for u in range(2)]
                s_xt, s_xfm, s_up, s_hid, s_down, s_yfm, s_yt, s_ytm = (
                    sem(f"l3c_{n}", st) for n in ("xt", "xfm", "up", "hid", "down", "yfm", "yt", "ytm"))

                def chunk_rows(dram, n):
                    return dram[bass.ds(n * CHUNK, CHUNK), :].rearrange("(q p) d -> p q d", q=2)

                with nc.Block() as block:
                    @block.sync
                    def _(sp):
                        def step(n, u, r, has):
                            if has(n):
                                if has(n - 2):
                                    sp.wait_ge(s_xt, n - 1)
                                sp.dma_start(xp_tm[:, u, :, :], chunk_rows(perm_dram, n)).then_inc(s_x[u], 16)
                            if has(n) and has(n - 2):
                                sp.wait_ge(s_down, n * 2 - 2)
                                fetch(sp, "l3_experts", width, n, u)
                            if has(n - 2):
                                sp.wait_ge(s_ytm, n)
                                sp.dma_start(chunk_rows(y_dram, n - 2), y_tm[:, u, :, :]).then_inc(s_y[u], 16)
                        for u in range(2):
                            sp.sem_inc(s_y[u], 16)
                        pipeline(sp, E, 2, step)
                        for u in range(2):
                            sp.wait_ge(s_y[u], 16 * (E // 2 + 1))

                    @block.tensor
                    def _(pe):
                        def step(n, u, r, has):
                            v = 1 - u
                            if has(n - 1):
                                pe.wait_ge(s_w[v], (r + base[v] + (1 if v == 0 else 0)) * 16)
                                pe.wait_ge(s_xfm, n)
                                for j in range(MT // 2):
                                    if has(n - 2):
                                        pe.wait_ge(s_hid, n * 4 - 7 + j)
                                    for i in range(2):
                                        for k in range(KT):
                                            at = k * L3_FF + (2 * j + i) * P
                                            mm = pe.matmul(ps[:, 1 + j, i * CHUNK:(i + 1) * CHUNK],
                                                           expert_w[:, v, at:at + P], xp_fm[:, v, k, :],
                                                           start=(k == 0), stop=(k == KT - 1))
                                    mm.then_inc(s_up, 1)
                            if has(n):
                                pe.wait_ge(s_x[u], (r + 1) * 16)
                                if has(n - 1):
                                    pe.wait_ge(s_xfm, n)
                                for k in range(KT):
                                    for q in range(2):
                                        mm = pe.transpose(ps[:, 0, k * CHUNK + q * HCH:k * CHUNK + (q + 1) * HCH],
                                                          xp_tm[:, u, q, k * P:(k + 1) * P], ident[0:HCH, 0:HCH])
                                mm.then_inc(s_xt, 1)
                            if has(n - 2):
                                pe.wait_ge(s_yfm, n * 2 - 2)
                                pe.wait_ge(s_ytm, n - 1)
                                for q in range(2):
                                    for m in range(KT):
                                        mm = pe.transpose(ps[0:HCH, 7, q * D + m * P:q * D + (m + 1) * P],
                                                          y_fm[:, u, m, q * HCH:(q + 1) * HCH], ident)
                                mm.then_inc(s_yt, 1)
                            if has(n - 1):
                                for m in range(KT):
                                    if has(n - 2):
                                        pe.wait_ge(s_yfm, n * 2 - 3 + m)
                                    for k in range(MT):
                                        if m == 0 and k % 2 == 0:
                                            pe.wait_ge(s_hid, n * 4 - 3 + k // 2)
                                        at = KT * L3_FF + k * D + m * P
                                        mm = pe.matmul(ps[:, 5 + m, 0:CHUNK], expert_w[:, v, at:at + P],
                                                       hid[:, v, k, :], start=(k == 0), stop=(k == MT - 1))
                                    mm.then_inc(s_down, 1)
                        pipeline(pe, E, 2, step)

                    @block.scalar
                    def _(act):
                        act.preload_act_table(ACT.Gelu)

                        def step(n, u, r, has):
                            if has(n - 1):
                                for j in range(MT // 2):
                                    act.wait_ge(s_up, n * 4 - 3 + j)
                                    act.activation(hid[:, 1 - u, 2 * j:2 * j + 2, :].rearrange("p i c -> p (i c)"),
                                                   ps[:, 1 + j, 0:2 * CHUNK], ACT.Gelu).then_inc(s_hid, 1)
                        pipeline(act, E, 1, step)

                    @block.vector
                    def _(dve):
                        dve.sem_inc(s_ytm, 1)

                        def step(n, u, r, has):
                            if has(n):
                                dve.wait_ge(s_xt, n + 1)
                                dve.tensor_copy(xp_fm[:, u, :, :].rearrange("p k c -> p (k c)"), ps[:, 0, 0:KT * CHUNK])\
                                    .then_inc(s_xfm, 1)
                            if has(n - 2):
                                dve.wait_ge(s_yt, n - 1)
                                dve.wait_ge(s_y[u], r * 16)
                                dve.tensor_copy(y_tm[:, u, :, :].rearrange("p q d -> p (q d)"), ps[0:HCH, 7, :])\
                                    .then_inc(s_ytm, 1)
                            if has(n - 1):
                                for m in range(KT):
                                    dve.wait_ge(s_down, n * 2 - 1 + m)
                                    dve.tensor_copy(y_fm[:, 1 - u, m, :], ps[:, 5 + m, 0:CHUNK]).then_inc(s_yfm, 1)
                        pipeline(dve, E, 2, step)

                back = sb("l3_back", [P, 2, TILES, D], where=st)
                s_back = [sem(f"l3b_back{t}", st) for t in range(TILES)]
                s_add, s_out = sem("l3b_add", st), sem("l3b_out", st)
                with nc.Block() as block:
                    @block.gpsimd
                    def _(pool):
                        for t in range(TILES):
                            rows = P if t < TILES - 1 else LAST
                            for i in range(2):
                                pool.indirect_dma_start(
                                    back[0:rows, i, t, :], None, y_dram,
                                    bass.IndirectOffsetOnAxis(ap=place_u[0:rows, i, t:t + 1], axis=0))\
                                    .then_inc(s_back[t], 16)

                    @block.vector
                    def _(dve):
                        for t in range(TILES):
                            rows = P if t < TILES - 1 else LAST
                            dve.wait_ge(s_back[t], 32)
                            for i in range(2):
                                if i:
                                    dve.wait_ge(s_add, 2 * t + 1)
                                x = h[0:rows, t, :]
                                dve.scalar_tensor_tensor(out=x, in0=back[0:rows, i, t, :],
                                                         scalar=share[0:rows, i, t:t + 1], in1=x,
                                                         op0=ALU.mult, op1=ALU.add).then_inc(s_add, 1)

                    @block.sync
                    def _(sp):
                        for t in range(TILES):
                            rows = P if t < TILES - 1 else LAST
                            sp.wait_ge(s_add, 2 * t + 2)
                            sp.dma_start(out[t * P:t * P + rows, :], h[0:rows, t, :]).then_inc(s_out, 16)
                        sp.wait_ge(s_out, 16 * TILES)

        l0_width, l1_width, l3_width = 3 * KT * D, 2 * KT * L1_PAD + L1_PAD // P * D, 4096

        tokens()
        with ExitStack() as st:
            q_fm, eq_fm, ek_fm = (sb(f"l0_{n}", [P, KT, Q_COLS], where=st) for n in ("q_fm", "eq_fm", "ek_fm"))
            k_fm = sb("l0_k_fm", [P, KT, PADDED], where=st)
            with ExitStack() as st2:
                v_fm = sb("l0_v_fm", [P, KT, PADDED], where=st2)
                v_tm = sb("l0_v_tm", [P, TILES, D], where=st2)
                project("l0p", "l0", plain("l0_v", v_fm, "l0_bv") + plain("l0_q", q_fm, "l0_bq")
                        + plain("l0_k", k_fm, "l0_bk") + plain("l0_eq", eq_fm, "l0_beq")
                        + plain("l0_ek", ek_fm, "l0_bek"), value_terms("l0_v"), row("l0_bv"), v_tm,
                        pads=(q_fm[:, :, TOKENS:], eq_fm[:, :, TOKENS:], ek_fm[:, :, TOKENS:], v_fm[:, :, TOKENS:]))
                mix_values(v_fm, v_tm)
            ctx_fm = sb("l0_ctx_fm", [P, KT, PADDED], where=st)
            zero_pads("l0z", ctx_fm)
            attend("l0a", ctx_fm, q_fm, k_fm, eq_fm, ek_fm, mask=const("decay"), scale=0.25)
            project_out("l0o", ctx_fm, "l0_o", row("l0_bo"), xn, (h, xn),
                        fetch_first("l0_experts", l0_width + L0_BIASES), affine=(row("l0_ln_g"), row("l0_ln_b")))
        with ExitStack() as st:
            gates = sb("l0_gates", [P, TILES, L0_E], where=st)
            at = WEIGHT_AT["l0_down_b"][0]
            experts("l0e", "l0_experts", L0_E, 2, gates,
                    lambda first: route("l0", L0_E, L0_TOP, weight("l0_router"), row("l0_rb"), gates[:, :, :],
                                        "softmax", down_b=w_sb[0:L0_E, at:at + D], first=first), clipped=True)

        recycle()
        load_next(("l2", "mla"))
        with ExitStack() as st:
            q_fm, k_fm, ctx_fm = (sb(f"l1_{n}", [P, KT, PADDED], where=st) for n in ("q_fm", "k_fm", "ctx_fm"))
            jobs = []
            for w, wr, dst in (("l1_q", "l1_qrot", q_fm), ("l1_k", "l1_krot", k_fm)):
                for (terms, _, d, _, _, _), (rterms, *_) in zip(plain(w, dst), plain(wr, dst)):
                    jobs.append((terms, rterms, d, None, const("cos1"), const("sin1")))
            project("l1p", "l1", jobs, value_terms("l1_v"), pads=(q_fm[:, :, TOKENS:], ctx_fm[:, :, TOKENS:]))
            attend_wide(ctx_fm, q_fm, k_fm, 1.0 / P)
            project_out("l1o", ctx_fm, "l1_o", None, h, (h, xn), fetch_first("l1_experts", l1_width))
        with ExitStack() as st:
            gates = sb("l1_gates", [P, TILES, L1_E], where=st)
            experts("l1e", "l1_experts", L1_E, L1_PAD // P, gates,
                    lambda first: route("l1", L1_E, 2, weight("l1_router"), None, gates[:, :, :], "softmax",
                                        first=first))

        recycle()
        load_next(("l3",))
        with ExitStack() as st:
            q_fm = sb("l2_q_fm", [P, KT, Q_COLS], where=st)
            k_fm, ctx_fm = (sb(f"l2_{n}", [P, KT, PADDED], where=st) for n in ("k_fm", "ctx_fm"))
            project("l2p", "l2", plain("l2_q", q_fm, "l2_bq") + plain("l2_k", k_fm, "l2_bk"), value_terms("l2_v"),
                    row("l2_bv"), pads=(q_fm[:, :, TOKENS:], ctx_fm[:, :, TOKENS:]))
            attend("l2a", ctx_fm, q_fm, k_fm, mask=const("sparse"), mask_op=ALU.mult, scale=0.25)
            project_out("l2o", ctx_fm, "l2_o", row("l2_bo"), h, (h, xn))
        with ExitStack() as st:
            x0n = sb("mla_x0n", [P, TILES, D], where=st)
            normalise(xn, x0n, rms=True, scale="w_ln1")
            lat = sb("mla_lat_fm", [P, PADDED], where=st)
            q_fm = sb("mla_q_fm", [P, KT, Q_COLS], where=st)
            k_fm, ctx_fm = (sb(f"mla_{n}", [P, KT, PADDED], where=st) for n in ("k_fm", "ctx_fm"))
            wl = weight("mla_lat")
            latents("mlal", lat, [(wl[:, k, :], x_fm[:, k, :]) for k in range(KT)])
            one = {n: weight(f"mla_{n}", 1)[:, 0, :] for n in ("q", "qrot", "k_lat", "v")}
            jobs = []
            for m in range(KT):
                f = slice(m * P, (m + 1) * P)
                jobs.append(([(one["q"][:, f], lat)], [(one["qrot"][:, f], lat)], q_fm[:, m, :], None,
                             const("cos2"), const("sin2")))
                jobs.append(([(one["k_lat"][:, f], lat)] + [(weight("mla_k")[:, k, f], x_fm[:, k, :]) for k in range(KT)],
                             [(weight("mla_krot")[:, k, f], x_fm[:, k, :]) for k in range(KT)], k_fm[:, m, :], None,
                             const("cos2"), const("sin2")))
            project("mlap", "mla", jobs, [(one["v"], lat)], pads=(q_fm[:, :, TOKENS:], ctx_fm[:, :, TOKENS:]))
            attend("mlaa", ctx_fm, q_fm, k_fm, mask=const("causal"), mask_op=ALU.add, scale=0.25)
            project_out("mlao", ctx_fm, "mla_o", None, xn, (xn, x0n, True, "w_ln2"),
                        fetch_first("l2_experts", l0_width))
            gates = sb("l2_gates", [P, TILES, L2_E], where=st)
            add_rows("l2h", gates)
            experts("l2e", "l2_experts", L2_E, 2, gates,
                    lambda first: route("l2", L2_E - 1, 2, weight("mla_router"), row("mla_rb", 7), gates[:, :, 1:],
                                        "sigmoid", first=first))

        recycle()
        with ExitStack() as st:
            q_fm = sb("l3_q_fm", [P, KT, Q_COLS], where=st)
            k_fm, ctx_fm = (sb(f"l3_{n}", [P, KT, PADDED], where=st) for n in ("k_fm", "ctx_fm"))
            project("l3p", "l3", plain("l3_q", q_fm, "l3_bq") + plain("l3_k", k_fm, "l3_bk"), value_terms("l3_v"),
                    row("l3_bv"), pads=(q_fm[:, :, TOKENS:], k_fm[:, :, TOKENS:], ctx_fm[:, :, TOKENS:]))
            attend_across(ctx_fm, q_fm, k_fm, 0.25)
            project_out("l3o", ctx_fm, "l3_o", row("l3_bo"), h, (h, xn), fetch_first("l3_experts", l3_width))
        chunked_experts()


def rows_of(w):
    w = np.asarray(w)
    return np.ascontiguousarray(w.reshape(-1, P, w.shape[1]).transpose(1, 0, 2)).reshape(P, -1)


def under(w, above=0, total=P):
    out = np.zeros((total, w.shape[1]), w.dtype)
    out[above:above + w.shape[0]] = w
    return out


def layout(i):
    z = np.float32
    x = np.asarray(i["x"]).reshape(IMAGES, CHANNELS, GRID, PATCH, GRID, PATCH).transpose(0, 2, 4, 3, 5, 1)
    patches = np.zeros((PADDED, PATCH_DIM), z)
    for b in range(IMAGES):
        patches[b * SEQ + 1:(b + 1) * SEQ] = x[b].reshape(GRID * GRID, PATCH_DIM)

    w = {"tok_w": rows_of(i["L0_tok_W"])}
    for n, k in (("q", "Wq"), ("k", "Wk"), ("v", "Wv"), ("eq", "Weq"), ("ek", "Wek"), ("o", "Wo")):
        w[f"l0_{n}"] = rows_of(i[f"L0_attn_{k}"].T)
    mix = np.zeros((D, 2, P), z)
    for hd in range(HEADS):
        m = i["L0_attn_mix_w"][hd].T
        c = (hd % HPT) * HD
        mix[hd * HD:(hd + 1) * HD, 0, c:c + HD] = m
        mix[hd * HD:(hd + 1) * HD, 1, c:c + HD] = np.roll(m, 1, axis=1)
    w["l0_mix"] = rows_of(mix.reshape(D, 2 * P))
    w["l0_ampph"] = rows_of(np.concatenate([i["L0_attn_amp_w"].T, i["L0_attn_ph_w"].T], 1))
    w["l0_router"] = rows_of(i["L0_ffn_router_weight"].T)
    w["l0_down_b"] = under(i["L0_ffn_down_bias"])
    swap = np.concatenate([np.arange(64, 128), np.arange(64)])
    for n, k in (("q", "wq"), ("k", "wk"), ("v", "wv")):
        m = i[f"L1_attn_{k}"]
        w[f"l1_{n}"] = rows_of(m.transpose(1, 0, 2).reshape(D, D))
        if n != "v":
            w[f"l1_{n}rot"] = rows_of(m[:, :, swap].transpose(1, 0, 2).reshape(D, D))
    w["l1_o"] = rows_of(i["L1_attn_wo"].reshape(D, D))
    w["l1_router"] = rows_of(i["L1_ffn_Wr"])
    for n, k in (("q", "Wq"), ("k", "Wk"), ("v", "Wv"), ("o", "Wo")):
        w[f"l2_{n}"] = rows_of(i[f"L2_attn_{k}"].T)
    w["mla_lat"] = rows_of(np.concatenate([i["L2_ffn_W_qd"], i["L2_ffn_W_kvd"]], 1))
    half_swap = np.concatenate([np.arange(4, 8), np.arange(4)])

    def heads(m, rope, rot=False):
        m = m.reshape(m.shape[0], HEADS, 8)
        if rot:
            m = m[:, :, half_swap]
        out = np.zeros((m.shape[0], HEADS, HD), z)
        out[:, :, 8 * rope:8 * rope + 8] = m
        return out.reshape(m.shape[0], D)

    qu, qr = heads(i["L2_ffn_W_qu"], 0), heads(i["L2_ffn_W_ropeq"], 1)
    both = np.where(np.arange(D)[None] % HD < 8, qu, qr)
    w["mla_q"] = under(both)
    w["mla_qrot"] = under(heads(i["L2_ffn_W_ropeq"], 1, True))
    w["mla_k_lat"] = under(heads(i["L2_ffn_W_ku"], 0), 64)
    w["mla_k"] = rows_of(heads(i["L2_ffn_W_ropek"], 1))
    w["mla_krot"] = rows_of(heads(i["L2_ffn_W_ropek"], 1, True))
    w["mla_v"] = under(i["L2_ffn_W_vu"], 64)
    w["mla_o"] = rows_of(i["L2_ffn_W_o"])
    w["mla_router"] = rows_of(np.concatenate([i["L2_ffn_W_router"], np.zeros((D, 1), z)], 1))
    ipw = i["L3_attn_in_proj_weight"].reshape(HEADS, 3, HD, D)
    ipb = i["L3_attn_in_proj_bias"].reshape(HEADS, 3, HD)
    for n, k in (("q", 0), ("k", 1), ("v", 2)):
        w[f"l3_{n}"] = rows_of(ipw[:, k].reshape(D, D).T)
    w["l3_o"] = rows_of(i["L3_attn_out_proj_weight"].T)
    w["l3_router"] = rows_of(i["L3_ffn_router_w"].T)
    weights = np.concatenate([w[n] for n in WEIGHT_FROM], 1)

    def cols(v):
        return np.asarray(v).reshape(-1, P).T
    c = {"ln1_g": cols(i["L0_tok_ln1_g"]), "ln1_b": cols(i["L0_tok_ln1_b"])}
    for n in ("bq", "bk", "beq", "bek", "bv"):
        c[f"l0_{n}"] = cols(i[f"L0_attn_{n}"])
    for n in ("bq", "bk"):
        c[f"l2_{n}"] = cols(i[f"L2_attn_{n}"])
    c["w_ln1"], c["w_ln2"] = cols(i["L2_ffn_w_ln1"]), cols(i["L2_ffn_w_ln2"])
    c["l3_bq"], c["l3_bk"] = cols(ipb[:, 0].reshape(-1)), cols(ipb[:, 1].reshape(-1))

    mb = i["L0_attn_mix_b"]
    mixb = np.stack([mb.reshape(2, P), np.roll(mb, 1, axis=1).reshape(2, P)], 1)
    r = {"cls": i["L0_tok_cls_token"], "cls_pos": i["L0_tok_cls_pos_embedding"], "tok_b": i["L0_tok_bias"],
         "ln2_g": i["L0_tok_ln2_g"], "ln2_b": i["L0_tok_ln2_b"], "l0_bv": i["L0_attn_bv"],
         "l0_bo": i["L0_attn_bo"], "l0_ln_g": i["L0_attn_ln_g"], "l0_ln_b": i["L0_attn_ln_b"], "l0_mixb": mixb,
         "l0_ampphb": np.concatenate([i["L0_attn_amp_b"], i["L0_attn_ph_b"]]), "l0_rb": i["L0_ffn_router_bias"],
         "l2_bv": i["L2_attn_bv"], "l2_bo": i["L2_attn_bo"],
         "mla_rb": np.concatenate([i["L2_ffn_routing_bias"], np.zeros(1, z)]), "l3_bv": ipb[:, 2],
         "l3_bo": i["L3_attn_out_proj_bias"]}

    def experts(*parts):
        return np.ascontiguousarray(np.concatenate(
            [p.reshape(p.shape[0], -1, P, p.shape[2]).transpose(0, 2, 1, 3).reshape(p.shape[0], P, -1)
             for p in parts], 2))

    gu = i["L0_ffn_gate_up_proj"]
    pad_out = ((0, 0), (0, 0), (0, L1_PAD - L1_HID))
    pad_in = ((0, 0), (0, L1_PAD - L1_HID), (0, 0))

    def with_shared(shared, routed):
        return np.concatenate([i[f"L2_ffn_{shared}"][None], i[f"L2_ffn_{routed}"]], 0)
    return {
        "patches": tiled(patches), "weights": weights,
        "cols": np.concatenate([c[n] for n in COL_AT], 1),
        "rows": np.concatenate([np.asarray(r[n]).reshape(1, -1) for n in ROW_AT], 1),
        "consts": constants(),
        "l0_experts": np.concatenate([
            experts(gu[:, :, :D], gu[:, :, D:], i["L0_ffn_down_proj"]),
            i["L0_ffn_gate_up_bias"].reshape(L0_E, L0_BIASES, P).transpose(0, 2, 1)], 2),
        "l1_experts": experts(np.pad(i["L1_ffn_W2"], pad_out), np.pad(i["L1_ffn_W1"], pad_out),
                              np.pad(i["L1_ffn_W3"], pad_in)),
        "l2_experts": experts(with_shared("Wg_s", "Wg_r"), with_shared("Wu_s", "Wu_r"), with_shared("Wd_s", "Wd_r")),
        "l3_experts": experts(i["L3_ffn_w1"], i["L3_ffn_w2"]),
    }


def kernel(**inputs):
    import concourse.bacc as bacc
    from concourse.bass_utils import run_bass_kernel_spmd

    nc = bacc.Bacc("TRN2", target_bir_lowering=False, num_devices=1)
    arrays, aps = {}, {}
    for name, v in layout({k: np.asarray(v) for k, v in inputs.items()}).items():
        arrays[f"in_{name}"] = np.ascontiguousarray(v)
        aps[name] = nc.dram_tensor(f"in_{name}", v.shape, mybir.dt.from_np(v.dtype), kind="ExternalInput").ap()
    out = nc.dram_tensor("out_dram", (TOKENS, D), F32, kind="ExternalOutput").ap()
    build(nc, aps, out)
    r = run_bass_kernel_spmd(nc, [arrays], core_ids=[0])
    return r.results[0]["out_dram"].reshape(IMAGES, SEQ, D)
```

```python
from contextlib import ExitStack

import numpy as np

import concourse.bass as bass
from concourse import mybir

F32 = mybir.dt.float32
F32R = mybir.dt.float32r
U32 = mybir.dt.uint32
ALU = mybir.AluOpType
ACT = mybir.ActivationFunctionType
AX = mybir.AxisListType

P = 128
IMAGES, SEQ, D = 16, 37, 256
GRID, PATCH, CHANNELS = 6, 16, 3
PATCH_DIM = CHANNELS * PATCH * PATCH
TOKENS = IMAGES * SEQ
TILES = -(-TOKENS // P)
PADDED = TILES * P
LAST = TOKENS - (TILES - 1) * P
HALF = TOKENS // 2
Q_COLS = PADDED + 64
KT = D // P
PK = PATCH_DIM // P
HEADS, HD = 16, 16
HPT = P // HD
EPS = 1e-5
REP = 3
BLOCKS = -(-HEADS // REP)
PAIR = 64 + SEQ

L0_E, L0_TOP, L0_ALPHA, L0_LIMIT = 16, 4, 1.702, 7.0
L0_BIASES = 4
L1_E, L1_HID, L1_PAD = 8, 352, 384
L2_E = 8
L3_E, L3_FF, L3_TOP = 8, 1024, 2
CHUNK = TOKENS * L3_TOP // L3_E
HCH = CHUNK // 2
L3_GROUPS = -(-SEQ // 4)


def offsets(parts):
    at, out = 0, {}
    for name, width in parts:
        out[name] = (at, width)
        at += width
    return out, at


WEIGHTS = {
    "tok": [("tok_w", PK * D)],
    "l0": [(n, KT * D) for n in ("l0_q", "l0_k", "l0_v", "l0_eq", "l0_ek", "l0_o", "l0_mix")]
    + [("l0_ampph", KT * 2 * HEADS), ("l0_router", KT * L0_E), ("l0_down_b", D)],
    "l1": [(n, KT * D) for n in ("l1_q", "l1_k", "l1_v", "l1_o")] + [("l1_router", KT * L1_E)],
    "l2": [(n, KT * D) for n in ("l2_q", "l2_k", "l2_v", "l2_o")],
    "mla": [("mla_lat", KT * P), ("mla_q", D), ("mla_qrot", D), ("mla_k_lat", D), ("mla_k", KT * D),
            ("mla_krot", KT * D), ("mla_v", D), ("mla_o", KT * D), ("mla_router", KT * 8)],
    "l3": [(n, KT * D) for n in ("l3_q", "l3_k", "l3_v", "l3_o")] + [("l3_router", KT * L3_E)],
}
WEIGHT_FROM, WEIGHT_COLS = offsets([p for parts in WEIGHTS.values() for p in parts])
WEIGHT_AT, FIRST_COLS = offsets(WEIGHTS["tok"] + WEIGHTS["l0"])
LATER_AT, LATER_COLS = offsets(WEIGHTS["l2"] + WEIGHTS["mla"])
FIRST_COLS = max(FIRST_COLS, LATER_COLS)
WEIGHT_AT.update(LATER_AT)
for layer in ("l1", "l3"):
    WEIGHT_AT.update({n: (FIRST_COLS + at, width) for n, (at, width) in offsets(WEIGHTS[layer])[0].items()})
WEIGHT_ROOM = FIRST_COLS + max(offsets(WEIGHTS[layer])[1] for layer in ("l1", "l3"))
COL_AT, COL_COLS = offsets([
    ("ln1_g", PK), ("ln1_b", PK), ("l0_bq", 2), ("l0_bk", 2), ("l0_beq", 2), ("l0_bek", 2), ("l0_bv", 2),
    ("l2_bq", 2), ("l2_bk", 2), ("w_ln1", 2), ("w_ln2", 2), ("l3_bq", 2), ("l3_bk", 2)])
ROW_AT, ROW_COLS = offsets([
    ("cls", D), ("cls_pos", D), ("tok_b", D), ("ln2_g", D), ("ln2_b", D), ("l0_bv", D), ("l0_bo", D),
    ("l0_ln_g", D), ("l0_ln_b", D), ("l0_mixb", 2 * D), ("l0_ampphb", 2 * HEADS), ("l0_rb", L0_E),
    ("l2_bv", D), ("l2_bo", D), ("mla_rb", 8), ("l3_bv", D), ("l3_bo", D)])
CONST_AT, CONST_COLS = offsets([
    ("ident", P), ("half", 2), ("minus_half", 2), ("ones", P), ("before", P), ("headmask", HPT), ("vmask37", HEADS), ("vmask16", HEADS),
    ("decay", SEQ), ("sparse", SEQ), ("causal", SEQ), ("cos1", SEQ), ("sin1", SEQ), ("cos2", SEQ),
    ("sin2", SEQ), ("pe", TILES * D), ("is_patch", TILES), ("is_cls", TILES), ("valid", TILES),
    ("earlier16", 256), ("earlier8", 64), ("earlier7", 49)])


FIRST_CONST = CONST_AT["ones"][0]
FIRST_ROW = ROW_AT["l0_bv"][0]


def constants():
    f = np.float32
    c = {}
    i128 = np.arange(P)
    c["ident"] = np.eye(P, dtype=f)
    c["ones"] = np.ones((P, P), f)
    c["before"] = (i128[:, None] < i128[None, :]).astype(f)
    c["headmask"] = (i128[:, None] // HD == np.arange(HPT)[None]).astype(f)
    c["vmask37"] = (i128[:, None] // SEQ == np.arange(HEADS)[None] % REP).astype(f)
    c["vmask16"] = (i128[:, None] // HD == np.arange(HEADS)[None] % HPT).astype(f)
    q = np.where(i128 % 64 < SEQ, i128 % 64, 0)
    j = np.arange(SEQ)
    c["decay"] = (f(0.5) * np.exp(f(-0.1) * np.abs(q[:, None] - j[None]).astype(f))).astype(f)
    sparse = np.zeros((SEQ, SEQ), f)
    for r in range(SEQ):
        sparse[r, r] = 1
        k = 0
        while 2 ** k <= r + 1:
            if r - 2 ** k >= 0:
                sparse[r, r - 2 ** k] = 1
            k += 1
    c["sparse"] = sparse[q]
    c["causal"] = np.where(q[:, None] >= j[None], 0, -1e30).astype(f)
    half = 64
    freq = np.power(f(10000.0), -(np.arange(half, dtype=f) / f(half))).astype(f)
    rad = (j.astype(f)[:, None] * freq[None]).astype(f)
    c["cos1"] = np.concatenate([np.cos(rad), np.cos(rad)], 1).T.astype(f)
    c["sin1"] = np.concatenate([-np.sin(rad), np.sin(rad)], 1).T.astype(f)
    inv = (f(1.0) / np.power(f(10000.0), np.arange(0, 8, 2, dtype=f) / f(8))).astype(f)
    ang = (j.astype(f)[:, None] * inv[None]).astype(f)
    cos8, sin8 = np.concatenate([np.cos(ang)] * 2, 1), np.concatenate([-np.sin(ang), np.sin(ang)], 1)
    head_cos = np.concatenate([np.ones((SEQ, 8)), cos8], 1)
    head_sin = np.concatenate([np.zeros((SEQ, 8)), sin8], 1)
    c["cos2"] = np.tile(head_cos, (1, HPT)).T.astype(f)
    c["sin2"] = np.tile(head_sin, (1, HPT)).T.astype(f)
    omega = (f(1.0) / np.power(f(10000.0), np.arange(D // 4, dtype=f) / f(D // 4 - 1))).astype(f)
    yy, xx = np.meshgrid(np.arange(GRID), np.arange(GRID), indexing="ij")
    ya, xa = yy.reshape(-1, 1) * omega[None], xx.reshape(-1, 1) * omega[None]
    pe = np.concatenate([np.sin(xa), np.cos(xa), np.sin(ya), np.cos(ya)], 1).astype(f)
    rows = np.zeros((PADDED, D), f)
    patch, cls, valid = (np.zeros(PADDED, f) for _ in range(3))
    for b in range(IMAGES):
        rows[b * SEQ + 1:(b + 1) * SEQ] = pe
        patch[b * SEQ + 1:(b + 1) * SEQ] = 1
        cls[b * SEQ] = 1
    valid[:TOKENS] = 1
    c["pe"] = tiled(rows)
    for name, v in (("is_patch", patch), ("is_cls", cls), ("valid", valid)):
        c[name] = np.ascontiguousarray(v.reshape(TILES, P).T)
    c["half"], c["minus_half"] = np.full((P, 2), 0.5, f), np.full((P, 2), -0.5, f)
    for e in (16, 8, 7):
        lower = (np.arange(e)[None] < np.arange(e)[:, None]).astype(f)
        c[f"earlier{e}"] = np.tile(lower.reshape(1, -1), (P, 1))
    return np.concatenate([c[n].reshape(P, -1) for n in CONST_AT], 1).astype(f)


def tiled(rows):
    n = rows.shape[1]
    return np.ascontiguousarray(rows.reshape(-1, P, n).transpose(1, 0, 2)).reshape(P, -1)


def ordered(eng, sem, start=0):
    count = [0]

    def signal(ins):
        ins.then_inc(sem, 1)
        count[0] += 1

    def wait():
        eng.wait_ge(sem, start + count[0])

    def link(ins):
        signal(ins)
        wait()
    return link, signal, wait, count


def spread(ap, pattern, shape, **sizes):
    return ap.rearrange(pattern, **sizes).broadcast_to(shape)


def pipeline(eng, total, late, step, first=None):
    def has(m):
        return not isinstance(m, int) or 0 <= m < total

    first = first or (2 if late <= 2 else 4)
    for n in range(first):
        step(n, n % 2, n // 2, has)
    with eng.Fori(first // 2, total // 2) as i:
        for u in range(2):
            step(i * 2 + u, u, i, has)
    for n in range(total - total % 2, total + late):
        step(n, n % 2, n // 2, has)


def build(nc, a, out):
    with ExitStack() as ctx:
        names = set()
        retired = []

        def sb(name, shape, dt=F32, where=ctx):
            return where.enter_context(nc.sbuf_tensor(name, shape, dt))

        def sem(name, where=None):
            assert name not in names
            names.add(name)
            if where is None:
                return ctx.enter_context(nc.semaphore(name))
            retired.append(nc.alloc_semaphore(name))
            return retired[-1]

        def recycle():
            nc.clear_and_free_semaphores(retired)
            del retired[:]
            nc.all_engine_barrier()

        ps = ctx.enter_context(nc.psum_tensor("ps", [P, 8, 512], F32))
        w_sb = sb("w_sb", [P, WEIGHT_ROOM])
        col_sb = sb("col_sb", [P, COL_COLS])
        row_sb = sb("row_sb", [P, ROW_COLS])
        const_sb = sb("const_sb", [P, CONST_COLS])
        h = sb("h", [P, TILES, D])
        xn = sb("xn", [P, TILES, D])
        x_fm = sb("x_fm", [P, KT, PADDED])
        v_dram = nc.dram_tensor("v_scratch", [PADDED, D], F32).ap()
        perm_dram = nc.dram_tensor("perm_scratch", [TOKENS * L3_TOP, D], F32).ap()
        y_dram = nc.dram_tensor("y_scratch", [TOKENS * L3_TOP, D], F32).ap()

        def weight(name, k=KT):
            at, width = WEIGHT_AT[name]
            return w_sb[:, at:at + width].rearrange("p (k n) -> p k n", k=k)

        def col(name, i=0, n=1):
            at = COL_AT[name][0] + i
            return col_sb[:, at:at + n]

        def row(name, n=None):
            at, width = ROW_AT[name]
            return row_sb[:, at:at + (n or width)]

        def const(name):
            at, width = CONST_AT[name]
            return const_sb[:, at:at + width]

        ident = const("ident")
        loaded = {n: sem(f"loaded_{n}") for n in [*WEIGHTS, "cols", "tok_rows", "rows", "ident", "consts"]}

        norm = {n: sem(f"norm_{n}") for n in ("chain", "var", "rstd", "normed", "turned", "copied_a", "copied_v")}
        stat_bufs = {n: (sb(f"{n}_stats", [P, TILES, 2, 6]), sb(f"{n}_mv", [P, TILES, 2]), sb(f"{n}_ve", [P, TILES]),
                         sb(f"{n}_r", [P, TILES])) for n in ("norm", "affine")}
        done = {"norms": 0, "chain": 0}
        GROUPS = ((0, 2), (2, 4), (4, TILES))

        def group_stats(dve, link, signal, wait, bufs, src, tiles, s_var, rms=False, parts=1):
            stats, mv, ve, _ = bufs
            t0, t1 = tiles
            n = src.shape[2] // parts
            for t in range(t0, t1):
                for q in range(parts):
                    signal(dve.bn_stats(stats[:, t, q, :], src[:, t, q * n:(q + 1) * n]))
            wait()
            for t in range(t0, t1):
                signal(dve.bn_aggr(mv[:, t, :], stats[:, t, 0:parts, :]))
            wait()
            ve = ve[:, t0:t1]
            if rms:
                link(dve.tensor_tensor(ve, mv[:, t0:t1, 0], mv[:, t0:t1, 0], ALU.mult))
                dve.tensor_tensor(ve, ve, mv[:, t0:t1, 1], ALU.add).then_inc(s_var, 1)
            else:
                dve.tensor_scalar(ve, mv[:, t0:t1, 1], EPS, None, ALU.add).then_inc(s_var, 1)

        def group_power(pool, bufs, tiles, root, s_rstd):
            _, _, ve, r = bufs
            t0, t1 = tiles
            power = const("half" if root else "minus_half")[:, 0:t1 - t0]
            pool.tensor_tensor(r[:, t0:t1], ve[:, t0:t1], power, ALU.pow).then_inc(s_rstd, 1)

        def norm_parts(src, dst, rms=False, scale=None):
            n = done["norms"]
            done["norms"] += 1
            bufs = stat_bufs["norm"]
            _, mv, _, r = bufs
            base = n * len(GROUPS)

            def vector(dve, ready=lambda dve, g: None):
                link, signal, wait, count = ordered(dve, norm["chain"], done["chain"])

                def scaled(g):
                    t0, t1 = GROUPS[g]
                    dve.wait_ge(norm["rstd"], base + g + 1)
                    if rms:
                        link(dve.tensor_scalar(r[:, t0:t1], r[:, t0:t1], EPS, None, ALU.add))
                        link(dve.reciprocal(r[:, t0:t1], r[:, t0:t1]))
                    for t in range(t0, t1):
                        if rms:
                            ins = dve.tensor_scalar(dst[:, t, :], src[:, t, :], r[:, t:t + 1], None, ALU.mult)
                        else:
                            ins = dve.tensor_scalar(dst[:, t, :], src[:, t, :], mv[:, t, 0:1], r[:, t:t + 1],
                                                    ALU.subtract, ALU.mult)
                        ins.then_inc(norm["normed"], 1)

                for g, tiles in enumerate(GROUPS):
                    ready(dve, g)
                    group_stats(dve, link, signal, wait, bufs, src, tiles, norm["var"], rms)
                    if g:
                        scaled(g - 1)
                scaled(len(GROUPS) - 1)
                done["chain"] += count[0]
                for part, (c0, c1) in enumerate(((0, 512), (512, PADDED))):
                    dve.wait_ge(norm["turned"], 2 * n + part + 1)
                    o, i = x_fm[:, 1, c0:c1], ps[:, 2 + part, 0:c1 - c0]
                    if scale is None:
                        dve.tensor_copy(o, i).then_inc(norm["copied_v"], 1)
                    else:
                        dve.tensor_scalar(o, i, col(scale, 1), None, ALU.mult).then_inc(norm["copied_v"], 1)

            def gpsimd(pool):
                for g, tiles in enumerate(GROUPS):
                    pool.wait_ge(norm["var"], base + g + 1)
                    group_power(pool, bufs, tiles, rms, norm["rstd"])

            def tensor(pe):
                for t in range(TILES):
                    pe.wait_ge(norm["normed"], TILES * n + t + 1)
                    for k in range(KT):
                        o = ps[:, 2 * k + t // 4, (t % 4) * P:(t % 4 + 1) * P]
                        mm = pe.transpose(o, dst[:, t, k * P:(k + 1) * P], ident)
                    if t >= 3:
                        mm.then_inc(norm["turned"], 1)

            def scalar(act):
                for part, (c0, c1) in enumerate(((0, 512), (512, PADDED))):
                    act.wait_ge(norm["turned"], 2 * n + part + 1)
                    act.activation(x_fm[:, 0, c0:c1], ps[:, part, 0:c1 - c0], ACT.Copy,
                                   scale=1.0 if scale is None else col(scale, 0)).then_inc(norm["copied_a"], 1)
            return vector, gpsimd, tensor, scalar

        def normalise(src, dst, rms=False, scale=None):
            vector, gpsimd, tensor, scalar = norm_parts(src, dst, rms, scale)
            with nc.Block() as block:
                @block.vector
                def _(dve):
                    vector(dve)

                @block.gpsimd
                def _(pool):
                    gpsimd(pool)

                @block.tensor
                def _(pe):
                    tensor(pe)

                @block.scalar
                def _(act):
                    scalar(act)

        def load(sp, layer):
            parts = WEIGHTS[layer]
            to, at = WEIGHT_AT[parts[0][0]][0], WEIGHT_FROM[parts[0][0]][0]
            width = sum(WEIGHT_FROM[parts[-1][0]]) - at
            sp.dma_start(w_sb[:, to:to + width], a["weights"][:, at:at + width]).then_inc(loaded[layer], 16)

        def load_next(layers):
            with nc.Block() as block:
                @block.sync
                def _(sp):
                    for layer in layers:
                        load(sp, layer)

        def tokens():
            with ExitStack() as st:
                pat = sb("pat", [P, TILES, PATCH_DIM], where=st)
                pat_n = sb("pat_n", [P, TILES, PATCH_DIM], where=st)
                pat_fm = sb("pat_fm", [P, PK, PADDED], where=st)
                fixed = sb("tok_fixed", [P, TILES, D], where=st)
                s_pat = [sem(f"tok_pat{t}") for t in range(TILES)]
                s_chain, s_var, s_rstd, s_normed, s_turned, s_fm, s_fm_v, s_mm, s_fix, s_var2, s_rstd2, s_gain = (
                    sem(f"tok_{n}") for n in ("chain", "var", "rstd", "normed", "turned", "fm", "fm_v", "mm", "fix",
                                              "var2", "rstd2", "gain"))
                vector, gpsimd, tensor, scalar = norm_parts(h, xn)
                ACT_K = 4

                with nc.Block() as block:
                    @block.sync
                    def _(sp):
                        for t in range(TILES):
                            sp.dma_start(pat[:, t, :], a["patches"][:, t * PATCH_DIM:(t + 1) * PATCH_DIM])\
                                .then_inc(s_pat[t], 16)
                        load(sp, "l0")
                        sp.dma_start(row_sb[:, FIRST_ROW:], a["rows"][:, FIRST_ROW:]
                                     .broadcast_to([P, ROW_COLS - FIRST_ROW])).then_inc(loaded["rows"], 16)
                        load(sp, "l1")

                    @block.scalar
                    def _(act):
                        act.dma_start(const_sb[:, 0:FIRST_CONST], a["consts"][:, 0:FIRST_CONST])\
                            .then_inc(loaded["ident"], 16)
                        act.dma_start(col_sb[:, :], a["cols"]).then_inc(loaded["cols"], 16)
                        load(act, "tok")
                        act.dma_start(row_sb[:, 0:FIRST_ROW], a["rows"][:, 0:FIRST_ROW].broadcast_to([P, FIRST_ROW]))\
                            .then_inc(loaded["tok_rows"], 16)
                        act.dma_start(const_sb[:, FIRST_CONST:], a["consts"][:, FIRST_CONST:])\
                            .then_inc(loaded["consts"], 16)
                        act.wait_ge(loaded["cols"], 16)
                        for t in range(TILES):
                            act.wait_ge(s_turned, t + 1)
                            for k in range(ACT_K):
                                act.activation(pat_fm[:, k, t * P:(t + 1) * P],
                                               ps[:, 2 * (t % 2), k * P:(k + 1) * P],
                                               ACT.Identity, scale=col("ln1_g", k), bias=col("ln1_b", k))\
                                    .then_inc(s_fm, 1)
                        scalar(act)

                    @block.gpsimd
                    def _(pool):
                        def powers(g):
                            pool.wait_ge(s_var, g + 1)
                            group_power(pool, stat_bufs["norm"], GROUPS[g], False, s_rstd)

                        pool.wait_ge(loaded["ident"], 16)
                        powers(0)
                        powers(1)
                        powers(2)
                        pool.wait_ge(loaded["tok_rows"], 16)
                        pool.tensor_tensor(row("cls"), row("cls"), row("cls_pos"), ALU.add).then_inc(s_fix, 1)
                        pool.wait_ge(loaded["consts"], 16)
                        for g, (t0, t1) in enumerate(GROUPS):
                            pool.wait_ge(s_var2, g + 1)
                            group_power(pool, stat_bufs["affine"], GROUPS[g], False, s_rstd2)
                            pool.wait_ge(s_rstd2, 2 * g + 1)
                            r = stat_bufs["affine"][3][:, t0:t1]
                            pool.tensor_tensor(r, r, const("is_patch")[:, t0:t1], ALU.mult).then_inc(s_rstd2, 1)
                        gpsimd(pool)

                    @block.tensor
                    def _(pe):
                        def turn(t):
                            if t == 0:
                                pe.wait_ge(loaded["ident"], 16)
                            pe.wait_ge(s_normed, t + 1)
                            if t >= 2:
                                pe.wait_ge(s_fm, ACT_K * (t - 1))
                                pe.wait_ge(s_fm_v, (PK - ACT_K) * (t - 1))
                            for k in range(PK):
                                o = ps[:, 2 * (t % 2) + k // ACT_K, (k % ACT_K) * P:(k % ACT_K + 1) * P]
                                mm = pe.transpose(o, pat_n[:, t, k * P:(k + 1) * P], ident)
                            mm.then_inc(s_turned, 1)

                        turn(0)
                        for t in range(TILES):
                            if t + 1 < TILES:
                                turn(t + 1)
                            if t == 0:
                                pe.wait_ge(loaded["tok"], 16)
                            pe.wait_ge(s_fm, ACT_K * (t + 1))
                            pe.wait_ge(s_fm_v, (PK - ACT_K) * (t + 1))
                            for k in range(PK):
                                mm = pe.matmul(ps[:, 4 + t // 2, (t % 2) * D:(t % 2 + 1) * D],
                                               pat_fm[:, k, t * P:(t + 1) * P], weight("tok_w", PK)[:, k, :],
                                               start=(k == 0), stop=(k == PK - 1))
                            if t % 2 or t == TILES - 1:
                                mm.then_inc(s_mm, 1)
                        tensor(pe)

                    @block.vector
                    def _(dve):
                        link, signal, wait, count = ordered(dve, s_chain)
                        _, mv, _, r = stat_bufs["norm"]

                        def normed(g):
                            dve.wait_ge(s_rstd, g + 1)
                            for t in range(*GROUPS[g]):
                                dve.tensor_scalar(pat_n[:, t, :], pat[:, t, :], mv[:, t, 0:1], r[:, t:t + 1],
                                                  ALU.subtract, ALU.mult).then_inc(s_normed, 1)

                        def copied(t):
                            dve.wait_ge(s_turned, t + 1)
                            for k in range(ACT_K, PK):
                                dve.tensor_scalar(pat_fm[:, k, t * P:(t + 1) * P],
                                                  ps[:, 2 * (t % 2) + 1, (k - ACT_K) * P:(k - ACT_K + 1) * P],
                                                  col("ln1_g", k), col("ln1_b", k), ALU.mult, ALU.add)\
                                    .then_inc(s_fm_v, 1)

                        def fix(t):
                            if t == 0:
                                dve.wait_ge(s_fix, 1)
                                dve.wait_ge(loaded["consts"], 16)
                            positions = const("pe").rearrange("p (t d) -> p t d", t=TILES)
                            for name, flag, rest in (("cls", "is_cls", positions[:, t, :]),
                                                     ("ln2_b", "is_patch", fixed[:, t, :])):
                                link(dve.scalar_tensor_tensor(out=fixed[:, t, :], in0=row(name),
                                                              scalar=const(flag)[:, t:t + 1], in1=rest,
                                                              op0=ALU.mult, op1=ALU.add))

                        def first(g):
                            affine_first(dve, link, signal, wait, h, s_mm, s_var2, row("ln2_g"),
                                         lambda t: dve.tensor_tensor(h[:, t, :],
                                                                     ps[:, 4 + t // 2, (t % 2) * D:(t % 2 + 1) * D],
                                                                     row("tok_b"), ALU.add), g)

                        for g, (t0, t1) in enumerate(GROUPS):
                            for t in range(t0, t1):
                                dve.wait_ge(s_pat[t], 16)
                            group_stats(dve, link, signal, wait, stat_bufs["norm"], pat, (t0, t1), s_var, parts=2)
                            if g == 0:
                                normed(0)
                            if g == 1:
                                dve.wait_ge(loaded["cols"], 16)
                                copied(0)
                                normed(1)
                                copied(1)
                        normed(2)
                        copied(2)
                        fix(0)
                        copied(3)
                        fix(1)
                        copied(4)
                        first(0)
                        for t in range(2, TILES):
                            fix(t)

                        def ready(dve, g):
                            if g + 1 < len(GROUPS):
                                first(g + 1)
                            wait()
                            dve.wait_ge(s_rstd2, 2 * g + 2)
                            for t in range(*GROUPS[g]):
                                signal(dve.scalar_tensor_tensor(
                                    out=h[:, t, :], in0=h[:, t, :], scalar=stat_bufs["affine"][3][:, t:t + 1],
                                    in1=fixed[:, t, :], op0=ALU.mult, op1=ALU.add))
                            wait()
                        vector(dve, ready)

        def affine_first(dve, link, signal, wait, x, s_mm, s_var, gain, value, g):
            bufs = stat_bufs["affine"]
            t0, t1 = GROUPS[g]
            dve.wait_ge(s_mm, g + 1)
            for t in range(t0, t1):
                signal(value(t))
            wait()
            group_stats(dve, link, signal, wait, bufs, x, (t0, t1), s_var)
            for t in range(t0, t1):
                if gain is not None:
                    signal(dve.scalar_tensor_tensor(out=x[:, t, :], in0=x[:, t, :], scalar=bufs[1][:, t, 0:1],
                                                    in1=gain, op0=ALU.subtract, op1=ALU.mult))

        def attend(tag, ctx_fm, q_fm, k_fm, eq_fm=None, ek_fm=None, mask=None, mask_op=None, scale=1.0):
            pairs = IMAGES // 2
            second = eq_fm is not None
            NMM = 2 if second else 1
            with ExitStack() as st:
                q_st = sb(f"{tag}_q_st", [P, 2, NMM, KT, PAIR], where=st)
                k_bd = sb(f"{tag}_k_bd", [P, 2, 2, NMM, KT, HPT, SEQ], where=st)
                v_rep = sb(f"{tag}_v_rep", [P, IMAGES, D], where=st)
                v_bd = sb(f"{tag}_v_bd", [P, 2, 2, HEADS, HD + 1], where=st)
                e_sc = sb(f"{tag}_e_sc", [P, KT, HPT, SEQ], where=st)
                shifted = sb(f"{tag}_shifted", [P, 2, HEADS, SEQ], where=st)
                top = sb(f"{tag}_top", [P, 2, HEADS], where=st)
                probs = sb(f"{tag}_probs", [P, 2, HEADS * SEQ], where=st)
                p_fm = sb(f"{tag}_p_fm", [P, 2, BLOCKS, PAIR], where=st)
                recip = sb(f"{tag}_recip", [P, 2, HEADS], where=st)
                ctx_tm = sb(f"{tag}_ctx_tm", [P, 2, HEADS, HD], where=st)
                s_vrep0, s_vrep1, s_vbd, s_stage, s_kbd, s_scores, s_shift, s_probs, s_pt, s_pfm, s_av, s_ctx, s_ct, \
                    s_ctfm, s_soft, s_norm, s_vmask, s_kbd_last = (sem(f"{tag}_{n}", st) for n in (
                        "vrep0", "vrep1", "vbd", "stage", "kbd", "scores", "shift", "probs", "pt", "pfm", "av", "ctx",
                        "ct", "ctfm", "soft", "norm", "vmask", "kbd_last"))
                s_vrep = (s_vrep0, s_vrep1)

                hm = spread(const("headmask"), "p (a h o) -> p a h o", [P, KT, HPT, SEQ], a=1, o=1)

                def block_diagonal(eng, n, u, s, m):
                    src = (k_fm, ek_fm)[m][:, :, bass.ds(n * (2 * SEQ) + s * SEQ, SEQ)]
                    return eng.tensor_tensor(k_bd[:, u, s, m, :, :, :],
                                             spread(src, "p k (o j) -> p k o j", [P, KT, HPT, SEQ], o=1), hm, ALU.mult)

                with nc.Block() as block:
                    @block.sync
                    def _(sp):
                        src = v_dram[0:TOKENS, :].rearrange("(b j) d -> j b d", j=SEQ)
                        for part, (b0, b1) in enumerate(((0, 4), (4, IMAGES))):
                            for q in range(REP):
                                sp.dma_start(v_rep[q * SEQ:(q + 1) * SEQ, b0:b1, :], src[:, b0:b1, :])\
                                    .then_inc(s_vrep[part], 16)

                    @block.gpsimd
                    def _(pool):
                        vm = const("vmask37")
                        vm = spread(vm[0:REP * SEQ], "p (h o) -> p h o", [REP * SEQ, HEADS, HD], o=1)

                        def step(n, u, r, has):
                            v = 1 - u
                            if has(n):
                                if has(n - 2):
                                    pool.wait_ge(s_scores, n * 2 - 2)
                                for m in range(NMM):
                                    for s in range(2):
                                        if (m, s) != (1, 1):
                                            block_diagonal(pool, n, u, s, m).then_inc(s_kbd, 1)
                            if isinstance(n, int) and n == 0:
                                for w in range(2):
                                    pool.tensor_copy(v_bd[:, w, :, :, HD],
                                                     spread(const("vmask37"), "p (a h) -> p a h", [P, 2, HEADS], a=1))\
                                        .then_inc(s_vmask, 1)
                                pool.wait_ge(s_vrep[0], 16 * REP)
                            if has(n - 1):
                                if has(n - 3):
                                    pool.wait_ge(s_av, n - 2)
                                for s in range(2):
                                    src = v_rep[0:REP * SEQ, bass.ds((n - 1) * 2 + s, 1), :]\
                                        .rearrange("p a (h d) -> p (a h) d", h=HEADS)
                                    pool.tensor_tensor(v_bd[0:REP * SEQ, v, s, :, 0:HD], src, vm, ALU.mult)\
                                        .then_inc(s_vbd, 1)
                            if isinstance(n, int) and n == 2:
                                pool.wait_ge(s_vrep[1], 16 * REP)
                        pipeline(pool, pairs, 3, step)

                    @block.scalar
                    def _(act):
                        act.preload_act_table(ACT.Exp)
                        act.sem_inc(s_ctfm, 1)

                        def stage(n, u):
                            for m, fm in enumerate((q_fm, eq_fm)[:NMM]):
                                act.activation(q_st[:, u, m, :, :], fm[:, :, bass.ds(n * (2 * SEQ), PAIR)],
                                               ACT.Copy).then_inc(s_stage, 1)

                        def step(n, u, r, has):
                            if isinstance(n, int) and n == 0:
                                stage(0, 0)
                            if has(n):
                                if has(n - 1):
                                    act.wait_ge(s_scores, n * 2)
                                stage(n + 1, 1 - u)
                            if has(n - 1):
                                act.wait_ge(s_pt, n)
                                act.activation(
                                    p_fm[0:REP * SEQ, 1 - u, 0:4, :],
                                    ps[0:REP * SEQ, 4, :].rearrange("p (b r) -> p b r", b=4)[:, :, 0:PAIR],
                                    ACT.Copy).then_inc(s_pfm, 1)
                                act.activation(p_fm[0:REP * SEQ, 1 - u, 4, :], ps[0:REP * SEQ, 5, 0:PAIR],
                                               ACT.Copy).then_inc(s_pfm, 1)
                                act.activation(p_fm[0:SEQ, 1 - u, 5, :], ps[0:SEQ, 5, P:P + PAIR],
                                               ACT.Copy).then_inc(s_pfm, 1)
                            if has(n - 3):
                                act.wait_ge(s_ct, n - 2)
                                src = ps[:, 7, 0:KT * P].rearrange("p (k s j) -> p k s j", k=KT, s=2)
                                dst = ctx_fm[:, :, bass.ds((n - 3) * (2 * SEQ), 2 * SEQ)]
                                act.activation(dst.rearrange("p k (s j) -> p k s j", s=2), src[:, :, :, 0:SEQ],
                                               ACT.Copy).then_inc(s_ctfm, 1)
                            if has(n):
                                act.wait_ge(s_shift, n * 2 + 2)
                                act.activation(probs[:, u, :], shifted[:, u, :, :].rearrange("p h j -> p (h j)"),
                                               ACT.Exp, scale=scale).then_inc(s_probs, 1)
                        pipeline(act, pairs, 3, step)

                    @block.tensor
                    def _(pe):
                        def scores(n, u, k, has):
                            if has(n - 1):
                                pe.wait_ge(s_shift, n * 2 + (k - 1))
                            for m in range(NMM):
                                for s in range(2):
                                    mm = pe.matmul(
                                        ps[64 * s:64 * s + 64, 2 * m + k, 0:HPT * SEQ],
                                        q_st[:, u, m, k, SEQ * s:SEQ * s + 64],
                                        k_bd[:, u, s, m, k, :, :].rearrange("p h j -> p (h j)"),
                                        start=True, stop=True)
                            mm.then_inc(s_scores, 1)

                        def step(n, u, r, has):
                            v = 1 - u
                            if has(n):
                                pe.wait_ge(s_stage, (n + 1) * NMM)
                                pe.wait_ge(s_kbd, (n + 1) * (3 if second else 2))
                                if second:
                                    pe.wait_ge(s_kbd_last, n + 1)
                                scores(n, u, 0, has)
                                scores(n, u, 1, has)
                            if has(n - 1):
                                pe.wait_ge(s_probs, n)
                                if has(n - 2):
                                    pe.wait_ge(s_pfm, n * 3 - 3)
                                for b in range(BLOCKS):
                                    w = min(REP, HEADS - REP * b) * SEQ
                                    mm = pe.transpose(ps[0:w, 4 + b // 4, (b % 4) * P:(b % 4 + 1) * P],
                                                      probs[:, v, b * REP * SEQ:b * REP * SEQ + w], ident)
                                mm.then_inc(s_pt, 1)
                            if has(n - 3):
                                pe.wait_ge(s_ctx, n - 2)
                                pe.wait_ge(s_ctfm, n - 2)
                                for k in range(KT):
                                    mm = pe.transpose(ps[:, 7, k * P:k * P + PAIR],
                                                      ctx_tm[0:PAIR, v, k * HPT:(k + 1) * HPT, :]
                                                      .rearrange("p h d -> p (h d)"), ident[0:PAIR, 0:PAIR])
                                mm.then_inc(s_ct, 1)
                            if has(n - 2):
                                pe.wait_ge(s_pfm, n * 3 - 3)
                                pe.wait_ge(s_vbd, n * 2 - 2)
                                pe.wait_ge(s_vmask, 2)
                                for s in range(2):
                                    rows = 64 if s == 0 else SEQ
                                    for b in range(BLOCKS):
                                        nh = min(REP, HEADS - REP * b)
                                        mm = pe.matmul(
                                            ps[64 * s:64 * s + rows, 6,
                                               b * REP * (HD + 1):(b * REP + nh) * (HD + 1)],
                                            p_fm[0:nh * SEQ, u, b, 64 * s:64 * s + rows],
                                            v_bd[0:nh * SEQ, u, s, b * REP:b * REP + nh, :]
                                            .rearrange("p h d -> p (h d)"),
                                            start=True, stop=True)
                                mm.then_inc(s_av, 1)
                        pipeline(pe, pairs, 3, step)

                    @block.vector
                    def _(dve):
                        links = 6 if second else 4
                        ORDER = (("mask", 0, 0), ("mask", 1, 0), ("max", 0, 1), ("max", 1, 2), ("shift", 0, 3),
                                 ("shift", 1, 4))
                        SECOND_ORDER = (("second", 0, 0), ("add", 0, 1), ("second", 1, 0), ("max", 0, 2),
                                        ("add", 1, 3), ("shift", 0, 4), ("max", 1, 5), ("shift", 1, 6))
                        mask3 = spread(mask, "p (b j) -> p b j", [P, HPT, SEQ], b=1)
                        out3 = ps[0:PAIR, 6, 0:HEADS * (HD + 1)].rearrange("p (h d) -> p h d", h=HEADS)

                        def step(n, u, r, has):
                            if second and isinstance(n, int) and n == 0:
                                block_diagonal(dve, 0, 0, 1, 1).then_inc(s_kbd_last, 1)
                            if second and has(n):
                                if has(n - 1):
                                    dve.wait_ge(s_scores, n * 2)
                                block_diagonal(dve, n + 1, 1 - u, 1, 1).then_inc(s_kbd_last, 1)
                            if has(n):
                                for op, k, after in SECOND_ORDER if second else ORDER:
                                    scores, scores2 = (ps[:, b + k, 0:HPT * SEQ].rearrange("p (h j) -> p h j", h=HPT)
                                                       for b in (0, 2))
                                    heads = slice(k * HPT, (k + 1) * HPT)
                                    if after:
                                        dve.wait_ge(s_soft, n * links + after)
                                    else:
                                        dve.wait_ge(s_scores, n * 2 + (k + 1))
                                    if op == "second":
                                        ins = dve.tensor_tensor(e_sc[:, k, :, :], scores2, mask3, ALU.mult)
                                    elif op == "add":
                                        ins = dve.tensor_tensor(scores, scores, e_sc[:, k, :, :], ALU.add)
                                    elif op == "mask":
                                        ins = dve.tensor_tensor(scores, scores, mask3, mask_op)
                                    elif op == "max":
                                        ins = dve.tensor_reduce(top[:, u, heads], scores, AX.X, ALU.max)
                                    else:
                                        ins = dve.tensor_tensor(
                                            shifted[:, u, heads, :], scores,
                                            spread(top[:, u, heads], "p (h o) -> p h o", [P, HPT, SEQ], o=1),
                                            ALU.subtract)
                                    ins.then_inc(s_shift if op == "shift" else s_soft, 1)
                            if has(n - 2):
                                dve.wait_ge(s_av, n - 1)
                                dve.reciprocal(recip[0:PAIR, u, :], out3[:, :, HD]).then_inc(s_norm, 1)
                                dve.wait_ge(s_norm, n - 1)
                                dve.tensor_tensor(ctx_tm[0:PAIR, u, :, :], out3[:, :, 0:HD],
                                                  spread(recip[0:PAIR, u, :], "p (h o) -> p h o",
                                                         [PAIR, HEADS, HD], o=1), ALU.mult).then_inc(s_ctx, 1)
                        pipeline(dve, pairs, 3, step)


        def project(tag, layer, jobs, v_terms, v_bias=None, v_tm=None, pads=(), between=None):
            rot = jobs[0][1] is not None
            swap = jobs[0][1] == "swap"
            both = rot and not swap
            slots = 2 if both else 4
            RING = 4

            def other_stage(name, eng, i):
                if between is not None and name in between:
                    between[name](eng, i)
            units = [(job, half) for job in jobs for half in range(2)]
            with ExitStack() as st:
                own_v = v_tm is None
                v_tm = v_tm if v_tm is not None else sb(f"{tag}_v_tm", [P, TILES, D], where=st)
                t1 = sb(f"{tag}_rot_a", [P, RING, HALF], where=st)
                t2 = sb(f"{tag}_rot_b", [P, RING, HALF], where=st)
                swapped = sb(f"{tag}_swapped", [P, 2, HALF], where=st) if swap else None
                s_swap = sem(f"{tag}_swap", st)
                s_unit, s_v, s_vout, s_vd, s_pads, s_t, s_sum = (
                    sem(f"{tag}_{n}", st) for n in ("unit", "v", "vout", "vd", "pads", "t", "sum"))
                s_free = [sem(f"{tag}_free{i}", st) for i in range(slots)]

                with nc.Block() as block:
                    @block.tensor
                    def _(pe):
                        pe.wait_ge(loaded[layer], 16)
                        for t in range(TILES):
                            if t >= 4:
                                pe.wait_ge(s_vout, t - 3)
                            for k, (w, src) in enumerate(v_terms):
                                mm = pe.matmul(ps[:, 4 + t % 4, 0:D], src[:, t * P:(t + 1) * P], w,
                                               start=(k == 0), stop=(k == len(v_terms) - 1))
                            mm.then_inc(s_v, 1)
                        for i, ((terms, rterms, _, _, _, _), half) in enumerate(units):
                            slot = i % slots
                            if i >= slots:
                                pe.wait_ge(s_free[slot], i // slots)
                            c0 = half * HALF
                            for b, part in enumerate((terms, rterms) if both else (terms,)):
                                for k, (w, src) in enumerate(part):
                                    mm = pe.matmul(ps[:, slot * (2 if both else 1) + b, 0:HALF], w,
                                                   src[:, c0:c0 + HALF], start=(k == 0), stop=(k == len(part) - 1))
                            mm.then_inc(s_unit, 1)
                            if between is not None and i == 3:
                                pe.wait_ge(s_vout, TILES)
                                pe.wait_ge(s_pads, len(pads))
                            other_stage("pe", pe, i)

                    @block.vector
                    def _(dve):
                        dve.wait_ge(loaded["rows"], 16)
                        for t in range(TILES):
                            dve.wait_ge(s_v, t + 1)
                            src = ps[:, 4 + t % 4, 0:D]
                            if v_bias is None:
                                dve.tensor_copy(v_tm[:, t, :], src).then_inc(s_vout, 1)
                            else:
                                dve.tensor_tensor(v_tm[:, t, :], src, v_bias, ALU.add).then_inc(s_vout, 1)
                        def turned(i, b):
                            (_, _, _, _, cos, sin), _ = units[i]
                            slot = i % slots
                            src = ps[:, slot * 2 + b, 0:HALF] if both else ps[:, slot, 0:HALF]
                            if swap and b:
                                dve.wait_ge(s_swap, 2 * (i + 1))
                                src = swapped[:, i % 2, :]
                            dve.tensor_tensor(
                                (t1, t2)[b][:, i % RING, :].rearrange("p (i j) -> p i j", j=SEQ),
                                src.rearrange("p (i j) -> p i j", j=SEQ),
                                spread((cos, sin)[b], "p (a j) -> p a j", [P, HALF // SEQ, SEQ], a=1), ALU.mult)\
                                .then_inc(s_free[slot] if b else s_t, 1)

                        for i, ((_, _, dst, bias, _, _), half) in enumerate(units):
                            slot, c0 = i % slots, half * HALF
                            if rot:
                                dve.wait_ge(s_unit, i + 1)
                                if i >= RING:
                                    dve.wait_ge(s_sum, i - RING + 1)
                                turned(i, 0)
                                if both:
                                    turned(i, 1)
                                elif i:
                                    turned(i - 1, 1)
                                if swap and i == len(units) - 1:
                                    turned(i, 1)
                            elif slot % 2:
                                dve.wait_ge(s_unit, i + 1)
                                dst, src = dst[:, c0:c0 + HALF], ps[:, slot, 0:HALF]
                                if bias is None:
                                    dve.tensor_copy(dst, src).then_inc(s_free[slot], 1)
                                else:
                                    dve.tensor_scalar(dst, src, bias, None, ALU.add).then_inc(s_free[slot], 1)
                            other_stage("dve", dve, i)

                    @block.scalar
                    def _(act):
                        if not rot:
                            for i, ((_, _, dst, bias, _, _), half) in enumerate(units):
                                slot, c0 = i % slots, half * HALF
                                if slot % 2 == 0:
                                    act.wait_ge(s_unit, i + 1)
                                    act.activation(dst[:, c0:c0 + HALF], ps[:, slot, 0:HALF], ACT.Identity,
                                                   bias=0.0 if bias is None else bias).then_inc(s_free[slot], 1)
                                other_stage("act", act, i)
                        if swap:
                            for i in range(len(units)):
                                slot = i % slots
                                act.wait_ge(s_t, i + 1)
                                if i >= 2:
                                    act.wait_ge(s_free[(i - 2) % slots], (i - 2) // slots + 1)
                                for low, high in ((0, 64), (64, 0)):
                                    act.activation(swapped[low:low + 64, i % 2, :], ps[high:high + 64, slot, 0:HALF],
                                                   ACT.Copy).then_inc(s_swap, 1)

                    @block.gpsimd
                    def _(pool):
                        for p in pads:
                            pool.memset(p, 0.0).then_inc(s_pads, 1)
                        if rot:
                            for i, ((_, _, dst, _, _, _), half) in enumerate(units):
                                c0 = half * HALF
                                pool.wait_ge(s_t, i + 1)
                                pool.wait_ge(s_free[i % slots], i // slots + 1)
                                pool.tensor_tensor(dst[:, c0:c0 + HALF], t1[:, i % RING, :], t2[:, i % RING, :],
                                                   ALU.add).then_inc(s_sum, 1)
                        for i in range(len(units)):
                            other_stage("pool", pool, i)

                    @block.sync
                    def _(sp):
                        if own_v:
                            for t in range(TILES):
                                sp.wait_ge(s_vout, t + 1)
                                sp.dma_start(v_dram[t * P:(t + 1) * P, :], v_tm[:, t, :]).then_inc(s_vd, 16)
                            sp.wait_ge(s_vd, 16 * TILES)
                        other_stage("sp", sp, 0)

        def plain(w_name, dst, bias=None):
            w = weight(w_name)
            return [([(w[:, k, m * P:(m + 1) * P], x_fm[:, k, :]) for k in range(KT)], None, dst[:, m, :],
                     None if bias is None else col(bias, m), None, None) for m in range(KT)]

        def value_terms(w_name):
            return [(weight(w_name)[:, k, :], x_fm[:, k, :]) for k in range(KT)]

        def project_out(tag, ctx_fm, w_name, bias, target, norm_args, prefetch=None, affine=None, to=None):
            two = affine is not None or to is not None
            vector, gpsimd, tensor, scalar = norm_parts(*norm_args)
            with ExitStack() as st:
                s_mm, s_add, s_bias, s_var, s_rstd, s_off = (
                    sem(f"{tag}_{n}", st) for n in ("omm", "oadd", "obias", "ovar", "orstd", "ooff"))
                with nc.Block() as block:
                    @block.tensor
                    def _(pe):
                        for t in range(TILES):
                            for k in range(KT):
                                mm = pe.matmul(ps[:, 4 + t // 2, (t % 2) * D:(t % 2 + 1) * D],
                                               ctx_fm[:, k, t * P:(t + 1) * P],
                                               weight(w_name)[:, k, :], start=(k == 0), stop=(k == KT - 1))
                            if t % 2 or t == TILES - 1:
                                mm.then_inc(s_mm, 1)
                        tensor(pe)

                    @block.scalar
                    def _(act):
                        scalar(act)

                    @block.gpsimd
                    def _(pool):
                        if bias is not None:
                            for t in range(TILES):
                                pool.tensor_tensor(target[:, t, :], target[:, t, :], bias, ALU.add)\
                                    .then_inc(s_bias, 1)
                        if affine is not None:
                            for t in range(TILES):
                                pool.tensor_tensor(h[:, t, :], h[:, t, :], affine[1], ALU.add).then_inc(s_off, 1)
                        if two:
                            for g, tiles in enumerate(GROUPS):
                                pool.wait_ge(s_var, g + 1)
                                group_power(pool, stat_bufs["affine"], tiles, False, s_rstd)
                        gpsimd(pool)

                    @block.vector
                    def _(dve):
                        link, signal, wait, count = ordered(dve, s_add)

                        def value(t):
                            if bias is not None:
                                dve.wait_ge(s_bias, t + 1)
                            return dve.tensor_tensor(target[:, t, :], ps[:, 4 + t // 2, (t % 2) * D:(t % 2 + 1) * D],
                                                     target[:, t, :], ALU.add)

                        def ready(dve, g):
                            if not two:
                                dve.wait_ge(s_mm, g + 1)
                                for t in range(*GROUPS[g]):
                                    signal(value(t))
                            else:
                                if g + 1 < len(GROUPS):
                                    first(g + 1)
                                wait()
                                dve.wait_ge(s_rstd, g + 1)
                                _, mv, _, r = stat_bufs["affine"]
                                if affine is not None:
                                    dve.wait_ge(s_off, TILES)
                                for t in range(*GROUPS[g]):
                                    if affine is not None:
                                        signal(dve.scalar_tensor_tensor(
                                            out=h[:, t, :], in0=target[:, t, :], scalar=r[:, t:t + 1],
                                            in1=h[:, t, :], op0=ALU.mult, op1=ALU.add))
                                    else:
                                        signal(dve.tensor_scalar(to[:, t, :], target[:, t, :], mv[:, t, 0:1],
                                                                 r[:, t:t + 1], ALU.subtract, ALU.mult))
                            wait()

                        def first(g):
                            affine_first(dve, link, signal, wait, target, s_mm, s_var,
                                         None if affine is None else affine[0], value, g)
                        if two:
                            first(0)
                        vector(dve, ready)

                    if prefetch is not None:
                        @block.sync
                        def _(sp):
                            prefetch(sp)

        def mix_values(st, v_fm, v_tm):
            PI = 3.1415925
            FIRST = 7
            ap_ = sb("mix_ap", [P, TILES, 2 * HEADS], where=st)
            amp = sb("mix_amp", [P, TILES, HEADS], where=st)
            ph = sb("mix_ph", [P, TILES, HEADS], where=st)
            sn = sb("mix_sin", [P, TILES, HEADS], where=st)
            hs = sb("mix_half_sin", [P, TILES, HEADS], where=st)
            coef = sb("mix_coef", [P, TILES, KT, 2, HPT], where=st)
            sup = sb("mix_sup", [P, 2, KT, 2, HPT, HD], where=st)
            s_ap, s_mm, s_chain, s_act, s_sup, s_pool, s_vd = (
                sem(f"mix_{n}", st) for n in ("ap", "mm", "chain", "act", "sup", "pool", "vd"))
            steps = {}

            def tensor(pe, i):
                if i == 3:
                    for t in range(TILES):
                        for k in range(KT):
                            mm = pe.matmul(ps[:, 4, t * 32:(t + 1) * 32], x_fm[:, k, t * P:(t + 1) * P],
                                           weight("l0_ampph")[:, k, :], start=(k == 0), stop=(k == KT - 1))
                    mm.then_inc(s_ap, 1)
                t = i - FIRST
                if 0 <= t < TILES:
                    if t >= 3:
                        pe.wait_ge(s_sup, t - 2)
                    for k in range(KT):
                        mm = pe.matmul(ps[:, 5 + t % 3, k * D:(k + 1) * D], v_fm[:, k, t * P:(t + 1) * P],
                                       weight("l0_mix")[:, k, :], start=True, stop=True)
                    mm.then_inc(s_mm, 1)

            def scalar(act, i):
                if i == 4:
                    act.wait_ge(s_chain, 1)
                    act.activation(amp[:, :, :], ap_[:, :, 0:HEADS], ACT.Sigmoid).then_inc(s_act, 1)
                    act.activation(ph[:, :, :], ap_[:, :, HEADS:], ACT.Tanh).then_inc(s_act, 1)
                    act.wait_ge(s_act, 2)
                    act.activation(sn[:, :, :], ph[:, :, :], ACT.Sin, scale=PI).then_inc(s_act, 1)
                    act.activation(hs[:, :, :], ph[:, :, :], ACT.Sin, scale=PI / 2).then_inc(s_act, 1)

            def vector(dve, i):
                if i == 3:
                    steps["chain"] = ordered(dve, s_chain)
                    link = steps["chain"][0]
                    dve.wait_ge(s_ap, 1)
                    link(dve.tensor_tensor(
                        ap_[:, :, :], ps[:, 4, 0:TILES * 32].rearrange("p (t n) -> p t n", t=TILES),
                        spread(row("l0_ampphb"), "p (a n) -> p a n", [P, TILES, 32], a=1), ALU.add))
                if i == FIRST:
                    link = steps["chain"][0]
                    dve.wait_ge(s_act, 4)
                    link(dve.tensor_tensor(hs[:, :, :], hs[:, :, :], hs[:, :, :], ALU.mult))
                    link(dve.tensor_scalar(hs[:, :, :], hs[:, :, :], -2.0, 1.0, ALU.mult, ALU.add))
                    link(dve.tensor_scalar(amp[:, :, :], amp[:, :, :], 0.3, None, ALU.mult))
                    for j, trig in enumerate((hs, sn)):
                        for k in range(KT):
                            link(dve.tensor_tensor(coef[:, :, k, j, :], amp[:, :, k * HPT:(k + 1) * HPT],
                                                   trig[:, :, k * HPT:(k + 1) * HPT], ALU.mult))
                t = i - FIRST - 1
                if 0 <= t < TILES:
                    link = steps["chain"][0]
                    bank = ps[:, 5 + t % 3, :]
                    dve.wait_ge(s_mm, t + 1)
                    if t >= 2:
                        dve.wait_ge(s_pool, 2 * (t - 1))
                    link(dve.tensor_tensor(bank, bank, row("l0_mixb"), ALU.add))
                    dve.tensor_tensor(
                        sup[:, t % 2, :, :, :, :].rearrange("p k i h d -> p (k i h) d"),
                        bank.rearrange("p (n d) -> p n d", d=HD),
                        spread(coef[:, t, :, :, :].rearrange("p k i h -> p (k i h)"), "p (n o) -> p n o",
                               [P, 2 * HEADS, HD], o=1), ALU.mult).then_inc(s_sup, 1)

            def gpsimd(pool, i):
                t = i - FIRST - 1
                if 0 <= t < TILES:
                    pool.wait_ge(s_sup, t + 1)
                    for j in range(2):
                        if j:
                            pool.wait_ge(s_pool, 2 * t + 1)
                        v = v_tm[:, t, :].rearrange("p (k n) -> p k n", k=KT)
                        pool.tensor_tensor(v, v, sup[:, t % 2, :, j, :, :].rearrange("p k h d -> p k (h d)"),
                                           ALU.add).then_inc(s_pool, 1)

            def sync(sp, i):
                for t in range(TILES):
                    sp.wait_ge(s_pool, 2 * (t + 1))
                    sp.dma_start(v_dram[t * P:(t + 1) * P, :], v_tm[:, t, :]).then_inc(s_vd, 16)
                sp.wait_ge(s_vd, 16 * TILES)
            return {"pe": tensor, "act": scalar, "dve": vector, "pool": gpsimd, "sp": sync}

        def attend_wide(ctx_fm, q_fm, k_fm, scale):
            pairs = IMAGES // 2
            units = pairs * KT
            with ExitStack() as st:
                v_img = sb("l1_v_img", [P, IMAGES, D], where=st)
                shifted = sb("l1_shifted", [P, 2, units // 2, SEQ], where=st)
                top = sb("l1_top", [P, 2, units // 2], where=st)
                total = sb("l1_total", [P, units], where=st)
                p_fm = sb("l1_p_fm", [P, units, PAIR], where=st)
                ctx_tm = sb("l1_ctx_tm", [P, pairs, D], where=st)
                s_v, s_scores, s_chain, s_probs, s_pt, s_pfm, s_av, s_ctx, s_ct, s_ctfm, s_total = (
                    sem(f"l1_{n}", st) for n in ("vimg", "scores", "chain", "probs", "pt", "pfm", "av", "ctx",
                                                 "ct", "ctfm", "total"))
                with nc.Block() as block:
                    @block.sync
                    def _(sp):
                        sp.dma_start(v_img[0:SEQ, :, :], v_dram[0:TOKENS, :].rearrange("(b j) d -> j b d", j=SEQ))\
                            .then_inc(s_v, 16)

                    @block.tensor
                    def _(pe):
                        for q in range(2):
                            for p in range(4 * q, 4 * q + 4):
                                for hd in range(KT):
                                    for s in range(2):
                                        c = (2 * p + s) * SEQ
                                        mm = pe.matmul(
                                            ps[64 * s:64 * s + 64, q, ((p % 4) * 2 + hd) * SEQ:((p % 4) * 2 + hd + 1) * SEQ],
                                            q_fm[:, hd, c:c + 64], k_fm[:, hd, c:c + SEQ], start=True, stop=True)
                            mm.then_inc(s_scores, 1)
                        for b in range(4):
                            pe.wait_ge(s_probs, b // 2 + 1)
                            for i in range(4):
                                n = 4 * b + i
                                mm = pe.transpose(ps[0:SEQ, 2 + b, i * P:(i + 1) * P],
                                                  shifted[:, n // 8, n % 8, :], ident)
                            mm.then_inc(s_pt, 1)
                        pe.wait_ge(s_v, 16)
                        for b in range(4):
                            pe.wait_ge(s_pfm, b + 1)
                            for i in range(4):
                                n = 4 * b + i
                                for s in range(2):
                                    rows = 64 if s == 0 else SEQ
                                    mm = pe.matmul(ps[64 * s:64 * s + rows, (6 + b) % 8, i * P:(i + 1) * P],
                                                   p_fm[0:SEQ, n, 64 * s:64 * s + rows],
                                                   v_img[0:SEQ, 2 * (n // 2) + s, (n % 2) * P:(n % 2 + 1) * P],
                                                   start=True, stop=True)
                            mm.then_inc(s_av, 1)
                        for b in range(4):
                            pe.wait_ge(s_ctx, b + 1)
                            for i in range(4):
                                n = 4 * b + i
                                mm = pe.transpose(ps[:, 2 + b, i * P:i * P + PAIR],
                                                  ctx_tm[0:PAIR, n // 2, (n % 2) * P:(n % 2 + 1) * P],
                                                  ident[0:PAIR, 0:PAIR])
                            mm.then_inc(s_ct, 1)

                    @block.vector
                    def _(dve):
                        link, signal, wait, count = ordered(dve, s_chain)
                        for q in range(2):
                            dve.wait_ge(s_scores, q + 1)
                            sc = ps[:, q, 0:8 * SEQ].rearrange("p (n j) -> p n j", j=SEQ)
                            link(dve.tensor_tensor(sc, sc, spread(const("causal"), "p (a j) -> p a j",
                                                                        [P, 8, SEQ], a=1), ALU.add))
                            link(dve.tensor_reduce(top[:, q, :], sc, AX.X, ALU.max))
                            signal(dve.tensor_tensor(shifted[:, q, :, :], sc,
                                                           spread(top[:, q, :], "p (n o) -> p n o", [P, 8, SEQ], o=1),
                                                           ALU.subtract))
                        for q in range(2):
                            dve.wait_ge(s_probs, q + 1)
                            signal(dve.tensor_reduce(total[:, 8 * q:8 * q + 8], shifted[:, q, :, :], AX.X, ALU.add))
                        wait()
                        link(dve.reciprocal(total[:, :], total[:, :]))
                        for b in range(4):
                            dve.wait_ge(s_av, b + 1)
                            dve.tensor_tensor(
                                ctx_tm[0:PAIR, 2 * b:2 * b + 2, :].rearrange("p a (h d) -> p (a h) d", h=KT),
                                ps[0:PAIR, (6 + b) % 8, :].rearrange("p (n d) -> p n d", n=4),
                                spread(total[0:PAIR, 4 * b:4 * b + 4], "p (n o) -> p n o", [PAIR, 4, P], o=1),
                                ALU.mult).then_inc(s_ctx, 1)

                    @block.scalar
                    def _(act):
                        for q in range(2):
                            act.wait_ge(s_chain, 3 * (q + 1))
                            act.activation(shifted[:, q, :, :], shifted[:, q, :, :], ACT.Exp, scale=scale)\
                                .then_inc(s_probs, 1)
                        for b in range(4):
                            act.wait_ge(s_pt, b + 1)
                            act.activation(p_fm[0:SEQ, 4 * b:4 * b + 4, :],
                                           ps[0:SEQ, 2 + b, :].rearrange("p (n r) -> p n r", n=4)[:, :, 0:PAIR],
                                           ACT.Copy).then_inc(s_pfm, 1)
                        for b in range(4):
                            act.wait_ge(s_ct, b + 1)
                            for p in range(2):
                                src = ps[:, 2 + b, p * 2 * P:(p + 1) * 2 * P].rearrange("p (k s j) -> p k s j", k=KT, s=2)
                                c = (2 * b + p) * 2 * SEQ
                                act.activation(ctx_fm[:, :, c:c + 2 * SEQ].rearrange("p k (s j) -> p k s j", s=2),
                                               src[:, :, :, 0:SEQ], ACT.Copy).then_inc(s_ctfm, 1)

        def attend_across(ctx_fm, q_fm, k_fm, scale):
            groups, S = L3_GROUPS, IMAGES
            tag = "l3a"
            with ExitStack() as st:
                q_st = sb(f"{tag}_q_st", [P, 2, KT, 4, 32], where=st)
                k_bd = sb(f"{tag}_k_bd", [P, 2, 4, KT, HPT, S], where=st)
                v_rep = sb(f"{tag}_v_rep", [P, 4 * groups, D], where=st)
                v_bd = sb(f"{tag}_v_bd", [P, 2, 4, HEADS, HD + 1], where=st)
                shifted = sb(f"{tag}_shifted", [P, 2, HEADS, S], where=st)
                top = sb(f"{tag}_top", [P, 2, HEADS], where=st)
                probs = sb(f"{tag}_probs", [P, 2, HEADS * S], where=st)
                p_fm = sb(f"{tag}_p_fm", [P, 2, KT, P], where=st)
                recip = sb(f"{tag}_recip", [P, 2, HEADS], where=st)
                ctx_tm = sb(f"{tag}_ctx_tm", [P, 2, HEADS, HD], where=st)
                s_vrep0, s_vrep1, s_vbd, s_stage, s_kbd, s_scores, s_shift, s_probs, s_pt, s_pfm, s_av, s_ctx, \
                    s_ct, s_ctfm, s_soft, s_norm, s_vmask, s_zero, s_vrep2 = (sem(f"{tag}_{n}", st) for n in (
                        "vrep0", "vrep1", "vbd", "stage", "kbd", "scores", "shift", "probs", "pt", "pfm", "av",
                        "ctx", "ct", "ctfm", "soft", "norm", "vmask", "zero", "vrep2"))
                s_vrep = (s_vrep0, s_vrep1, s_vrep2)

                def positions(fm, g, n=4):
                    cols = fm[:, :, bass.ds(g * 4, TOKENS)]
                    return cols.rearrange("p k (s b) -> p k b s", b=SEQ)[:, :, 0:n, :]

                with nc.Block() as block:
                    @block.sync
                    def _(sp):
                        for part, (b0, b1) in enumerate(((0, 8), (8, 16), (16, 4 * groups))):
                            src = v_dram[b0:b0 + TOKENS, :].rearrange("(s b) d -> s b d", b=SEQ)[:, 0:b1 - b0, :]
                            for q in range(HPT):
                                sp.dma_start(v_rep[q * S:(q + 1) * S, b0:b1, :], src).then_inc(s_vrep[part], 16)

                    @block.gpsimd
                    def _(pool):
                        hm = spread(const("headmask"), "p (a h o) -> p a h o", [P, KT, HPT, S], a=1, o=1)

                        def step(n, u, r, has):
                            if not has(n):
                                return
                            if has(n - 2):
                                pool.wait_ge(s_scores, n - 1)
                            for c in range(4):
                                src = k_fm[:, :, bass.ds(n * 4 + c, TOKENS)]
                                src = src.rearrange("p k (s b) -> p k b s", b=SEQ)[:, :, 0:1, :]
                                pool.tensor_tensor(k_bd[:, u, c, :, :, :], src.broadcast_to([P, KT, HPT, S]), hm,
                                                   ALU.mult).then_inc(s_kbd, 1)
                            if isinstance(n, int) and n == 0:
                                for w in range(2):
                                    pool.tensor_copy(v_bd[:, w, :, :, HD],
                                                     spread(const("vmask16"), "p (a h) -> p a h", [P, 4, HEADS], a=1))\
                                        .then_inc(s_vmask, 1)
                        pipeline(pool, groups, 0, step)

                    @block.scalar
                    def _(act):
                        act.preload_act_table(ACT.Exp)
                        act.sem_inc(s_ctfm, 1)

                        def stage(n, u):
                            act.activation(q_st[:, u, :, :, 0:S], positions(q_fm, n), ACT.Copy).then_inc(s_stage, 1)

                        def step(n, u, r, has):
                            if isinstance(n, int) and n == 0:
                                act.wait_ge(s_zero, 2)
                                stage(0, 0)
                            if has(n - 1):
                                act.wait_ge(s_pt, n)
                                act.activation(p_fm[:, 1 - u, :, :].rearrange("p k r -> p (k r)"),
                                               ps[:, 4, 0:KT * P], ACT.Copy).then_inc(s_pfm, 1)
                            if has(n) and has(n + 1):
                                if has(n - 1):
                                    act.wait_ge(s_scores, n)
                                stage(n + 1, 1 - u)
                            if has(n - 2):
                                act.wait_ge(s_ct, n - 1)
                                real = 4 if not isinstance(n, int) or n - 2 < groups - 1 else SEQ - 4 * (groups - 1)
                                src = ps[:, 7, 0:KT * P].rearrange("p (k c s) -> p k c s", k=KT, c=4)
                                act.activation(positions(ctx_fm, n - 2, real), src[:, :, 0:real, 0:S],
                                               ACT.Copy).then_inc(s_ctfm, 1)
                            if has(n):
                                act.wait_ge(s_shift, n + 1)
                                act.activation(probs[:, u, :], shifted[:, u, :, :].rearrange("p h j -> p (h j)"),
                                               ACT.Exp, scale=scale).then_inc(s_probs, 1)
                        pipeline(act, groups, 2, step)

                    @block.tensor
                    def _(pe):
                        def step(n, u, r, has):
                            v = 1 - u
                            if has(n - 1):
                                pe.wait_ge(s_probs, n)
                                if has(n - 2):
                                    pe.wait_ge(s_pfm, n - 1)
                                for k in range(KT):
                                    mm = pe.transpose(ps[:, 4, k * P:(k + 1) * P],
                                                      probs[:, v, k * P:(k + 1) * P], ident)
                                mm.then_inc(s_pt, 1)
                            if has(n):
                                pe.wait_ge(s_stage, n + 1)
                                pe.wait_ge(s_kbd, (n + 1) * 4)
                                if has(n - 1):
                                    pe.wait_ge(s_shift, n)
                                for c in range(4):
                                    for k in range(KT):
                                        mm = pe.matmul(ps[32 * c:32 * c + 32, k, 0:HPT * S], q_st[:, u, k, c, :],
                                                       k_bd[:, u, c, k, :, :].rearrange("p h j -> p (h j)"),
                                                       start=True, stop=True)
                                mm.then_inc(s_scores, 1)
                            if has(n - 2):
                                pe.wait_ge(s_ctx, n - 1)
                                pe.wait_ge(s_ctfm, n - 1)
                                for k in range(KT):
                                    mm = pe.transpose(ps[:, 7, k * P:(k + 1) * P],
                                                      ctx_tm[:, u, k * HPT:(k + 1) * HPT, :]
                                                      .rearrange("p h d -> p (h d)"), ident)
                                mm.then_inc(s_ct, 1)
                            if has(n - 1):
                                pe.wait_ge(s_pfm, n)
                                pe.wait_ge(s_vbd, n)
                                pe.wait_ge(s_vmask, 2)
                                for c in range(4):
                                    for k in range(KT):
                                        mm = pe.matmul(
                                            ps[32 * c:32 * c + 32, 6, k * HPT * (HD + 1):(k + 1) * HPT * (HD + 1)],
                                            p_fm[:, v, k, 32 * c:32 * c + 32],
                                            v_bd[:, v, c, k * HPT:(k + 1) * HPT, :].rearrange("p h d -> p (h d)"),
                                            start=True, stop=True)
                                mm.then_inc(s_av, 1)
                        pipeline(pe, groups, 2, step)

                    @block.vector
                    def _(dve):
                        scores = ps[:, 0:2, 0:HPT * S].rearrange("p k (h j) -> p k h j", h=HPT)
                        out3 = ps[:, 6, 0:HEADS * (HD + 1)].rearrange("p (h d) -> p h d", h=HEADS)
                        vm = spread(const("vmask16"), "p (a h o) -> p a h o", [P, 4, HEADS, HD], a=1, o=1)
                        for u in range(2):
                            dve.memset(q_st[:, u, :, :, :], 0.0).then_inc(s_zero, 1)

                        def step(n, u, r, has):
                            if has(n):
                                dve.wait_ge(s_scores, n + 1)
                                t3 = top[:, u, :].rearrange("p (k h) -> p k h", k=KT)
                                dve.tensor_reduce(t3, scores, AX.X, ALU.max).then_inc(s_soft, 1)
                                dve.wait_ge(s_soft, n + 1)
                                dve.tensor_tensor(shifted[:, u, :, :].rearrange("p (k h) j -> p k h j", k=KT), scores,
                                                  spread(t3, "p k (h o) -> p k h o", [P, KT, HPT, S], o=1),
                                                  ALU.subtract).then_inc(s_shift, 1)
                                if isinstance(n, int) and n == 0:
                                    dve.wait_ge(s_vrep[0], 16 * HPT)
                                if has(n - 2):
                                    dve.wait_ge(s_av, n - 1)
                                dve.tensor_tensor(v_bd[:, u, :, :, 0:HD],
                                                  v_rep[:, bass.ds(n * 4, 4), :]
                                                  .rearrange("p c (h d) -> p c h d", h=HEADS),
                                                  vm, ALU.mult).then_inc(s_vbd, 1)
                                if isinstance(n, int) and n in (1, 3):
                                    dve.wait_ge(s_vrep[(n + 1) // 2], 16 * HPT)
                            if has(n - 1):
                                dve.wait_ge(s_av, n)
                                dve.reciprocal(recip[:, u, :], out3[:, :, HD]).then_inc(s_norm, 1)
                                dve.wait_ge(s_norm, n)
                                dve.tensor_tensor(ctx_tm[:, 1 - u, :, :], out3[:, :, 0:HD],
                                                  spread(recip[:, u, :], "p (h o) -> p h o", [P, HEADS, HD], o=1),
                                                  ALU.mult).then_inc(s_ctx, 1)
                        pipeline(dve, groups, 2, step, first=4)

        def zero_pads(tag, fm):
            with ExitStack() as st:
                s_zero = sem(tag, st)
                with nc.Block() as block:
                    @block.gpsimd
                    def _(pool):
                        pool.memset(fm[:, :, TOKENS:], 0.0).then_inc(s_zero, 1)

        def latents(tag, lat, terms):
            with ExitStack() as st:
                s_mm, s_cp = sem(f"{tag}_mm", st), sem(f"{tag}_cp", st)
                with nc.Block() as block:
                    @block.tensor
                    def _(pe):
                        pe.wait_ge(loaded["mla"], 16)
                        for half in range(2):
                            for k, (w, src) in enumerate(terms):
                                mm = pe.matmul(ps[:, half, 0:HALF], w, src[:, half * HALF:(half + 1) * HALF],
                                               start=(k == 0), stop=(k == KT - 1))
                            mm.then_inc(s_mm, 1)

                    @block.scalar
                    def _(act):
                        for half in range(2):
                            act.wait_ge(s_mm, half + 1)
                            act.activation(lat[:, half * HALF:(half + 1) * HALF], ps[:, half, 0:HALF], ACT.Copy)\
                                .then_inc(s_cp, 1)

                    @block.gpsimd
                    def _(pool):
                        pool.memset(lat[:, TOKENS:], 0.0).then_inc(s_cp, 1)

        expert_w = sb("expert_w", [P, 2, 4096])
        s_w = [sem("expert_w0"), sem("expert_w1")]
        fetched = [0, 0]

        def fetch(sp, name, width, e, u):
            sp.dma_start(expert_w[:, u, 0:width], a[name][bass.ds(e, 1), :, :].rearrange("e p n -> p (e n)"))\
                .then_inc(s_w[u], 16)

        def fetch_first(name, width):
            def run(sp):
                for e in range(2):
                    fetch(sp, name, width, e, e)
            return run

        def ranks(tag, st, link, signal, dve, score, E):
            above = sb(f"{tag}_above", [P, TILES, E, E], where=st)
            same = sb(f"{tag}_same", [P, TILES, E, E], where=st)
            rank = sb(f"{tag}_rank", [P, TILES, E], where=st)
            shape = [P, TILES, E, E]
            other, own = (spread(score, pattern, shape, o=1) for pattern in ("p t (o e) -> p t o e", "p t (e o) -> p t e o"))
            earlier = spread(const(f"earlier{E}"), "p (t e f) -> p t e f", shape, t=1, f=E)
            signal(dve.tensor_tensor(above[:, :, :, :], other, own, ALU.is_gt))
            link(dve.tensor_tensor(same[:, :, :, :], other, own, ALU.is_equal))
            link(dve.tensor_tensor(same[:, :, :, :], same[:, :, :, :], earlier, ALU.mult))
            link(dve.tensor_tensor(above[:, :, :, :], above[:, :, :, :], same[:, :, :, :], ALU.add))
            link(dve.tensor_reduce(rank[:, :, :], above[:, :, :, :], AX.X, ALU.add))
            return rank

        def first_of(tag, st, link, signal, dve, score, top, fronts, s_fronts):
            E = 16
            best = sb(f"{tag}_best", [P, TILES, 8], where=st)
            above = sb(f"{tag}_above", [P, TILES, E], where=st)
            number = sb(f"{tag}_number", [P, TILES], where=st)
            for t in range(TILES):
                ins = dve.max(best[:, t, :], score[:, t, :])
                if t < TILES - 1:
                    signal(ins)
            link(ins)
            limit = spread(best[:, :, top - 1], "p (t o) -> p t o", [P, TILES, E], o=1)
            dve.wait_ge(s_fronts, 2)
            signal(dve.tensor_tensor(fronts[2][:, :, E:], score, limit, ALU.is_equal))
            signal(dve.tensor_tensor(fronts[0][:, :, E:], score, limit, ALU.is_equal))
            link(dve.tensor_tensor(above[:, :, :], score, limit, ALU.is_gt))
            signal(dve.tensor_reduce(number[:, :], above[:, :, :], AX.X, ALU.add))
            shift, src, dst = 1, fronts[0], fronts[1]
            while shift < E:
                link(dve.tensor_tensor(dst[:, :, E:], src[:, :, E:], src[:, :, E - shift:2 * E - shift], ALU.add))
                shift, src, dst = 2 * shift, dst, src
            count, equal = src[:, :, E:], fronts[2][:, :, E:]
            link(dve.tensor_tensor(count, count, spread(number[:, :], "p (t o) -> p t o", [P, TILES, E], o=1),
                                   ALU.add))
            link(dve.scalar_tensor_tensor(out=equal, in0=count, scalar=float(top), in1=equal, op0=ALU.is_le,
                                          op1=ALU.mult))
            link(dve.tensor_tensor(above[:, :, :], above[:, :, :], equal, ALU.add))
            return above

        def route(tag, E, top, router, bias, gates, kind, first):
            with ExitStack() as st:
                lg = sb(f"{tag}_lg", [P, TILES, E], where=st)
                red = sb(f"{tag}_red", [P, TILES], where=st)
                fronts = [sb(f"{tag}_front{i}", [P, TILES, 2 * E], where=st) for i in range(3)] if E == 16 else ()
                s_mm, s_chain, s_exp, s_fronts = (sem(f"{tag}_r{n}", st) for n in ("mm", "chain", "exp", "fronts"))
                red3 = spread(red[:, :], "p (t o) -> p t o", [P, TILES, E], o=1)
                width = router.shape[2]
                with nc.Block() as block:
                    @block.tensor
                    def _(pe):
                        for t in range(TILES):
                            for k in range(KT):
                                mm = pe.matmul(ps[:, 0, t * width:(t + 1) * width], x_fm[:, k, t * P:(t + 1) * P],
                                               router[:, k, :], start=(k == 0), stop=(k == KT - 1))
                        mm.then_inc(s_mm, 1)

                    @block.scalar
                    def _(act):
                        first["act"](act)
                        act.wait_ge(s_chain, 3 if kind == "softmax" else 1)
                        func = ACT.Exp if kind == "softmax" else ACT.Sigmoid
                        act.activation(lg[:, :, :], lg[:, :, :], func).then_inc(s_exp, 1)

                    @block.gpsimd
                    def _(pool):
                        for front in fronts[0:2]:
                            pool.memset(front[:, :, 0:E], 0.0).then_inc(s_fronts, 1)
                        if "gate" in first:
                            first["gate"](pool)
                        first["pool"](pool)

                    @block.vector
                    def _(dve):
                        link, signal, wait, count = ordered(dve, s_chain)
                        if "dve" in first:
                            first["dve"](dve)
                        dve.wait_ge(s_mm, 1)
                        src = ps[:, 0, 0:TILES * width].rearrange("p (t e) -> p t e", t=TILES)[:, :, 0:E]
                        if bias is None:
                            link(dve.tensor_copy(lg[:, :, :], src))
                        else:
                            link(dve.tensor_tensor(lg[:, :, :], src, spread(bias, "p (a e) -> p a e", [P, TILES, E], a=1),
                                                         ALU.add))
                        if kind == "softmax":
                            link(dve.tensor_reduce(red[:, :], lg[:, :, :], AX.X, ALU.max))
                            link(dve.tensor_tensor(lg[:, :, :], lg[:, :, :], red3, ALU.subtract))
                            dve.wait_ge(s_exp, 1)
                            link(dve.tensor_reduce(red[:, :], lg[:, :, :], AX.X, ALU.add))
                            link(dve.reciprocal(red[:, :], red[:, :]))
                            link(dve.tensor_tensor(lg[:, :, :], lg[:, :, :], red3, ALU.mult))
                        dve.wait_ge(s_exp, 1)
                        if E == 16:
                            chosen = first_of(tag, st, link, signal, dve, lg[:, :, :], top, fronts, s_fronts)
                        else:
                            chosen = ranks(tag, st, link, signal, dve, lg[:, :, :], E)
                            link(dve.tensor_scalar(chosen[:, :, :], chosen[:, :, :], float(top), None, ALU.is_lt))
                        link(dve.tensor_tensor(gates, chosen[:, :, :], lg[:, :, :], ALU.mult))
                        if kind == "sigmoid":
                            link(dve.tensor_reduce(red[:, :], gates, AX.X, ALU.add))
                            link(dve.reciprocal(red[:, :], red[:, :]))
                            link(dve.tensor_tensor(gates, gates, red3, ALU.mult))

        def experts(tag, w_in, E, mt, gates, routing, clipped=False, down_b=None):
            units = 2 * mt
            up_w, down_w = KT * mt * P, mt * D
            width = 2 * up_w + down_w
            fetch_w = width + (L0_BIASES if clipped else 0)
            base = list(fetched)
            with ExitStack() as st:
                x_hi, x_lo = (sb(f"{tag}_x_{n}", [P, KT, PADDED], F32R, where=st) for n in ("hi", "lo"))
                up_hi, up_lo = (sb(f"{tag}_up_{n}", [P, 2, 2 * up_w], F32R, where=st) for n in ("hi", "lo"))
                down_hi, down_lo = (sb(f"{tag}_down_{n}", [P, 2, down_w], F32R, where=st) for n in ("hi", "lo"))
                hid_hi, hid_lo = (sb(f"{tag}_hid_{n}", [P, 2, mt, PADDED], F32R, where=st) for n in ("hi", "lo"))
                bias_sb = sb(f"{tag}_bias_sb", [P, 2, L0_BIASES], where=st) if clipped else None
                gate_sb, up_sb, hid = (sb(f"{tag}_{n}", [P, 2, HALF], where=st) for n in ("gate_sb", "up_sb", "hid"))
                (s_pads, s_whi, s_wlo, s_up, s_gate, s_upb, s_clip, s_silu, s_hid, s_hhi, s_hlo, s_down, s_acc) = (
                    sem(f"{tag}_{n}", st) for n in ("pads", "whi", "wlo", "up", "gate", "upb", "clip", "silu", "hid",
                                                    "hhi", "hlo", "down", "acc"))

                def wa(part, u, which, k, m):
                    at = which * up_w + k * mt * P + m * P
                    return part[:, u, at:at + P]

                def up_high(act, n, u, r, has):
                    act.wait_ge(s_w[u], (r + (1 + base[u])) * 16)
                    if has(n - 2):
                        act.wait_ge(s_up, (n - 1) * units)
                    act.activation(up_hi[:, u, :], expert_w[:, u, 0:2 * up_w], ACT.Copy).then_inc(s_whi, 1)
                    if clipped:
                        act.activation(bias_sb[:, u, :], expert_w[:, u, width:width + L0_BIASES], ACT.Copy)\
                            .then_inc(s_bias, 1)

                def down_high(act, n, u, has):
                    if has(n - 2):
                        act.wait_ge(s_down, n * 3 - 3)
                    act.activation(down_hi[:, u, :], expert_w[:, u, 2 * up_w:width], ACT.Copy).then_inc(s_whi, 1)

                def up_low(pool, n, u):
                    pool.wait_ge(s_whi, 1 if isinstance(n, int) and n == 0 else 2 * n)
                    pool.tensor_tensor(up_lo[:, u, :], expert_w[:, u, 0:2 * up_w], up_hi[:, u, :].bitcast(F32),
                                       ALU.subtract).then_inc(s_wlo, 1)

                def down_low(pool, n, u, E_last):
                    pool.wait_ge(s_whi, n * 2 + (2 if E_last else 3))
                    pool.tensor_tensor(down_lo[:, u, :], expert_w[:, u, 2 * up_w:width], down_hi[:, u, :].bitcast(F32),
                                       ALU.subtract).then_inc(s_wlo, 1)

                gate_fm = sb(f"{tag}_gate_fm", [E, PADDED], where=st) if down_b is not None else None
                s_gt, s_gfm, s_db, s_dbadd = (sem(f"{tag}_{n}", st) for n in ("gt", "gfm", "db", "dbadd"))

                s_xhi, s_scaled, s_bias = (sem(f"{tag}_{n}", st) for n in ("xhi", "scaled", "bias"))

                def first_act(act):
                    for k in range(KT):
                        act.activation(x_hi[:, k, :], x_fm[:, k, :], ACT.Copy).then_inc(s_xhi, 1)
                    up_high(act, 0, 0, 0, lambda m: m == 0)

                def first_pool(pool):
                    for k in range(KT):
                        pool.wait_ge(s_xhi, k + 1)
                        pool.tensor_tensor(x_lo[:, k, :], x_fm[:, k, :], x_hi[:, k, :].bitcast(F32), ALU.subtract)\
                            .then_inc(s_pads, 1)
                    up_low(pool, 0, 0)
                routing({"act": first_act, "pool": first_pool})
                vector, gpsimd, tensor, scalar = norm_parts(h, xn)

                with nc.Block() as block:
                    @block.sync
                    def _(sp):
                        def step(n, u, r, has):
                            if has(n - 2):
                                sp.wait_ge(s_wlo, n * 2 - 1)
                                if clipped:
                                    sp.wait_ge(s_bias, n)
                                fetch(sp, w_in, fetch_w, n, u)
                        pipeline(sp, E, 0, step)

                    @block.gpsimd
                    def _(pool):
                        for part in (hid_hi, hid_lo):
                            pool.memset(part[:, :, :, TOKENS:].bitcast(F32), 0.0).then_inc(s_pads, 1)

                        def step(n, u, r, has):
                            if has(n) and not (isinstance(n, int) and n == 0):
                                up_low(pool, n, u)
                            if has(n - 1):
                                v = 1 - u
                                down_low(pool, n - 1, v, not has(n))
                                for j in range(units):
                                    m, half, slot = j // 2, j % 2, j % 2
                                    cols = slice(half * HALF, (half + 1) * HALF)
                                    pool.wait_ge(s_hhi, n * units + (j + 1 - units))
                                    pool.tensor_tensor(hid_lo[:, v, m, cols], hid[:, slot, :],
                                                       hid_hi[:, v, m, cols].bitcast(F32), ALU.subtract)\
                                        .then_inc(s_hlo, 1)
                        pipeline(pool, E, 1, step)
                        gpsimd(pool)

                    @block.tensor
                    def _(pe):
                        pe.wait_ge(s_pads, 4)
                        if down_b is not None:
                            for t in range(TILES):
                                mm = pe.transpose(ps[0:E, 4 + t // 4, (t % 4) * P:(t % 4 + 1) * P], gates[:, t, :], ident)
                            mm.then_inc(s_gt, 1)

                        def products(out, left, right, last):
                            for k in range(last + 1):
                                (lh, ll), (rh, rl) = left(k), right(k)
                                pe.matmul(out, lh, rh, start=(k == 0), stop=False)
                                pe.matmul(out, lh, rl, start=False, stop=False)
                                mm = pe.matmul(out, ll, rh, start=False, stop=(k == last))
                            return mm

                        def step(n, u, r, has):
                            if has(n):
                                pe.wait_ge(s_wlo, 1 if isinstance(n, int) and n == 0 else n * 2)
                                for j in range(units):
                                    m, half, slot = j // 2, j % 2, j % 2
                                    cols = slice(half * HALF, (half + 1) * HALF)
                                    for which in range(2):
                                        if has(n - 1) or j >= 2:
                                            if clipped:
                                                s = s_upb if which else s_gate
                                            else:
                                                s = s_hid if which else s_silu
                                            pe.wait_ge(s, n * units + (j - 1))
                                        mm = products(ps[:, 2 * slot + which, 0:HALF],
                                                      lambda k: (wa(up_hi, u, which, k, m), wa(up_lo, u, which, k, m)),
                                                      lambda k: (x_hi[:, k, cols], x_lo[:, k, cols]), KT - 1)
                                    mm.then_inc(s_up, 1)
                            if down_b is not None and isinstance(n, int) and n == 0:
                                pe.wait_ge(s_gfm, 2)
                                for t in range(TILES):
                                    pe.matmul(ps[:, 4 + t // 2, (t % 2) * D:(t % 2 + 1) * D],
                                              gate_fm[:, t * P:(t + 1) * P], down_b, start=True, stop=True)\
                                        .then_inc(s_db, 1)
                            if has(n - 1):
                                v = 1 - u
                                if down_b is not None and isinstance(n, int) and n == 1:
                                    pe.wait_ge(s_dbadd, TILES)
                                pe.wait_ge(s_hlo, n * units)
                                pe.wait_ge(s_wlo, n * 2 + 1 if has(n) else n * 2)
                                for b in range(3):
                                    if has(n - 2):
                                        pe.wait_ge(s_acc, n * 3 - 5 + b)
                                    for t in range(2 * b, min(2 * b + 2, TILES)):
                                        rows = slice(t * P, (t + 1) * P)
                                        mm = products(ps[:, 4 + b, (t % 2) * D:(t % 2 + 1) * D],
                                                      lambda m: (hid_hi[:, v, m, rows], hid_lo[:, v, m, rows]),
                                                      lambda m: (down_hi[:, v, m * D:(m + 1) * D],
                                                                 down_lo[:, v, m * D:(m + 1) * D]), mt - 1)
                                    mm.then_inc(s_down, 1)
                        pipeline(pe, E, 1, step)
                        tensor(pe)

                    @block.scalar
                    def _(act):
                        act.preload_act_table(ACT.Silu)
                        if down_b is not None:
                            act.wait_ge(s_gt, 1)
                            for b, (c0, c1) in enumerate(((0, 512), (512, PADDED))):
                                act.activation(gate_fm[:, c0:c1], ps[0:E, 4 + b, 0:c1 - c0], ACT.Copy)\
                                    .then_inc(s_gfm, 1)

                        def step(n, u, r, has):
                            if has(n) and not (isinstance(n, int) and n == 0):
                                up_high(act, n, u, r, has)
                            if has(n - 1):
                                v, e = 1 - u, n - 1
                                down_high(act, e, v, has)

                                def high(j):
                                    m, half, slot = j // 2, j % 2, j % 2
                                    act.wait_ge(s_hid, e * units + (j + 1))
                                    act.activation(hid_hi[:, v, m, half * HALF:(half + 1) * HALF], hid[:, slot, :],
                                                   ACT.Copy).then_inc(s_hhi, 1)

                                for j in range(units):
                                    m, slot = j // 2, j % 2
                                    if has(n - 2) or j >= 2:
                                        act.wait_ge(s_hid, e * units + (j - 1))
                                    if clipped:
                                        if j == 0:
                                            act.wait_ge(s_bias, n)
                                        act.wait_ge(s_up, e * units + (j + 1))
                                        act.activation(up_sb[:, slot, :], ps[:, 2 * slot + 1, 0:HALF], ACT.Identity,
                                                       bias=bias_sb[:, v, mt + m:mt + m + 1]).then_inc(s_upb, 1)
                                        act.wait_ge(s_gate, e * units + (j + 1))
                                        act.activation(gate_sb[:, slot, :], gate_sb[:, slot, :], ACT.Silu,
                                                       scale=L0_ALPHA).then_inc(s_silu, 1)
                                    else:
                                        act.wait_ge(s_up, e * units + (j + 1))
                                        act.activation(gate_sb[:, slot, :], ps[:, 2 * slot, 0:HALF], ACT.Silu)\
                                            .then_inc(s_silu, 1)
                                    if j:
                                        high(j - 1)
                                high(units - 1)
                        pipeline(act, E, 1, step)
                        scalar(act)

                    @block.vector
                    def _(dve):
                        if clipped:
                            dve.wait_ge(s_gt, 1)
                            dve.tensor_scalar(gates[:, :, :], gates[:, :, :], 1.0 / L0_ALPHA, None, ALU.mult)\
                                .then_inc(s_scaled, 1)
                            dve.wait_ge(s_scaled, 1)

                        def step(n, u, r, has):
                            if has(n):
                                def hidden(j):
                                    m, slot = j // 2, j % 2
                                    g = n * units + j
                                    dve.wait_ge(s_silu, g + 1)
                                    if has(n - 1) or j >= 2:
                                        dve.wait_ge(s_hlo, g - 1)
                                    if clipped:
                                        dve.wait_ge(s_clip, g + 1)
                                        dve.scalar_tensor_tensor(out=hid[:, slot, :], in0=up_sb[:, slot, :], scalar=1.0,
                                                                 in1=gate_sb[:, slot, :], op0=ALU.add, op1=ALU.mult)\
                                            .then_inc(s_hid, 1)
                                    else:
                                        dve.tensor_tensor(hid[:, slot, :], ps[:, 2 * slot + 1, 0:HALF],
                                                          gate_sb[:, slot, :], ALU.mult).then_inc(s_hid, 1)

                                for j in range(units):
                                    m, slot = j // 2, j % 2
                                    g = n * units + j
                                    if clipped:
                                        if j == 0:
                                            dve.wait_ge(s_bias, n + 1)
                                        dve.wait_ge(s_up, g + 1)
                                        if has(n - 1) or j >= 2:
                                            dve.wait_ge(s_hid, g - 1)
                                        dve.tensor_scalar(gate_sb[:, slot, :], ps[:, 2 * slot, 0:HALF],
                                                          bias_sb[:, u, m:m + 1], L0_LIMIT, ALU.add, ALU.min)\
                                            .then_inc(s_gate, 1)
                                        dve.wait_ge(s_upb, g + 1)
                                        dve.tensor_scalar(up_sb[:, slot, :], up_sb[:, slot, :], L0_LIMIT, -L0_LIMIT,
                                                          ALU.min, ALU.max).then_inc(s_clip, 1)
                                        if j:
                                            hidden(j - 1)
                                        if j == units - 1:
                                            hidden(j)
                                    else:
                                        hidden(j)
                            if down_b is not None and isinstance(n, int) and n == 0:
                                for t in range(TILES):
                                    dve.wait_ge(s_db, t // 2 * 2 + 2 if t < TILES - 1 else TILES)
                                    dve.tensor_tensor(h[:, t, :], ps[:, 4 + t // 2, (t % 2) * D:(t % 2 + 1) * D],
                                                      h[:, t, :], ALU.add).then_inc(s_dbadd, 1)
                                dve.wait_ge(s_dbadd, TILES)
                            if has(n - 1) and has(n):
                                for b in range(3):
                                    add(n, b, has)

                        def add(n, b, has=lambda m: True):
                            dve.wait_ge(s_down, n * 3 - 2 + b)
                            if has(n - 2):
                                dve.wait_ge(s_acc, n * 3 - 5 + b)
                            for t in range(*GROUPS[b]):
                                ins = dve.scalar_tensor_tensor(
                                    out=h[:, t, :], in0=ps[:, 4 + b, (t % 2) * D:(t % 2 + 1) * D],
                                    scalar=gates[:, t, bass.ds(n - 1, 1)], in1=h[:, t, :],
                                    op0=ALU.mult, op1=ALU.add)
                            ins.then_inc(s_acc, 1)
                        pipeline(dve, E, 1, step)

                        def ready(dve, g):
                            add(E, g)
                            dve.wait_ge(s_acc, 3 * (E - 1) + g + 1)
                        vector(dve, ready)
            fetched[0] += E // 2
            fetched[1] += E // 2

        def chunked_experts():
            E = L3_E
            base = list(fetched)
            with ExitStack() as st:
                lg = sb("l3_lg", [P, TILES, E], where=st)
                cnt = sb("l3_cnt", [P, TILES, E], where=st)
                pick = sb("l3_pick", [P, 2, TILES, E], where=st)
                tmp = sb("l3_tmp", [P, TILES, E], where=st)
                chosen = sb("l3_chosen", [P, TILES, E], where=st)
                offs = sb("l3_offs", [P, E, E], where=st)
                off = sb("l3_off", [P, E], where=st)
                tot = sb("l3_tot", [P, E], where=st)
                place = sb("l3_place", [P, 2, TILES], where=st)
                place_u = sb("l3_place_u", [P, 2, TILES], U32, where=st)
                best = sb("l3_best", [P, 2, TILES], where=st)
                share = sb("l3_share", [P, 2, TILES], where=st)
                s_mm, s_chain, s_m, s_cnt, s_e, s_idx, s_sc = (
                    sem(f"l3r_{n}", st) for n in ("mm", "chain", "m", "cnt", "e", "idx", "sc"))
                with nc.Block() as block:
                    @block.tensor
                    def _(pe):
                        router = weight("l3_router")
                        for t in range(TILES):
                            for k in range(KT):
                                mm = pe.matmul(ps[:, 0, t * E:(t + 1) * E], x_fm[:, k, t * P:(t + 1) * P],
                                               router[:, k, :], start=(k == 0), stop=(k == KT - 1))
                        mm.then_inc(s_mm, 1)
                        pe.wait_ge(s_m, 1)
                        flat = chosen[:, :, :].rearrange("p t e -> p (t e)")
                        for b, table in ((1, "before"), (2, "ones")):
                            mm = pe.matmul(ps[:, b, 0:TILES * E], const(table), flat, start=True, stop=True)
                        mm.then_inc(s_cnt, 1)

                    @block.scalar
                    def _(act):
                        act.wait_ge(s_idx, 1)
                        act.activation(share[:, 1, :], share[:, 1, :], ACT.Exp).then_inc(s_e, 1)

                    @block.vector
                    def _(dve):
                        link, signal, wait, count = ordered(dve, s_chain)
                        dve.wait_ge(s_mm, 1)
                        link(dve.tensor_copy(lg[:, :, :], ps[:, 0, 0:TILES * E].rearrange("p (t e) -> p t e", t=TILES)))
                        rank = ranks("l3", st, link, signal, dve, lg[:, :, :], E)
                        valid = spread(const("valid"), "p (t o) -> p t o", [P, TILES, E], o=1)
                        link(dve.tensor_scalar(chosen[:, :, :], rank[:, :, :], float(L3_TOP), None, ALU.is_lt))
                        link(dve.tensor_tensor(chosen[:, :, :], chosen[:, :, :], valid, ALU.mult))
                        dve.sem_inc(s_m, 1)
                        for i in range(2):
                            link(dve.tensor_scalar(pick[:, i, :, :], rank[:, :, :], float(i), None, ALU.is_equal))
                            link(dve.tensor_tensor(tmp[:, :, :], pick[:, i, :, :], lg[:, :, :], ALU.mult))
                            link(dve.tensor_reduce(best[:, i, :], tmp[:, :, :], AX.X, ALU.add))
                        link(dve.tensor_tensor(share[:, 1, :], best[:, 1, :], best[:, 0, :], ALU.subtract))
                        dve.sem_inc(s_idx, 1)
                        dve.wait_ge(s_e, 1)
                        link(dve.tensor_scalar(share[:, 0, :], share[:, 1, :], 1.0, None, ALU.add))
                        link(dve.reciprocal(share[:, 0, :], share[:, 0, :]))
                        link(dve.tensor_tensor(share[:, 1, :], share[:, 1, :], share[:, 0, :], ALU.mult))
                        dve.wait_ge(s_cnt, 1)
                        link(dve.tensor_copy(cnt[:, :, :], ps[:, 1, 0:TILES * E].rearrange("p (t e) -> p t e", t=TILES)))
                        link(dve.tensor_copy(tot[:, :], ps[:, 2, 0:E]))
                        for t in range(1, TILES):
                            link(dve.tensor_tensor(cnt[:, t, :], cnt[:, t, :], tot[:, :], ALU.add))
                            link(dve.tensor_tensor(tot[:, :], ps[:, 2, t * E:(t + 1) * E], tot[:, :], ALU.add))
                        link(dve.tensor_tensor(offs[:, :, :], spread(tot[:, :], "p (o e) -> p o e", [P, E, E], o=1),
                                                     const("earlier8").rearrange("p (e f) -> p e f", e=E), ALU.mult))
                        link(dve.tensor_reduce(off[:, :], offs[:, :, :], AX.X, ALU.add))
                        link(dve.tensor_tensor(cnt[:, :, :], cnt[:, :, :],
                                                     spread(off[:, :], "p (o e) -> p o e", [P, TILES, E], o=1), ALU.add))
                        for i in range(2):
                            link(dve.tensor_tensor(tmp[:, :, :], pick[:, i, :, :], cnt[:, :, :], ALU.mult))
                            link(dve.tensor_reduce(place[:, i, :], tmp[:, :, :], AX.X, ALU.add))
                            link(dve.tensor_copy(place_u[:, i, :], place[:, i, :]))
                        dve.sem_inc(s_idx, 1)

                    @block.gpsimd
                    def _(pool):
                        pool.wait_ge(s_idx, 2)
                        for t in range(TILES):
                            rows = P if t < TILES - 1 else LAST
                            for i in range(2):
                                pool.indirect_dma_start(
                                    perm_dram, bass.IndirectOffsetOnAxis(ap=place_u[0:rows, i, t:t + 1], axis=0),
                                    xn[0:rows, t, :], None).then_inc(s_sc, 16)
                        pool.wait_ge(s_sc, 16 * 2 * TILES)

                width = KT * L3_FF + L3_FF // P * D
                MT = L3_FF // P
                xp_tm = sb("l3_xp_tm", [HCH, 2, 2, D], where=st)
                xp_fm = sb("l3_xp_fm", [P, 2, KT, CHUNK], where=st)
                hid = sb("l3_hid", [P, 2, MT, CHUNK], where=st)
                y_fm = sb("l3_y_fm", [P, 2, KT, CHUNK], where=st)
                y_tm = sb("l3_y_tm", [HCH, 2, 2, D], where=st)
                s_x = [sem(f"l3c_x{u}", st) for u in range(2)]
                s_y = [sem(f"l3c_y{u}", st) for u in range(2)]
                s_xt, s_xfm, s_up, s_hid, s_down, s_yfm, s_yt, s_ytm = (
                    sem(f"l3c_{n}", st) for n in ("xt", "xfm", "up", "hid", "down", "yfm", "yt", "ytm"))

                def chunk_rows(dram, n):
                    return dram[bass.ds(n * CHUNK, CHUNK), :].rearrange("(q p) d -> p q d", q=2)

                with nc.Block() as block:
                    @block.sync
                    def _(sp):
                        def step(n, u, r, has):
                            if has(n):
                                if has(n - 2):
                                    sp.wait_ge(s_xt, n - 1)
                                sp.dma_start(xp_tm[:, u, :, :], chunk_rows(perm_dram, n)).then_inc(s_x[u], 16)
                            if has(n) and has(n - 2):
                                sp.wait_ge(s_down, n * 2 - 2)
                                fetch(sp, "l3_experts", width, n, u)
                            if has(n - 2):
                                sp.wait_ge(s_ytm, n)
                                sp.dma_start(chunk_rows(y_dram, n - 2), y_tm[:, u, :, :]).then_inc(s_y[u], 16)
                        for u in range(2):
                            sp.sem_inc(s_y[u], 16)
                        pipeline(sp, E, 2, step)
                        for u in range(2):
                            sp.wait_ge(s_y[u], 16 * (E // 2 + 1))

                    @block.tensor
                    def _(pe):
                        def step(n, u, r, has):
                            v = 1 - u
                            if has(n - 1):
                                pe.wait_ge(s_w[v], (r + base[v] + (1 if v == 0 else 0)) * 16)
                                pe.wait_ge(s_xfm, n)
                                for j in range(MT // 2):
                                    if has(n - 2):
                                        pe.wait_ge(s_hid, n * 4 - 7 + j)
                                    for i in range(2):
                                        for k in range(KT):
                                            at = k * L3_FF + (2 * j + i) * P
                                            mm = pe.matmul(ps[:, 1 + j, i * CHUNK:(i + 1) * CHUNK],
                                                           expert_w[:, v, at:at + P], xp_fm[:, v, k, :],
                                                           start=(k == 0), stop=(k == KT - 1))
                                    mm.then_inc(s_up, 1)
                            if has(n):
                                pe.wait_ge(s_x[u], (r + 1) * 16)
                                if has(n - 1):
                                    pe.wait_ge(s_xfm, n)
                                for k in range(KT):
                                    for q in range(2):
                                        mm = pe.transpose(ps[:, 0, k * CHUNK + q * HCH:k * CHUNK + (q + 1) * HCH],
                                                          xp_tm[:, u, q, k * P:(k + 1) * P], ident[0:HCH, 0:HCH])
                                mm.then_inc(s_xt, 1)
                            if has(n - 2):
                                pe.wait_ge(s_yfm, n * 2 - 2)
                                pe.wait_ge(s_ytm, n - 1)
                                for q in range(2):
                                    for m in range(KT):
                                        mm = pe.transpose(ps[0:HCH, 7, q * D + m * P:q * D + (m + 1) * P],
                                                          y_fm[:, u, m, q * HCH:(q + 1) * HCH], ident)
                                mm.then_inc(s_yt, 1)
                            if has(n - 1):
                                for m in range(KT):
                                    if has(n - 2):
                                        pe.wait_ge(s_yfm, n * 2 - 3 + m)
                                    for k in range(MT):
                                        if m == 0 and k % 2 == 0:
                                            pe.wait_ge(s_hid, n * 4 - 3 + k // 2)
                                        at = KT * L3_FF + k * D + m * P
                                        mm = pe.matmul(ps[:, 5 + m, 0:CHUNK], expert_w[:, v, at:at + P],
                                                       hid[:, v, k, :], start=(k == 0), stop=(k == MT - 1))
                                    mm.then_inc(s_down, 1)
                        pipeline(pe, E, 2, step)

                    @block.scalar
                    def _(act):
                        act.preload_act_table(ACT.Gelu)

                        def step(n, u, r, has):
                            if has(n - 1):
                                for j in range(MT // 2):
                                    act.wait_ge(s_up, n * 4 - 3 + j)
                                    act.activation(hid[:, 1 - u, 2 * j:2 * j + 2, :].rearrange("p i c -> p (i c)"),
                                                   ps[:, 1 + j, 0:2 * CHUNK], ACT.Gelu).then_inc(s_hid, 1)
                        pipeline(act, E, 1, step)

                    @block.vector
                    def _(dve):
                        dve.sem_inc(s_ytm, 1)

                        def step(n, u, r, has):
                            if has(n):
                                dve.wait_ge(s_xt, n + 1)
                                dve.tensor_copy(xp_fm[:, u, :, :].rearrange("p k c -> p (k c)"), ps[:, 0, 0:KT * CHUNK])\
                                    .then_inc(s_xfm, 1)
                            if has(n - 2):
                                dve.wait_ge(s_yt, n - 1)
                                dve.wait_ge(s_y[u], r * 16)
                                dve.tensor_copy(y_tm[:, u, :, :].rearrange("p q d -> p (q d)"), ps[0:HCH, 7, :])\
                                    .then_inc(s_ytm, 1)
                            if has(n - 1):
                                for m in range(KT):
                                    dve.wait_ge(s_down, n * 2 - 1 + m)
                                    dve.tensor_copy(y_fm[:, 1 - u, m, :], ps[:, 5 + m, 0:CHUNK]).then_inc(s_yfm, 1)
                        pipeline(dve, E, 2, step)

                back = sb("l3_back", [P, 2, TILES, D], where=st)
                s_back = [sem(f"l3b_back{t}", st) for t in range(TILES)]
                s_add, s_out = sem("l3b_add", st), sem("l3b_out", st)
                with nc.Block() as block:
                    @block.gpsimd
                    def _(pool):
                        for t in range(TILES):
                            rows = P if t < TILES - 1 else LAST
                            for i in range(2):
                                pool.indirect_dma_start(
                                    back[0:rows, i, t, :], None, y_dram,
                                    bass.IndirectOffsetOnAxis(ap=place_u[0:rows, i, t:t + 1], axis=0))\
                                    .then_inc(s_back[t], 16)

                    @block.vector
                    def _(dve):
                        for t in range(TILES):
                            rows = P if t < TILES - 1 else LAST
                            dve.wait_ge(s_back[t], 32)
                            for i in range(2):
                                if i:
                                    dve.wait_ge(s_add, 2 * t + 1)
                                x = h[0:rows, t, :]
                                dve.scalar_tensor_tensor(out=x, in0=back[0:rows, i, t, :],
                                                         scalar=share[0:rows, i, t:t + 1], in1=x,
                                                         op0=ALU.mult, op1=ALU.add).then_inc(s_add, 1)

                    @block.sync
                    def _(sp):
                        for t in range(TILES):
                            rows = P if t < TILES - 1 else LAST
                            sp.wait_ge(s_add, 2 * t + 2)
                            sp.dma_start(out[t * P:t * P + rows, :], h[0:rows, t, :]).then_inc(s_out, 16)
                        sp.wait_ge(s_out, 16 * TILES)

        l0_width, l1_width, l3_width = 3 * KT * D, 2 * KT * L1_PAD + L1_PAD // P * D, 4096

        tokens()
        with ExitStack() as st:
            q_fm, eq_fm, ek_fm = (sb(f"l0_{n}", [P, KT, Q_COLS], where=st) for n in ("q_fm", "eq_fm", "ek_fm"))
            k_fm = sb("l0_k_fm", [P, KT, PADDED], where=st)
            with ExitStack() as st2:
                v_fm = sb("l0_v_fm", [P, KT, PADDED], where=st2)
                v_tm = sb("l0_v_tm", [P, TILES, D], where=st2)
                mixing = mix_values(st2, v_fm, v_tm)
                project("l0p", "l0", plain("l0_v", v_fm, "l0_bv") + plain("l0_q", q_fm, "l0_bq")
                        + plain("l0_k", k_fm, "l0_bk") + plain("l0_eq", eq_fm, "l0_beq")
                        + plain("l0_ek", ek_fm, "l0_bek"), value_terms("l0_v"), row("l0_bv"), v_tm,
                        pads=(q_fm[:, :, TOKENS:], eq_fm[:, :, TOKENS:], ek_fm[:, :, TOKENS:], v_fm[:, :, TOKENS:]), between=mixing)
            ctx_fm = sb("l0_ctx_fm", [P, KT, PADDED], where=st)
            zero_pads("l0z", ctx_fm)
            attend("l0a", ctx_fm, q_fm, k_fm, eq_fm, ek_fm, mask=const("decay"), scale=0.25)
            project_out("l0o", ctx_fm, "l0_o", row("l0_bo"), xn, (h, xn),
                        fetch_first("l0_experts", l0_width + L0_BIASES), affine=(row("l0_ln_g"), row("l0_ln_b")))
        with ExitStack() as st:
            gates = sb("l0_gates", [P, TILES, L0_E], where=st)
            at = WEIGHT_AT["l0_down_b"][0]
            experts("l0e", "l0_experts", L0_E, 2, gates,
                    lambda first: route("l0", L0_E, L0_TOP, weight("l0_router"), row("l0_rb"), gates[:, :, :],
                                        "softmax", first), clipped=True, down_b=w_sb[0:L0_E, at:at + D])

        recycle()
        load_next(("l2", "mla"))
        with ExitStack() as st:
            q_fm, k_fm, ctx_fm = (sb(f"l1_{n}", [P, KT, PADDED], where=st) for n in ("q_fm", "k_fm", "ctx_fm"))
            jobs = []
            for w, dst in (("l1_q", q_fm), ("l1_k", k_fm)):
                for terms, _, d, _, _, _ in plain(w, dst):
                    jobs.append((terms, "swap", d, None, const("cos1"), const("sin1")))
            project("l1p", "l1", jobs, value_terms("l1_v"), pads=(q_fm[:, :, TOKENS:], ctx_fm[:, :, TOKENS:]))
            attend_wide(ctx_fm, q_fm, k_fm, 1.0 / P)
            project_out("l1o", ctx_fm, "l1_o", None, h, (h, xn), fetch_first("l1_experts", l1_width))
        with ExitStack() as st:
            gates = sb("l1_gates", [P, TILES, L1_E], where=st)
            experts("l1e", "l1_experts", L1_E, L1_PAD // P, gates,
                    lambda first: route("l1", L1_E, 2, weight("l1_router"), None, gates[:, :, :], "softmax",
                                        first))

        recycle()
        load_next(("l3",))
        st0 = ExitStack()
        x0n = sb("mla_x0n", [P, TILES, D], where=st0)
        with ExitStack() as st:
            q_fm = sb("l2_q_fm", [P, KT, Q_COLS], where=st)
            k_fm, ctx_fm = (sb(f"l2_{n}", [P, KT, PADDED], where=st) for n in ("k_fm", "ctx_fm"))
            project("l2p", "l2", plain("l2_q", q_fm, "l2_bq") + plain("l2_k", k_fm, "l2_bk"), value_terms("l2_v"),
                    row("l2_bv"), pads=(q_fm[:, :, TOKENS:], ctx_fm[:, :, TOKENS:]))
            attend("l2a", ctx_fm, q_fm, k_fm, mask=const("sparse"), mask_op=ALU.mult, scale=0.25)
            project_out("l2o", ctx_fm, "l2_o", row("l2_bo"), h, (xn, x0n, True, "w_ln1"), to=xn)
        with ExitStack() as st:
            lat = sb("mla_lat_fm", [P, PADDED], where=st)
            q_fm = sb("mla_q_fm", [P, KT, Q_COLS], where=st)
            k_fm, ctx_fm = (sb(f"mla_{n}", [P, KT, PADDED], where=st) for n in ("k_fm", "ctx_fm"))
            wl = weight("mla_lat")
            latents("mlal", lat, [(wl[:, k, :], x_fm[:, k, :]) for k in range(KT)])
            one = {n: weight(f"mla_{n}", 1)[:, 0, :] for n in ("q", "qrot", "k_lat", "v")}
            jobs = []
            for m in range(KT):
                f = slice(m * P, (m + 1) * P)
                jobs.append(([(one["q"][:, f], lat)], [(one["qrot"][:, f], lat)], q_fm[:, m, :], None,
                             const("cos2"), const("sin2")))
                jobs.append(([(one["k_lat"][:, f], lat)] + [(weight("mla_k")[:, k, f], x_fm[:, k, :]) for k in range(KT)],
                             [(weight("mla_krot")[:, k, f], x_fm[:, k, :]) for k in range(KT)], k_fm[:, m, :], None,
                             const("cos2"), const("sin2")))
            project("mlap", "mla", jobs, [(one["v"], lat)], pads=(q_fm[:, :, TOKENS:], ctx_fm[:, :, TOKENS:]))
            attend("mlaa", ctx_fm, q_fm, k_fm, mask=const("causal"), mask_op=ALU.add, scale=0.25)
            project_out("mlao", ctx_fm, "mla_o", None, xn, (xn, x0n, True, "w_ln2"),
                        fetch_first("l2_experts", l0_width))
            gates = sb("l2_gates", [P, TILES, L2_E], where=st)
            s_h = sem("l2_h", st)

            def add_h(dve):
                for t in range(TILES):
                    dve.tensor_tensor(h[:, t, :], h[:, t, :], xn[:, t, :], ALU.add).then_inc(s_h, 1)

            def shared_gate(pool):
                pool.memset(gates[:, :, 0:1], 1.0).then_inc(s_h, 1)
            experts("l2e", "l2_experts", L2_E, 2, gates,
                    lambda first: route("l2", L2_E - 1, 2, weight("mla_router"), row("mla_rb", 7), gates[:, :, 1:],
                                        "sigmoid", {**first, "dve": add_h, "gate": shared_gate}))
        st0.close()

        recycle()
        with ExitStack() as st:
            q_fm = sb("l3_q_fm", [P, KT, Q_COLS], where=st)
            k_fm, ctx_fm = (sb(f"l3_{n}", [P, KT, PADDED], where=st) for n in ("k_fm", "ctx_fm"))
            project("l3p", "l3", plain("l3_q", q_fm, "l3_bq") + plain("l3_k", k_fm, "l3_bk"), value_terms("l3_v"),
                    row("l3_bv"), pads=(q_fm[:, :, TOKENS:], k_fm[:, :, TOKENS:], ctx_fm[:, :, TOKENS:]))
            attend_across(ctx_fm, q_fm, k_fm, 0.25)
            project_out("l3o", ctx_fm, "l3_o", row("l3_bo"), h, (h, xn), fetch_first("l3_experts", l3_width))
        chunked_experts()


def rows_of(w):
    w = np.asarray(w)
    return np.ascontiguousarray(w.reshape(-1, P, w.shape[1]).transpose(1, 0, 2)).reshape(P, -1)


def under(w, above=0, total=P):
    out = np.zeros((total, w.shape[1]), w.dtype)
    out[above:above + w.shape[0]] = w
    return out


def layout(i):
    z = np.float32
    x = np.asarray(i["x"]).reshape(IMAGES, CHANNELS, GRID, PATCH, GRID, PATCH).transpose(0, 2, 4, 3, 5, 1)
    patches = np.zeros((PADDED, PATCH_DIM), z)
    for b in range(IMAGES):
        patches[b * SEQ + 1:(b + 1) * SEQ] = x[b].reshape(GRID * GRID, PATCH_DIM)

    w = {"tok_w": rows_of(i["L0_tok_W"])}
    for n, k in (("q", "Wq"), ("k", "Wk"), ("v", "Wv"), ("eq", "Weq"), ("ek", "Wek"), ("o", "Wo")):
        w[f"l0_{n}"] = rows_of(i[f"L0_attn_{k}"].T)
    mix = np.zeros((D, 2, P), z)
    for hd in range(HEADS):
        m = i["L0_attn_mix_w"][hd].T
        c = (hd % HPT) * HD
        mix[hd * HD:(hd + 1) * HD, 0, c:c + HD] = m
        mix[hd * HD:(hd + 1) * HD, 1, c:c + HD] = np.roll(m, 1, axis=1)
    w["l0_mix"] = rows_of(mix.reshape(D, 2 * P))
    w["l0_ampph"] = rows_of(np.concatenate([i["L0_attn_amp_w"].T, i["L0_attn_ph_w"].T], 1))
    w["l0_router"] = rows_of(i["L0_ffn_router_weight"].T)
    w["l0_down_b"] = under(i["L0_ffn_down_bias"])
    for n, k in (("q", "wq"), ("k", "wk"), ("v", "wv")):
        m = i[f"L1_attn_{k}"]
        w[f"l1_{n}"] = rows_of(m.transpose(1, 0, 2).reshape(D, D))
    w["l1_o"] = rows_of(i["L1_attn_wo"].reshape(D, D))
    w["l1_router"] = rows_of(i["L1_ffn_Wr"])
    for n, k in (("q", "Wq"), ("k", "Wk"), ("v", "Wv"), ("o", "Wo")):
        w[f"l2_{n}"] = rows_of(i[f"L2_attn_{k}"].T)
    w["mla_lat"] = rows_of(np.concatenate([i["L2_ffn_W_qd"], i["L2_ffn_W_kvd"]], 1))
    half_swap = np.concatenate([np.arange(4, 8), np.arange(4)])

    def heads(m, rope, rot=False):
        m = m.reshape(m.shape[0], HEADS, 8)
        if rot:
            m = m[:, :, half_swap]
        out = np.zeros((m.shape[0], HEADS, HD), z)
        out[:, :, 8 * rope:8 * rope + 8] = m
        return out.reshape(m.shape[0], D)

    qu, qr = heads(i["L2_ffn_W_qu"], 0), heads(i["L2_ffn_W_ropeq"], 1)
    both = np.where(np.arange(D)[None] % HD < 8, qu, qr)
    w["mla_q"] = under(both)
    w["mla_qrot"] = under(heads(i["L2_ffn_W_ropeq"], 1, True))
    w["mla_k_lat"] = under(heads(i["L2_ffn_W_ku"], 0), 64)
    w["mla_k"] = rows_of(heads(i["L2_ffn_W_ropek"], 1))
    w["mla_krot"] = rows_of(heads(i["L2_ffn_W_ropek"], 1, True))
    w["mla_v"] = under(i["L2_ffn_W_vu"], 64)
    w["mla_o"] = rows_of(i["L2_ffn_W_o"])
    w["mla_router"] = rows_of(np.concatenate([i["L2_ffn_W_router"], np.zeros((D, 1), z)], 1))
    ipw = i["L3_attn_in_proj_weight"].reshape(HEADS, 3, HD, D)
    ipb = i["L3_attn_in_proj_bias"].reshape(HEADS, 3, HD)
    for n, k in (("q", 0), ("k", 1), ("v", 2)):
        w[f"l3_{n}"] = rows_of(ipw[:, k].reshape(D, D).T)
    w["l3_o"] = rows_of(i["L3_attn_out_proj_weight"].T)
    w["l3_router"] = rows_of(i["L3_ffn_router_w"].T)
    weights = np.concatenate([w[n] for n in WEIGHT_FROM], 1)

    def cols(v):
        return np.asarray(v).reshape(-1, P).T
    c = {"ln1_g": cols(i["L0_tok_ln1_g"]), "ln1_b": cols(i["L0_tok_ln1_b"])}
    for n in ("bq", "bk", "beq", "bek", "bv"):
        c[f"l0_{n}"] = cols(i[f"L0_attn_{n}"])
    for n in ("bq", "bk"):
        c[f"l2_{n}"] = cols(i[f"L2_attn_{n}"])
    c["w_ln1"], c["w_ln2"] = cols(i["L2_ffn_w_ln1"]), cols(i["L2_ffn_w_ln2"])
    c["l3_bq"], c["l3_bk"] = cols(ipb[:, 0].reshape(-1)), cols(ipb[:, 1].reshape(-1))

    mb = i["L0_attn_mix_b"]
    mixb = np.stack([mb.reshape(2, P), np.roll(mb, 1, axis=1).reshape(2, P)], 1)
    r = {"cls": i["L0_tok_cls_token"], "cls_pos": i["L0_tok_cls_pos_embedding"], "tok_b": i["L0_tok_bias"],
         "ln2_g": i["L0_tok_ln2_g"], "ln2_b": i["L0_tok_ln2_b"], "l0_bv": i["L0_attn_bv"],
         "l0_bo": i["L0_attn_bo"], "l0_ln_g": i["L0_attn_ln_g"], "l0_ln_b": i["L0_attn_ln_b"], "l0_mixb": mixb,
         "l0_ampphb": np.concatenate([i["L0_attn_amp_b"], i["L0_attn_ph_b"]]), "l0_rb": i["L0_ffn_router_bias"],
         "l2_bv": i["L2_attn_bv"], "l2_bo": i["L2_attn_bo"],
         "mla_rb": np.concatenate([i["L2_ffn_routing_bias"], np.zeros(1, z)]), "l3_bv": ipb[:, 2],
         "l3_bo": i["L3_attn_out_proj_bias"]}

    def experts(*parts):
        return np.ascontiguousarray(np.concatenate(
            [p.reshape(p.shape[0], -1, P, p.shape[2]).transpose(0, 2, 1, 3).reshape(p.shape[0], P, -1)
             for p in parts], 2))

    gu = i["L0_ffn_gate_up_proj"]
    pad_out = ((0, 0), (0, 0), (0, L1_PAD - L1_HID))
    pad_in = ((0, 0), (0, L1_PAD - L1_HID), (0, 0))

    def with_shared(shared, routed):
        return np.concatenate([i[f"L2_ffn_{shared}"][None], i[f"L2_ffn_{routed}"]], 0)
    return {
        "patches": tiled(patches), "weights": weights,
        "cols": np.concatenate([c[n] for n in COL_AT], 1),
        "rows": np.concatenate([np.asarray(r[n]).reshape(1, -1) for n in ROW_AT], 1),
        "consts": constants(),
        "l0_experts": np.concatenate([
            experts(gu[:, :, :D], gu[:, :, D:], i["L0_ffn_down_proj"]),
            i["L0_ffn_gate_up_bias"].reshape(L0_E, L0_BIASES, P).transpose(0, 2, 1)], 2),
        "l1_experts": experts(np.pad(i["L1_ffn_W2"], pad_out), np.pad(i["L1_ffn_W1"], pad_out),
                              np.pad(i["L1_ffn_W3"], pad_in)),
        "l2_experts": experts(with_shared("Wg_s", "Wg_r"), with_shared("Wu_s", "Wu_r"), with_shared("Wd_s", "Wd_r")),
        "l3_experts": experts(i["L3_ffn_w1"], i["L3_ffn_w2"]),
    }


def kernel(**inputs):
    import concourse.bacc as bacc
    from concourse.bass_utils import run_bass_kernel_spmd

    nc = bacc.Bacc("TRN2", target_bir_lowering=False, num_devices=1)
    arrays, aps = {}, {}
    for name, v in layout({k: np.asarray(v) for k, v in inputs.items()}).items():
        arrays[f"in_{name}"] = np.ascontiguousarray(v)
        aps[name] = nc.dram_tensor(f"in_{name}", v.shape, mybir.dt.from_np(v.dtype), kind="ExternalInput").ap()
    out = nc.dram_tensor("out_dram", (TOKENS, D), F32, kind="ExternalOutput").ap()
    build(nc, aps, out)
    r = run_bass_kernel_spmd(nc, [arrays], core_ids=[0])
    return r.results[0]["out_dram"].reshape(IMAGES, SEQ, D)
```
